# Optimizing a Trainium2 kernel written in Bass

```python
import numpy as np
import jax
import jax.numpy as jnp

def _softmax(x, axis=-1):
    return jax.nn.softmax(x, axis=axis)

def _gelu(x):
    return jax.nn.gelu(x, approximate=True)

def _silu(x):
    return jax.nn.silu(x)

def _sigmoid(x):
    return jax.nn.sigmoid(x)

def _layernorm(x, axis=-1, eps=1e-05):
    m = jnp.mean(x, axis=axis, keepdims=True)
    v = jnp.var(x, axis=axis, keepdims=True)
    return (x - m) / jnp.sqrt(v + eps)

def _scatter_add(tgt, idx, src, axis=0):
    return tgt.at[idx].add(src)

def _segment_sum(src, seg, n):
    return jax.ops.segment_sum(src, seg, n)
kernel_name = 'mk_prb_d1_jaxref_r4_11a978'

def setup_inputs(seed: int=0):
    np.random.seed(seed)
    _w = jnp.asarray

    def _L0_attn_setup():
        import jax, jax.numpy as jnp
        import numpy as np
        D_MODEL = 256
        N_HEADS = 16
        LATENT_HEADS = 8
        LATENT_DIM = 128
        N_LATENTS = 64
        WINDOW = 64
        HEAD_DIM = D_MODEL // N_HEADS
        LAT_HD = LATENT_DIM // LATENT_HEADS
        B, S = (2, 1024)

        def _pool_to_latents(x):
            Bx, Sx, C = x.shape
            chunk = max(1, Sx // N_LATENTS)
            return x.reshape(Bx, N_LATENTS, chunk, C).mean(axis=2)

        def _local_window_attn(Q, K, V):
            Bx, H, Sx, D = Q.shape
            W = WINDOW
            nb = Sx // W
            Qb = Q.reshape(Bx, H, nb, W, D)
            Kp = jnp.pad(K, ((0, 0), (0, 0), (W, 0), (0, 0))).reshape(Bx, H, nb + 1, W, D)
            Vp = jnp.pad(V, ((0, 0), (0, 0), (W, 0), (0, 0))).reshape(Bx, H, nb + 1, W, D)
            Kw = jnp.concatenate([Kp[:, :, :-1], Kp[:, :, 1:]], axis=3)
            Vw = jnp.concatenate([Vp[:, :, :-1], Vp[:, :, 1:]], axis=3)
            i = jnp.arange(W)[:, None]
            j = jnp.arange(2 * W)[None, :]
            base = (j > i) & (j <= i + W)
            blk0 = (jnp.arange(nb) > 0)[:, None, None] | (j >= W)[None, :, :]
            mask = base[None, :, :] & blk0
            sc = jnp.einsum('bhnid,bhnjd->bhnij', Qb, Kw) / np.sqrt(D).astype(np.float32)
            sc = jnp.where(mask[None, None], sc, -jnp.inf)
            p = jax.nn.softmax(sc, axis=-1)
            out = jnp.einsum('bhnij,bhnjd->bhnid', p, Vw)
            return out.reshape(Bx, H, Sx, D)
        key = jax.random.key(seed)
        ks = jax.random.split(key, 11)
        std = 0.02
        w = lambda k, shp: jax.random.normal(k, shp, jnp.float32) * std
        return {'x': jax.random.normal(ks[0], (B, S, D_MODEL), jnp.float32), 'wq': w(ks[1], (D_MODEL, D_MODEL)), 'wk': w(ks[2], (D_MODEL, D_MODEL)), 'wv': w(ks[3], (D_MODEL, D_MODEL)), 'wgq': w(ks[4], (D_MODEL, LATENT_DIM)), 'wgk': w(ks[5], (D_MODEL, LATENT_DIM)), 'wgv': w(ks[6], (D_MODEL, LATENT_DIM)), 'r_out_w': w(ks[7], (LATENT_DIM, D_MODEL)), 'gate_local_w': w(ks[8], (N_HEADS, HEAD_DIM)), 'gate_remote_w': w(ks[9], (N_HEADS, HEAD_DIM)), 'w_out': w(ks[10], (D_MODEL, D_MODEL))}
    _L0_attn_in = _L0_attn_setup()

    def _L0_ffn_setup():
        import jax, jax.numpy as jnp
        import numpy as np
        NUM_EXPERTS = 8
        TOP_K = 2
        FIXED_IDX = 0
        D_MODEL = 256
        D_FF = 1024
        B, S = (4, 512)

        def _route(flat_x, Wr):
            logits = flat_x @ Wr.T
            probs = jax.nn.softmax(logits.astype(jnp.float32), axis=-1).astype(flat_x.dtype)
            fixed_probs = probs[:, FIXED_IDX:FIXED_IDX + 1]
            remaining = probs[:, 1:]
            other_probs, other_local = jax.lax.top_k(remaining, TOP_K - 1)
            other_idx = other_local + 1
            topk_idx = jnp.concatenate([jnp.full((flat_x.shape[0], 1), FIXED_IDX, dtype=jnp.int32), other_idx], axis=1)
            topk_probs = jnp.concatenate([fixed_probs, other_probs], axis=1)
            topk_probs = topk_probs / jnp.clip(topk_probs.sum(axis=-1, keepdims=True), 1e-09)
            gates = jnp.sum(jax.nn.one_hot(topk_idx, NUM_EXPERTS, dtype=topk_probs.dtype) * topk_probs[..., None], axis=1)
            return gates
        key = jax.random.key(seed)
        ks = jax.random.split(key, 5)
        scale_r = 1.0 / np.sqrt(D_MODEL)
        return {'x': jax.random.normal(ks[0], (B, S, D_MODEL), dtype=jnp.float32), 'Wr': jax.random.normal(ks[1], (NUM_EXPERTS, D_MODEL), dtype=jnp.float32) * scale_r, 'W1': jax.random.normal(ks[2], (NUM_EXPERTS, D_FF, D_MODEL), dtype=jnp.float32) * scale_r, 'W2': jax.random.normal(ks[3], (NUM_EXPERTS, D_MODEL, D_FF), dtype=jnp.float32) * (1.0 / np.sqrt(D_FF)), 'W3': jax.random.normal(ks[4], (NUM_EXPERTS, D_FF, D_MODEL), dtype=jnp.float32) * scale_r}
    _L0_ffn_in = _L0_ffn_setup()
    _d = {'L0_attn_x': _L0_attn_in['x'], 'L0_attn_wq': _L0_attn_in['wq'], 'L0_attn_wk': _L0_attn_in['wk'], 'L0_attn_wv': _L0_attn_in['wv'], 'L0_attn_wgq': _L0_attn_in['wgq'], 'L0_attn_wgk': _L0_attn_in['wgk'], 'L0_attn_wgv': _L0_attn_in['wgv'], 'L0_attn_r_out_w': _L0_attn_in['r_out_w'], 'L0_attn_gate_local_w': _L0_attn_in['gate_local_w'], 'L0_attn_gate_remote_w': _L0_attn_in['gate_remote_w'], 'L0_attn_w_out': _L0_attn_in['w_out'], 'L0_ffn_Wr': _L0_ffn_in['Wr'], 'L0_ffn_W1': _L0_ffn_in['W1'], 'L0_ffn_W2': _L0_ffn_in['W2'], 'L0_ffn_W3': _L0_ffn_in['W3']}
    _x0 = _d['L0_attn_x']
    _d['L0_attn_x'] = jax.random.normal(jax.random.fold_in(jax.random.key(seed), 1), (1, 4096, 256), dtype=_x0.dtype)
    del _x0
    return _d

def reference(L0_attn_x, L0_attn_wq, L0_attn_wk, L0_attn_wv, L0_attn_wgq, L0_attn_wgk, L0_attn_wgv, L0_attn_r_out_w, L0_attn_gate_local_w, L0_attn_gate_remote_w, L0_attn_w_out, L0_ffn_Wr, L0_ffn_W1, L0_ffn_W2, L0_ffn_W3):

    def _L0_attn_ref(x, wq, wk, wv, wgq, wgk, wgv, r_out_w, gate_local_w, gate_remote_w, w_out):
        import jax, jax.numpy as jnp
        import numpy as np
        D_MODEL = 256
        N_HEADS = 16
        LATENT_HEADS = 8
        LATENT_DIM = 128
        N_LATENTS = 64
        WINDOW = 64
        HEAD_DIM = D_MODEL // N_HEADS
        LAT_HD = LATENT_DIM // LATENT_HEADS
        B, S = (2, 1024)

        def _pool_to_latents(x):
            Bx, Sx, C = x.shape
            chunk = max(1, Sx // N_LATENTS)
            return x.reshape(Bx, N_LATENTS, chunk, C).mean(axis=2)

        def _local_window_attn(Q, K, V):
            Bx, H, Sx, D = Q.shape
            W = WINDOW
            nb = Sx // W
            Qb = Q.reshape(Bx, H, nb, W, D)
            Kp = jnp.pad(K, ((0, 0), (0, 0), (W, 0), (0, 0))).reshape(Bx, H, nb + 1, W, D)
            Vp = jnp.pad(V, ((0, 0), (0, 0), (W, 0), (0, 0))).reshape(Bx, H, nb + 1, W, D)
            Kw = jnp.concatenate([Kp[:, :, :-1], Kp[:, :, 1:]], axis=3)
            Vw = jnp.concatenate([Vp[:, :, :-1], Vp[:, :, 1:]], axis=3)
            i = jnp.arange(W)[:, None]
            j = jnp.arange(2 * W)[None, :]
            base = (j > i) & (j <= i + W)
            blk0 = (jnp.arange(nb) > 0)[:, None, None] | (j >= W)[None, :, :]
            mask = base[None, :, :] & blk0
            sc = jnp.einsum('bhnid,bhnjd->bhnij', Qb, Kw) / np.sqrt(D).astype(np.float32)
            sc = jnp.where(mask[None, None], sc, -jnp.inf)
            p = jax.nn.softmax(sc, axis=-1)
            out = jnp.einsum('bhnij,bhnjd->bhnid', p, Vw)
            return out.reshape(Bx, H, Sx, D)
        Bx, Sx, _ = x.shape
        chunk = max(1, Sx // N_LATENTS)
        Q = (x @ wq).reshape(Bx, Sx, N_HEADS, HEAD_DIM).transpose(0, 2, 1, 3)
        K = (x @ wk).reshape(Bx, Sx, N_HEADS, HEAD_DIM).transpose(0, 2, 1, 3)
        V = (x @ wv).reshape(Bx, Sx, N_HEADS, HEAD_DIM).transpose(0, 2, 1, 3)
        local = _local_window_attn(Q, K, V)
        GQ = (x @ wgq).reshape(Bx, Sx, LATENT_HEADS, LAT_HD).transpose(0, 2, 1, 3)
        GK = _pool_to_latents(x @ wgk).reshape(Bx, N_LATENTS, LATENT_HEADS, LAT_HD).transpose(0, 2, 1, 3)
        GV = _pool_to_latents(x @ wgv).reshape(Bx, N_LATENTS, LATENT_HEADS, LAT_HD).transpose(0, 2, 1, 3)
        lsc = jnp.einsum('bhsd,bhnd->bhsn', GQ, GK) / np.sqrt(LAT_HD).astype(np.float32)
        lmask = jnp.arange(N_LATENTS)[None, :] <= (jnp.arange(Sx) // chunk)[:, None]
        lsc = jnp.where(lmask[None, None], lsc, -jnp.inf)
        lp = jax.nn.softmax(lsc, axis=-1)
        rem = jnp.einsum('bhsn,bhnd->bhsd', lp, GV)
        rem = rem.transpose(0, 2, 1, 3).reshape(Bx, Sx, LATENT_DIM) @ r_out_w
        rem = rem.reshape(Bx, Sx, N_HEADS, HEAD_DIM).transpose(0, 2, 1, 3)
        gl = jax.nn.sigmoid(jnp.einsum('bhsd,hd->bhs', Q, gate_local_w))[..., None]
        gr = jax.nn.sigmoid(jnp.einsum('bhsd,hd->bhs', Q, gate_remote_w))[..., None]
        out = gl * local + gr * rem
        out = out.transpose(0, 2, 1, 3).reshape(Bx, Sx, D_MODEL)
        return out @ w_out

    def _L0_ffn_ref(x, Wr, W1, W2, W3):
        import jax, jax.numpy as jnp
        import numpy as np
        NUM_EXPERTS = 8
        TOP_K = 2
        FIXED_IDX = 0
        D_MODEL = 256
        D_FF = 1024
        B, S = (4, 512)

        def _route(flat_x, Wr):
            logits = flat_x @ Wr.T
            probs = jax.nn.softmax(logits.astype(jnp.float32), axis=-1).astype(flat_x.dtype)
            fixed_probs = probs[:, FIXED_IDX:FIXED_IDX + 1]
            remaining = probs[:, 1:]
            other_probs, other_local = jax.lax.top_k(remaining, TOP_K - 1)
            other_idx = other_local + 1
            topk_idx = jnp.concatenate([jnp.full((flat_x.shape[0], 1), FIXED_IDX, dtype=jnp.int32), other_idx], axis=1)
            topk_probs = jnp.concatenate([fixed_probs, other_probs], axis=1)
            topk_probs = topk_probs / jnp.clip(topk_probs.sum(axis=-1, keepdims=True), 1e-09)
            gates = jnp.sum(jax.nn.one_hot(topk_idx, NUM_EXPERTS, dtype=topk_probs.dtype) * topk_probs[..., None], axis=1)
            return gates
        batch, seq, d_model = x.shape
        flat_x = x.reshape(batch * seq, d_model)
        gates = _route(flat_x, Wr)
        out = jnp.zeros_like(flat_x)
        for e in range(NUM_EXPERTS):
            h = jax.nn.silu(flat_x @ W1[e].T) * (flat_x @ W3[e].T)
            out = out + gates[:, e:e + 1] * (h @ W2[e].T)
        return out.reshape(batch, seq, d_model)
    x = L0_attn_x
    xn = _layernorm(x, axis=-1)
    x = x + _L0_attn_ref(xn, L0_attn_wq, L0_attn_wk, L0_attn_wv, L0_attn_wgq, L0_attn_wgk, L0_attn_wgv, L0_attn_r_out_w, L0_attn_gate_local_w, L0_attn_gate_remote_w, L0_attn_w_out) + _L0_ffn_ref(xn, L0_ffn_Wr, L0_ffn_W1, L0_ffn_W2, L0_ffn_W3)
    return x

_drawn_inputs = setup_inputs


def setup_inputs(seed=0):
    import zlib

    import numpy as np

    out = dict(_drawn_inputs(seed))
    spreads = {}
    factors = {'L0_attn_wq': 8.0,
     'L0_attn_wk': 8.0,
     'L0_attn_wv': 8.0,
     'L0_attn_wgq': 8.0,
     'L0_attn_wgk': 8.0,
     'L0_attn_wgv': 8.0,
     'L0_attn_r_out_w': 8.0,
     'L0_attn_gate_local_w': 8.0,
     'L0_attn_gate_remote_w': 8.0,
     'L0_attn_w_out': 8.0}
    for name, (base, spread) in spreads.items():
        noise = np.random.default_rng([zlib.crc32(name.encode()), seed]).standard_normal(out[name].shape)
        drawn = base * np.exp(spread * noise) if base else spread * noise
        out[name] = jnp.asarray(drawn.astype(out[name].dtype))
    for name, factor in factors.items():
        out[name] = (out[name] * factor).astype(out[name].dtype)
    return out
```

```python
from contextlib import ExitStack

import concourse.bass as bass
from concourse import mybir

ALU = mybir.AluOpType
ACT = mybir.ActivationFunctionType
AX = mybir.AxisListType
F32 = mybir.dt.float32
F32R = mybir.dt.float32r
BF16 = mybir.dt.bfloat16
I32 = mybir.dt.int32

P = 128
D = 256
KD = D // P
S = 4096
NT = S // P
SUP = 4
NS = NT // SUP
SW = SUP * P
H, HD = 16, 16
VW = HD + 1
GH = 8
NL = 64
W = 64
KW = W + P
E = 8
R = E - 1
FF = 1024
FT = FF // P
NG = (S + R * (P - 1)) // P
NF = NG + NT
NEG = -1.0e30
EPS = 1e-5


def moe_block(nc, x, wq, wk, wv, wgq, wgk, wgv, r_out, gate_l, gate_r, w_out, wr_t, w1_t, w3_t, w2_t, out):
    xn_rows = nc.dram_tensor("xn_rows", (S, D), F32, kind="Internal").ap()
    xg_rows = nc.dram_tensor("xg_rows", (NG * P, D), F32, kind="Internal").ap()
    yg_rows = nc.dram_tensor("yg_rows", (NG * P, D), F32, kind="Internal").ap()

    with ExitStack() as ctx:
        def sb(name, shape, dt=F32, c=ctx):
            return c.enter_context(nc.sbuf_tensor(name, shape, dt))

        def sem(name):
            return ctx.enter_context(nc.semaphore(name))

        bank = [ctx.enter_context(nc.psum_tensor(f"bank{i}", [P, 512], F32)) for i in range(8)]

        acc = sb("acc", [P, NT, D])
        ident = sb("ident", [P, P])
        ident_b = sb("ident_b", [P, P], BF16)
        slot = sb("slot", [P, NT], I32)
        gate0 = sb("gate0", [P, NT])
        gate1 = sb("gate1", [P, NT])
        rank_tab = sb("rank_tab", [1, NF + 2], I32)
        par_tab = sb("par_tab", [1, NF + 2], I32)
        end_tab = sb("end_tab", [1, 8], I32)

        names = """consts x_in w_in x_norm_d x_norm_t xn_out xt_ps xt_dve xt_act lg_ps lg_sb rstd_a rstd_d
            wprep pool_zero pooled zero_out rt_exp rt_oh rt_pre rt_done gk_ps gk_done gmats
            x_split proj_ps proj_a proj_d s_ps s_sub p_exp pt_ps pt_a pt_d pv o_a cmb1 xr_ps xr_a rem_ps
            cmb2 yt_ps yt_a o_ps o_d mx_done
            tl_in sc_out stage st_done w_split xin xt2_ps xh2 xl2 u_ps silu h_sb ht_ps hh hl y_ps y_sb y_out gath fin gt out_done""".split()
        m = {n: sem("q_" + n) for n in names}
        x_in = [sem(f"q_x_in{j}") for j in range(2)]
        xn_out = [sem(f"q_xn_out{j}") for j in range(2)]
        tl_in = [sem(f"q_tl_in{j}") for j in range(4)]
        sc_out = [sem(f"q_sc_out{j}") for j in range(4)]
        xin_in = [sem(f"q_xin_in{j}") for j in range(2)]
        y_out = [sem(f"q_y_out{j}") for j in range(2)]
        gath = [sem(f"q_gath{j}") for j in range(4)]
        dch, ach, pch = sem("dve_chain"), sem("act_chain"), sem("pool_chain")

        class Chain:
            def __init__(self, eng, s):
                self.eng, self.s, self.n, self.base, self.per, self.it = eng, s, 0, 0, 0, None

            def link(self, ins):
                self.n += 1
                ins.then_inc(self.s, 1)
                v = self.base + self.n
                self.eng.wait_ge(self.s, v if self.it is None else self.it * self.per + v)

            def loop(self, it, per):
                self.it, self.per, self.base, self.n = it, per, self.base + self.n, 0

            def done(self, times):
                assert self.n == self.per, self.n
                self.base, self.n, self.it = self.base + times * self.per, 0, None

        att = ExitStack()
        with att:
            def sa(name, shape, dt=F32):
                return sb(name, shape, dt, att)

            xnt = sa("xnt", [P, KD, W + S + W])
            xn_t = [sa(f"xn_t{j}", [P, SUP, D]) for j in range(2)]
            xts = [sa(f"xts{j}", [P, KD, SW]) for j in range(2)]
            stat = sa("stat", [P, SUP, 6])
            mv = sa("mv", [P, SUP, 2])
            rstd = sa("rstd", [P, SUP])
            tick = sa("tick", [P, 4])
            eps_t = sa("eps_t", [P, 1])
            wrt = sa("wrt", [P, KD, E])
            logit = sa("logit", [P, NT, E])
            NW = 2 * D + D + P + D
            QC, KC, GC, VC = 0, 2 * D, 3 * D, 3 * D + P
            wraw = sa("wraw", [P, KD, 3 * D + 3 * P])
            wh = sa("wh", [P, KD, NW], F32R)
            wl = sa("wl", [P, KD, NW], F32R)
            rw = sa("rw", [P, D])
            ow = sa("ow", [P, KD, D])
            gw_raw = sa("gw_raw", [P, 2, 2])
            gw = sa("gw", [P, 2, 2 * H])
            hmask = sa("hmask", [P, GH])
            hmask16 = sa("hmask16", [P, 2, H])
            pmask = sa("pmask", [P, 2])
            mask = sa("mask", [P, NS, KW], BF16)
            lmask = sa("lmask", [P, 2 * NL], BF16)
            pool_t = sa("pool_t", [P, KD, 2, NL])
            gkbd = sa("gkbd", [P, GH, NL])
            gvbd = sa("gvbd", [P, GH, VW])
            XW = W + SW + W
            xh = sa("xh", [P, KD, XW], F32R)
            xl = sa("xl", [P, KD, XW], F32R)
            qt = sa("qt", [P, 2, 2, SW])
            kt = sa("kt", [P, 2, W + SW])
            gqt = sa("gqt", [P, SW])
            v2 = sa("v2", [P, SUP + 1, H, VW])
            mx = [sa(f"mx{j}", [P, 8]) for j in range(2)]
            sub = [sa(f"sub{j}", [P, 4, KW]) for j in range(2)]
            prob = [sa(f"prob{j}", [P, 4, KW]) for j in range(2)]
            pt1 = [sa(f"pt1_{j}", [P, 512]) for j in range(2)]
            pt2 = [sa(f"pt2_{j}", [W, 512]) for j in range(2)]
            osb = sa("osb", [P, 440])
            rcp = sa("rcp", [P, 24])
            gsg = sa("gsg", [P, 2, H])
            loc = sa("loc", [P, H, HD])
            remn = sa("remn", [P, GH, HD])
            remt = sa("remt", [P, P])
            mix = sa("mix", [P, H, HD])
            mixt = sa("mixt", [P, KD, P])
            zrow = sa("zrow", [P, D])
            u_tri = sa("u_tri", [P, P])
            ones = sa("ones", [P, P])
            it128 = sa("it128", [P, NT])
            wgt = sa("wgt", [P, R])
            gidx = sa("gidx", [1, NF + 2])
            last = sa("last", [1, NF + 2])
            lmx = sa("lmx", [P, NT])
            le = sa("le", [P, NT, E])
            lsum = sa("lsum", [P, NT])
            p1 = sa("p1", [P, NT])
            eq = sa("eq", [P, NT, R])
            oh = sa("oh", [P, R, NT])
            cum = [sa(f"cum{j}", [P, R, NT]) for j in range(2)]
            pre = sa("pre", [P, R, NT])
            cnt = sa("cnt", [P, R, NT])
            ntl = sa("ntl", [P, R])
            st_e = sa("st_e", [P, R + 1])
            ge = sa("ge", [1, R - 1, NF + 2])
            rtf = sa("rtf", [1, 2, NF + 2])
            slotf = sa("slotf", [P, NT])
            tl = [sa(f"tl{j}", [P, D]) for j in range(4)]

            LAG = 2
            UN = 5
            NU = SUP * UN
            STEPS = NU + 7

            def unit(n):
                return n // UN, (0, -1, 1, 2, 3)[n % UN]

            def tail(n):
                q = n - (UN - 1) - LAG - 1
                return (q // UN, q % UN) if q >= 0 and q // UN < SUP and q % UN < 4 else None

            xr = x.rearrange("(t p) d -> p t d", p=P)

            blk = nc.Block()
            with blk as block:
                @block.sync
                def _(sp):
                    for s in range(NS):
                        if s >= 2:
                            sp.wait_ge(x_in[s % 2], 16 * (s // 2))
                        sp.dma_start(acc[:, SUP * s:SUP * s + SUP, :], xr[:, SUP * s:SUP * s + SUP, :]).then_inc(x_in[s % 2], 16)
                        if s == 0:
                            sp.dma_start(wrt[:], wr_t.rearrange("(k p) e -> p k e", p=P)).then_inc(m["w_in"], 16)
                            for w_, c in ((wq, 0), (wk, D), (wv, 2 * D), (wgq, 3 * D), (wgk, 3 * D + P), (wgv, 3 * D + 2 * P)):
                                sp.dma_start(wraw[:, :, c:c + w_.shape[1]], w_.rearrange("(k p) n -> p k n", p=P)).then_inc(m["w_in"], 16)
                            sp.dma_start(rw[:], r_out).then_inc(m["w_in"], 16)
                            sp.dma_start(ow[:], w_out.rearrange("(k p) n -> p k n", p=P)).then_inc(m["w_in"], 16)
                            for j, g in enumerate((gate_l, gate_r)):
                                sp.dma_start(gw_raw[:, :, j:j + 1], g.rearrange("(g h) (d o) -> (h d) g o", g=2, o=1),
                                             allow_slow_non_contiguous=True).then_inc(m["w_in"], 16)
                    sp.wait_ge(m["pool_zero"], 1)
                    sp.dma_start(xg_rows.rearrange("(g p) d -> p g d", p=P),
                                 zrow[:].rearrange("p (o d) -> p o d", o=1).broadcast_to([P, NG, D])).then_inc(m["zero_out"], 16)
                    with sp.Fori(0, NS // 2) as i:
                        for j in range(2):
                            sp.wait_ge(m["x_norm_t"], i * 2 + (j + 1))
                            sp.dma_start(xn_rows[bass.ds(i * (2 * SW) + j * SW, SW), :].rearrange("(t p) d -> p t d", p=P),
                                         xn_t[j][:]).then_inc(xn_out[j], 16)
                    for j in range(2):
                        sp.wait_ge(xn_out[j], 16 * (NS // 2))
                    for t in range(NT):
                        if t >= 4:
                            sp.wait_ge(sc_out[t % 4], 16 * (t // 4))
                        sp.dma_start(tl[t % 4][:], xn_rows[t * P:t * P + P, :]).then_inc(tl_in[t % 4], 16)

                @block.gpsimd
                def _(g):
                    ch = Chain(g, pch)
                    G = nc.gpsimd
                    G.memset(zrow[:], 0.0).then_inc(m["pool_zero"], 1)
                    G.memset(eps_t[:], EPS)
                    G.memset(ones[:], 1.0)
                    G.memset(v2[:].rearrange("p a h v -> p (a h v)"), 1.0)
                    G.memset(xnt[:, :, 0:W], 0.0)
                    G.memset(xnt[:, :, W + S:], 0.0)
                    G.memset(hmask[:], 1.0)
                    G.memset(pmask[:], 1.0)
                    G.memset(ident[:], 0.0)
                    G.memset(u_tri[:], 1.0)
                    G.memset(mask[:], 0.0)
                    ch.link(G.memset(lmask[:], 0.0))
                    G.affine_select(out=ident[:], in_=ident[:], compare_op=ALU.not_equal, fill=1.0, base=0,
                                    pattern=[[-1, P]], channel_multiplier=1)
                    G.affine_select(out=u_tri[:], in_=u_tri[:], compare_op=ALU.is_gt, fill=0.0, base=0,
                                    pattern=[[1, P]], channel_multiplier=-1)
                    ch.link(G.affine_select(out=hmask[:], in_=hmask[:], compare_op=ALU.is_ge, fill=0.0, base=0,
                                            pattern=[[-HD, GH]], channel_multiplier=1))
                    ch.link(G.affine_select(out=hmask[:], in_=hmask[:], compare_op=ALU.is_ge, fill=0.0, base=HD - 1,
                                            pattern=[[HD, GH]], channel_multiplier=-1))
                    ch.link(G.affine_select(out=pmask[:], in_=pmask[:], compare_op=ALU.is_ge, fill=0.0, base=0,
                                            pattern=[[-NL, 2]], channel_multiplier=1))
                    ch.link(G.affine_select(out=pmask[:], in_=pmask[:], compare_op=ALU.is_ge, fill=0.0, base=NL - 1,
                                            pattern=[[NL, 2]], channel_multiplier=-1))
                    ch.link(G.affine_select(out=mask[:], in_=mask[:], compare_op=ALU.is_gt, fill=NEG, base=0,
                                            pattern=[[0, NS], [1, KW]], channel_multiplier=-1))
                    ch.link(G.affine_select(out=mask[:], in_=mask[:], compare_op=ALU.is_ge, fill=NEG, base=W,
                                            pattern=[[0, NS], [-1, KW]], channel_multiplier=1))
                    ch.link(G.affine_select(out=mask[:, 0, :], in_=mask[:, 0, :], compare_op=ALU.is_ge, fill=NEG, base=-W,
                                            pattern=[[1, KW]], channel_multiplier=0))
                    ch.link(G.affine_select(out=lmask[:], in_=lmask[:], compare_op=ALU.is_ge, fill=NEG, base=NL * (NL - 2),
                                            pattern=[[-NL, 2 * NL]], channel_multiplier=1))
                    G.tensor_copy(ident_b[:], ident[:])
                    G.tensor_copy(hmask16[:, :, 0:GH], hmask[:].rearrange("p (o h) -> p o h", o=1).broadcast_to([P, 2, GH]))
                    G.iota(it128[:], pattern=[[P, NT]], base=0, channel_multiplier=0, allow_small_or_imprecise_dtypes=True)
                    G.iota(wgt[:], pattern=[[-1, R]], base=R, channel_multiplier=0, allow_small_or_imprecise_dtypes=True)
                    ch.link(G.iota(gidx[:], pattern=[[1, NF + 2]], base=0, channel_multiplier=0, allow_small_or_imprecise_dtypes=True))
                    ch.link(G.tensor_scalar(last[:], gidx[:], float(NG), None, ALU.is_ge))
                    G.memset(wh[:, :, 0:2 * D].bitcast(F32), 0.0)
                    G.memset(wl[:, :, 0:2 * D].bitcast(F32), 0.0).then_inc(m["consts"], 1)
                    g.wait_ge(m["w_in"], 16 * 11)
                    g.wait_ge(m["consts"], 1)
                    q_raw = wraw[:, :, 0:D].rearrange("p k (a b d) -> p k a b d", b=2, d=HD)
                    for k in range(KD):
                        for b in range(2):
                            hv = wh[:, k, D * b:D * b + D].rearrange("p (a b d) -> p a b d", b=2, d=HD)[:, :, b, :]
                            lv = wl[:, k, D * b:D * b + D].rearrange("p (a b d) -> p a b d", b=2, d=HD)[:, :, b, :]
                            ch.link(G.tensor_copy(hv, q_raw[:, k, :, b, :]))
                            G.tensor_tensor(lv, q_raw[:, k, :, b, :], hv.bitcast(F32), ALU.subtract)
                        for c0, r0, n in ((KC, D, D), (VC, 2 * D, D), (GC, 3 * D, P)):
                            ch.link(G.tensor_copy(wh[:, k, c0:c0 + n], wraw[:, k, r0:r0 + n]))
                            G.tensor_tensor(wl[:, k, c0:c0 + n], wraw[:, k, r0:r0 + n], wh[:, k, c0:c0 + n].bitcast(F32), ALU.subtract)
                    G.memset(gw[:], 0.0).then_inc(m["wprep"], 1)
                    g.wait_ge(m["xt_dve"], NS)
                    with g.Fori(0, NS) as s:
                        G.tensor_copy(xh[:], xnt[:, :, bass.ds(s * SW, XW)]).then_inc(m["x_split"], 1)
                        g.wait_ge(m["x_split"], s * 2 + 1)
                        G.tensor_tensor(tick[:, 2:3], zrow[:, 0:1], zrow[:, 0:1], ALU.add)
                        G.tensor_tensor(xl[:], xnt[:, :, bass.ds(s * SW, XW)], xh[:].bitcast(F32), ALU.subtract).then_inc(m["x_split"], 1)
                        g.wait_ge(m["proj_ps"], s * 13 + 13)
                        G.tensor_tensor(tick[:, 1:2], zrow[:, 0:1], zrow[:, 0:1], ALU.add)
                    g.wait_ge(m["rt_done"], 1)
                    g.wait_ge(m["zero_out"], 16)
                    for t in range(NT):
                        g.wait_ge(tl_in[t % 4], 16 * (t // 4 + 1))
                        G.indirect_dma_start(xg_rows, bass.IndirectOffsetOnAxis(slot[:, t:t + 1], 0), tl[t % 4][:], None).then_inc(sc_out[t % 4], 16)
                    for j in range(4):
                        g.wait_ge(sc_out[j], 16 * (NT // 4))

                @block.tensor
                def _(pe):
                    T = nc.tensor
                    pe.wait_ge(m["consts"], 1)
                    with pe.Fori(0, NS // 2) as i:
                        for j in range(2):
                            pe.wait_ge(m["x_norm_t"], i * 2 + (j + 1))
                            if j:
                                pe.wait_ge(m["xt_dve"], i * 2 + 1)
                            for k in range(KD):
                                for t in range(SUP):
                                    last_ = T.transpose(bank[k][:, P * t:P * t + P], xn_t[j][:, t, P * k:P * k + P], ident[:])
                            last_.then_inc(m["xt_ps"], 1)
                            pe.wait_ge(m["xt_act"], i * 2 + (j + 1))
                            pe.wait_ge(m["w_in"], 16 * 11)
                            if j:
                                pe.wait_ge(m["lg_sb"], i * 2 + 1)
                            for t in range(SUP):
                                for k in range(KD):
                                    last_ = T.matmul(bank[2][:, E * t:E * t + E], xts[j][:, k, P * t:P * t + P], wrt[:, k, :],
                                                     start=(k == 0), stop=(k == KD - 1))
                            last_.then_inc(m["lg_ps"], 1)
                        pe.wait_ge(m["xt_dve"], i * 2 + 2)
                        pe.wait_ge(m["lg_sb"], i * 2 + 2)
                    pe.wait_ge(m["rt_oh"], 1)
                    T.matmul(bank[3][:, 0:R * NT], u_tri[:], oh[:].rearrange("p e t -> p (e t)"), start=True, stop=True)
                    T.matmul(bank[3][:, 256:256 + R * NT], ones[:], oh[:].rearrange("p e t -> p (e t)"), start=True, stop=True).then_inc(m["rt_pre"], 1)
                    pe.wait_ge(m["pooled"], 1)
                    for k in range(KD):
                        T.matmul(bank[4][:, 0:NL], wraw[:, k, 3 * D + P:3 * D + 2 * P], pool_t[:, k, 0, :], start=(k == 0), stop=(k == KD - 1))
                    for k in range(KD):
                        last_ = T.matmul(bank[4][:, 256:256 + P], pool_t[:, k, :, :].rearrange("p a n -> p (a n)"),
                                         wraw[:, k, 3 * D + 2 * P:3 * D + 3 * P], start=(k == 0), stop=(k == KD - 1))
                    last_.then_inc(m["gk_ps"], 1)
                    pe.wait_ge(m["wprep"], 1)
                    pe.wait_ge(m["gk_done"], 1)

                    def three(dst, stat_h, stat_l, mov_h, mov_l, ks):
                        n = 0
                        for k in ks:
                            for a, b in ((stat_h, mov_h), (stat_h, mov_l), (stat_l, mov_h)):
                                last_ = T.matmul(dst, a(k), b(k), start=(n == 0), stop=(n == 3 * len(ks) - 1))
                                n += 1
                        return last_

                    with pe.Fori(0, NS) as s:
                        pe.wait_ge(m["x_split"], s * 2 + 2)
                        wcol = lambda c: ((lambda k: wh[:, k, c:c + P]), (lambda k: wl[:, k, c:c + P]))
                        pieces = []
                        for b in range(2):
                            for g2 in range(2):
                                pieces.append((QC + D * b + P * g2, W, SW))
                        pieces += [(KC, W, SW), (KC + P, W, SW)]
                        for n_, (c, x0, w_) in enumerate(pieces):
                            three(bank[n_][:, 0:w_], *wcol(c), lambda k: xh[:, k, x0:x0 + w_], lambda k: xl[:, k, x0:x0 + w_],
                                  range(KD)).then_inc(m["proj_ps"], 1)
                        for g2 in range(2):
                            last_ = three(bank[6][:, W * g2:W * g2 + W], *wcol(KC + P * g2), lambda k: xh[:, k, 0:W], lambda k: xl[:, k, 0:W], range(KD))
                        last_.then_inc(m["proj_ps"], 1)
                        three(bank[7][:], *wcol(GC), lambda k: xh[:, k, W:W + SW], lambda k: xl[:, k, W:W + SW], range(KD)).then_inc(m["proj_ps"], 1)
                        for c in range(SUP + 1):
                            if c % 2 == 0:
                                pe.wait_ge(m["proj_a"], s * 7 + (c // 2 + 1))
                            else:
                                pe.wait_ge(m["proj_d"], s * 6 + (c // 2 + 1))
                            three(bank[c][:, 0:D], lambda k: xh[:, k, P * c:P * c + P], lambda k: xl[:, k, P * c:P * c + P],
                                  lambda k: wh[:, k, VC:VC + D], lambda k: wl[:, k, VC:VC + D], range(KD)).then_inc(m["proj_ps"], 1)
                        pe.wait_ge(m["proj_a"], s * 7 + 7)
                        pe.wait_ge(m["proj_d"], s * 6 + 6)

                        for n in range(STEPS):
                            if n < NU:
                                i, u = unit(n)
                                if u < 0:
                                    if i >= 2:
                                        pe.wait_ge(m["o_d"], s * SUP + i - 1)
                                    elif i == 1:
                                        pe.wait_ge(m["s_sub"], s * NU + n - UN + 1)
                                    T.matmul(bank[7][:].rearrange("p (h n) -> p h n", h=GH), ident_b[:],
                                             lmask[:, bass.ds(s * (-2 * SUP) + (NL - 2 - 2 * i), NL)].rearrange("p (o n) -> p o n", o=1).broadcast_to([P, GH, NL]),
                                             start=True, stop=False)
                                    T.matmul(bank[7][:], gqt[:, P * i:P * i + P], gkbd[:].rearrange("p h n -> p (h n)"),
                                             start=False, stop=True).then_inc(m["s_ps"], 1)
                                else:
                                    g2, jp = u // 2, u % 2
                                    if n >= 3:
                                        pe.wait_ge(m["s_sub"], s * NU + (n - 2 if u in (0, 3) else n - 3) + 1)
                                    for j in (2 * jp, 2 * jp + 1):
                                        mk = mask[:, bass.ds(s, 1), :] if i == 0 else mask[:, 1:2, :]
                                        T.matmul(bank[j][:].rearrange("p (h k) -> p h k", h=2)[:, :, 0:KW], ident_b[:],
                                                 mk.broadcast_to([P, 2, KW]), start=True, stop=False)
                                    for b in range(2):
                                        for j in (2 * jp, 2 * jp + 1):
                                            last_ = T.matmul(bank[j][:, 256 * b:256 * b + KW], qt[32 * j:32 * j + 32, b, g2, P * i:P * i + P],
                                                             kt[32 * j:32 * j + 32, g2, P * i:P * i + KW], start=False, stop=(b == 1))
                                    last_.then_inc(m["s_ps"], 1)
                            if 1 <= n <= NU:
                                i, u = unit(n - 1)
                                pe.wait_ge(m["p_exp"], s * NU + n)
                                if n >= 2:
                                    pe.wait_ge(m["pt_a"], s * NU + n - 1)
                                    pe.wait_ge(m["pt_d"], s * NU + n - 1)
                                if u < 0:
                                    pl = prob[(n - 1) % 2][:].rearrange("p a b -> p (a b)")
                                    for c in range(4):
                                        last_ = T.transpose(bank[4][:, P * c:P * c + P], pl[:, P * c:P * c + P], ident[:])
                                else:
                                    for c in range(4):
                                        T.transpose(bank[4][:, P * c:P * c + P], prob[(n - 1) % 2][:, c, 0:P], ident[:])
                                        last_ = T.transpose(bank[5][0:W, P * c:P * c + P], prob[(n - 1) % 2][:, c, P:KW], ident[:])
                                last_.then_inc(m["pt_ps"], 1)
                            if LAG <= n < NU + LAG:
                                i, u = unit(n - LAG)
                                pe.wait_ge(m["pt_a"], s * NU + n - 1)
                                pe.wait_ge(m["pt_d"], s * NU + n - 1)
                                b_ = (n - LAG) % 2
                                if u == 0 and i:
                                    pe.wait_ge(m["o_a"], s * SUP + i)
                                if u < 0:
                                    n_ = 0
                                    for b in range(2):
                                        for g2 in range(2):
                                            T.matmul(bank[6][:, 408:440], qt[:, b, g2, P * i:P * i + P], gw[:, g2, :], start=(n_ == 0), stop=(n_ == 3))
                                            n_ += 1
                                    for c in range(4):
                                        last_ = T.matmul(bank[6][:, 272 + 34 * c:306 + 34 * c], pt1[b_][:, P * c:P * c + P],
                                                         gvbd[:, 2 * c:2 * c + 2, :].rearrange("p h v -> p (h v)"), start=True, stop=True)
                                else:
                                    g2, jp = u // 2, u % 2
                                    for c in range(4):
                                        h = 8 * g2 + 2 * (2 * jp + c // 2) + c % 2
                                        T.matmul(bank[6][:, VW * h:VW * h + VW], pt1[b_][:, P * c:P * c + P], v2[:, i, h, :], start=True, stop=False)
                                        last_ = T.matmul(bank[6][:, VW * h:VW * h + VW], pt2[b_][:, P * c:P * c + P], v2[0:W, i + 1, h, :], start=False, stop=True)
                                last_.then_inc(m["pv"], 1)
                            if tail(n):
                                i, stage = tail(n)
                                if stage == 0:
                                    pe.wait_ge(m["cmb1"], s * SUP + i + 1)
                                    pe.wait_ge(m["s_sub"], s * NU + min(i + 1, SUP - 1) * UN + 2)
                                    T.transpose(bank[7][:, 0:P], remn[:].rearrange("p h d -> p (h d)"), ident[:]).then_inc(m["xr_ps"], 1)
                                elif stage == 1:
                                    pe.wait_ge(m["xr_a"], s * SUP + i + 1)
                                    T.matmul(bank[7][:, 0:D], remt[:], rw[:], start=True, stop=True).then_inc(m["rem_ps"], 1)
                                elif stage == 2:
                                    pe.wait_ge(m["cmb2"], s * SUP + i + 1)
                                    for k in range(KD):
                                        last_ = T.transpose(bank[7][:, P * k:P * k + P], mix[:].rearrange("p h d -> p (h d)")[:, P * k:P * k + P], ident[:])
                                    last_.then_inc(m["yt_ps"], 1)
                                else:
                                    pe.wait_ge(m["yt_a"], s * SUP + i + 1)
                                    for k in range(KD):
                                        last_ = T.matmul(bank[7][:, 0:D], mixt[:, k, :], ow[:, k, :], start=(k == 0), stop=(k == KD - 1))
                                    last_.then_inc(m["o_ps"], 1)
                        pe.wait_ge(m["o_d"], s * SUP + SUP)

                @block.vector
                def _(v):
                    V = nc.vector
                    ch = Chain(v, dch)
                    v.wait_ge(m["consts"], 1)
                    with v.Fori(0, NS // 2) as i:
                        ch.loop(i, 2 * 2)
                        for j in range(2):
                            v.wait_ge(x_in[j], i * 16 + 16)
                            for t in range(SUP):
                                ins = V.bn_stats(stat[:, t, :], acc[:, bass.ds(i * (2 * SUP) + (SUP * j + t), 1), :].rearrange("p o d -> p (o d)"))
                            ch.link(ins)
                            V.memset(tick[:, 0:1], 0.0)
                            for t in range(SUP):
                                ins = V.bn_aggr(mv[:, t, :], stat[:, t, :])
                            ins.then_inc(m["rstd_d"], 1)
                            v.wait_ge(m["rstd_a"], i * 2 + (j + 1))
                            ch.link(V.reciprocal(rstd[:], rstd[:]))
                            for t in range(SUP):
                                ins = V.tensor_scalar(xn_t[j][:, t, :], acc[:, bass.ds(i * (2 * SUP) + (SUP * j + t), 1), :].rearrange("p o d -> p (o d)"),
                                                      mv[:, t, 0:1], rstd[:, t:t + 1], ALU.subtract, ALU.mult)
                            ins.then_inc(m["x_norm_t"], 1)
                            v.wait_ge(m["xt_act"], i * 2 + (j + 1))
                            for k in range(KD):
                                ins = V.tensor_copy(xnt[:, k, bass.ds(i * (2 * SW) + (W + SW * j), SW)], bank[k][:])
                            ins.then_inc(m["xt_dve"], 1)
                            v.wait_ge(m["lg_ps"], i * 2 + (j + 1))
                            V.tensor_copy(logit[:, bass.ds(i * (2 * SUP) + SUP * j, SUP), :],
                                          bank[2][:, 0:SUP * E].rearrange("p (t e) -> p t e", e=E)).then_inc(m["lg_sb"], 1)
                        for j in range(2):
                            v.wait_ge(xn_out[j], i * 16 + 16)
                        ch.done(NS // 2)

                    v.wait_ge(m["lg_sb"], NS)
                    bc = lambda a, n: a.rearrange("p (t o) -> p t o", o=1).broadcast_to([P, NT, n])
                    be = lambda a: a.rearrange("p (e o) -> p e o", o=1).broadcast_to([P, R, NT])
                    ch.link(V.tensor_reduce(lmx[:], logit[:], AX.X, ALU.max))
                    V.tensor_tensor(le[:], logit[:], bc(lmx[:], E), ALU.subtract).then_inc(m["rt_exp"], 1)
                    v.wait_ge(m["rt_exp"], 2)
                    ch.link(V.tensor_reduce(lsum[:], le[:], AX.X, ALU.add))
                    ch.link(V.reciprocal(lsum[:], lsum[:]))
                    ch.link(V.tensor_tensor(le[:], le[:], bc(lsum[:], E), ALU.mult))
                    ch.link(V.tensor_reduce(p1[:], le[:, :, 1:E], AX.X, ALU.max))
                    ch.link(V.tensor_tensor(eq[:], le[:, :, 1:E], bc(p1[:], R), ALU.is_equal))
                    ch.link(V.tensor_tensor(eq[:], eq[:], wgt[:].rearrange("p (o e) -> p o e", o=1).broadcast_to([P, NT, R]), ALU.mult))
                    ch.link(V.tensor_reduce(lmx[:], eq[:], AX.X, ALU.max))
                    V.tensor_tensor(oh[:].rearrange("p e t -> p t e"), eq[:], bc(lmx[:], R), ALU.is_equal).then_inc(m["rt_oh"], 1)
                    ch.link(V.tensor_tensor(lsum[:], le[:, :, 0], p1[:], ALU.add))
                    ch.link(V.tensor_scalar(lsum[:], lsum[:], 1e-9, None, ALU.max))
                    ch.link(V.reciprocal(lsum[:], lsum[:]))
                    V.tensor_tensor(gate0[:], le[:, :, 0], lsum[:], ALU.mult)
                    V.tensor_tensor(gate1[:], p1[:], lsum[:], ALU.mult)
                    v.wait_ge(m["rt_pre"], 1)
                    V.tensor_copy(pre[:], bank[3][:, 0:R * NT].rearrange("p (e t) -> p e t", e=R))
                    tot = bank[3][:, 256:256 + R * NT].rearrange("p (e t) -> p e t", e=R)
                    ch.link(V.tensor_copy(cum[0][:], tot))
                    a = 0
                    for sh in (1, 2, 4, 8, 16):
                        V.tensor_copy(cum[1 - a][:, :, 0:sh], cum[a][:, :, 0:sh])
                        ch.link(V.tensor_tensor(cum[1 - a][:, :, sh:], cum[a][:, :, sh:], cum[a][:, :, 0:NT - sh], ALU.add))
                        a = 1 - a
                    ch.link(V.tensor_tensor(cnt[:], cum[a][:, :, NT - 1:NT].broadcast_to([P, R, NT]),
                                            it128[:].rearrange("p (o t) -> p o t", o=1).broadcast_to([P, R, NT]), ALU.is_gt))
                    V.memset(st_e[:], 0.0)
                    ch.link(V.tensor_reduce(ntl[:], cnt[:], AX.X, ALU.add))
                    for e in range(R):
                        ch.link(V.tensor_tensor(st_e[:, e + 1:e + 2], st_e[:, e:e + 1], ntl[:, e:e + 1], ALU.add))
                    ch.link(V.tensor_tensor(cum[a][:], cum[a][:], tot, ALU.subtract))
                    ch.link(V.tensor_tensor(pre[:], pre[:], cum[a][:], ALU.add))
                    ch.link(V.scalar_tensor_tensor(out=pre[:], in0=be(st_e[:, 0:R]), scalar=float(P), in1=pre[:], op0=ALU.mult, op1=ALU.add))
                    ch.link(V.tensor_tensor(pre[:], pre[:], oh[:], ALU.mult))
                    ch.link(V.tensor_reduce(slotf[:], pre[:].rearrange("p e t -> p t e"), AX.X, ALU.add))
                    V.tensor_copy(slot[:], slotf[:])
                    ch.link(V.tensor_tensor(ge[:], gidx[:].rearrange("p (o g) -> p o g", o=1).broadcast_to([1, R - 1, NF + 2]),
                                            st_e[0:1, 1:R].rearrange("p (e o) -> p e o", o=1).broadcast_to([1, R - 1, NF + 2]), ALU.is_ge))
                    ch.link(V.tensor_reduce(rtf[:, 0, :], ge[:].rearrange("p e g -> p g e"), AX.X, ALU.add))
                    V.tensor_tensor(rtf[:, 0, :], rtf[:, 0, :], last[:], ALU.add)
                    ch.link(V.tensor_tensor(ge[:, 0:3, :], ge[:, 0:6:2, :], ge[:, 1:6:2, :], ALU.subtract))
                    ch.link(V.tensor_reduce(rtf[:, 1, :], ge[:, 0:3, :].rearrange("p e g -> p g e"), AX.X, ALU.add))
                    ch.link(V.tensor_tensor(rtf[:, 1, :], rtf[:, 1, :], last[:], ALU.add))
                    V.tensor_copy(end_tab[0:1, 0:R], st_e[0:1, 1:R + 1])
                    V.tensor_copy(rank_tab[:], rtf[:, 0, :])
                    V.tensor_copy(par_tab[:], rtf[:, 1, :]).then_inc(m["rt_done"], 1)

                    v.wait_ge(m["xt_dve"], NS)
                    for k in range(KD):
                        ins = V.tensor_reduce(pool_t[:, k, 0, :], xnt[:, k, W:W + S].rearrange("p (n c) -> p n c", n=NL), AX.X, ALU.add)
                    ch.link(ins)
                    ch.link(V.tensor_scalar(pool_t[:, :, 0, :], pool_t[:, :, 0, :], 1.0 / (S // NL), None, ALU.mult))
                    V.tensor_copy(pool_t[:, :, 1, :], pool_t[:, :, 0, :]).then_inc(m["pooled"], 1)
                    v.wait_ge(m["gk_ps"], 1)
                    V.tensor_tensor(gkbd[:], bank[4][:, 0:NL].rearrange("p (o n) -> p o n", o=1).broadcast_to([P, GH, NL]),
                                    hmask[:].rearrange("p (h o) -> p h o", o=1).broadcast_to([P, GH, NL]), ALU.mult)
                    pm = pmask[:].rearrange("p (a b o) -> p a b o", a=1, o=1)
                    gv4 = gvbd[:].rearrange("p (a b) v -> p a b v", b=2)
                    for b in range(2):
                        V.tensor_scalar(gv4[:, :, b, 0:HD], bank[4][:, 256:256 + P].rearrange("p (a b d) -> p a b d", b=2, d=HD)[:, :, b, :],
                                        pmask[:, b:b + 1], None, ALU.mult)
                    V.tensor_copy(gv4[:, :, :, HD:VW], pm.broadcast_to([P, 4, 2, 1])).then_inc(m["gk_done"], 1)
                    v.wait_ge(m["wprep"], 1)
                    v.wait_ge(m["w_in"], 16 * 11)
                    for g2 in range(2):
                        for j in range(2):
                            ins = V.tensor_scalar(gw[:, g2, H * j + GH * g2:H * j + GH * g2 + GH], hmask[:], gw_raw[:, g2, j:j + 1], None, ALU.mult)
                    ins.then_inc(m["gmats"], 1)

                    with v.Fori(0, NS) as s:
                        ch.loop(s, 5 * SUP)

                        def maxes(n):
                            return sum(1 if unit(k)[1] < 0 else 2 for k in range(n))

                        for p_ in (1, 3, 5, 7, 9, 11):
                            v.wait_ge(m["proj_ps"], s * 13 + p_ + 1)
                            if p_ < 4:
                                ins = V.tensor_copy(qt[:, p_ // 2, p_ % 2, :], bank[p_][:])
                            elif p_ == 5:
                                ins = V.tensor_copy(kt[:, 1, W:], bank[5][:])
                            elif p_ == 7:
                                ins = V.tensor_copy(gqt[:], bank[7][:])
                            else:
                                ins = V.tensor_copy(v2[:, p_ - 8, :, 0:HD], bank[p_ - 8][:, 0:D].rearrange("p (h d) -> p h d", d=HD))
                            ins.then_inc(m["proj_d"], 1)
                        for n in range(STEPS):
                            if n < NU:
                                i, u = unit(n)
                                b_ = n % 2
                                v.wait_ge(m["s_ps"], s * NU + n + 1)
                                if u < 0:
                                    src = bank[7][:].rearrange("p (h n) -> p h n", h=GH)
                                    V.tensor_reduce(mx[b_][:], src, AX.X, ALU.max).then_inc(m["mx_done"], 1)
                                    dst = sub[b_][:].rearrange("p a b -> p (a b)")[:, 0:512].rearrange("p (h n) -> p h n", h=GH)
                                    v.wait_ge(m["mx_done"], s * (9 * SUP) + maxes(n + 1))
                                    if n >= 2:
                                        v.wait_ge(m["p_exp"], s * NU + n - 1)
                                    V.tensor_tensor(dst, src, mx[b_][:].rearrange("p (h o) -> p h o", o=1).broadcast_to([P, GH, NL]),
                                                    ALU.subtract).then_inc(m["s_sub"], 1)
                                else:
                                    jp = u % 2
                                    for q in range(2):
                                        src = bank[2 * jp + q][:].rearrange("p (h k) -> p h k", h=2)[:, :, 0:KW]
                                        V.tensor_reduce(mx[b_][:, 2 * q:2 * q + 2], src, AX.X, ALU.max).then_inc(m["mx_done"], 1)
                                    v.wait_ge(m["mx_done"], s * (9 * SUP) + maxes(n + 1))
                                    if n >= 2:
                                        v.wait_ge(m["p_exp"], s * NU + n - 1)
                                    for q in range(2):
                                        src = bank[2 * jp + q][:].rearrange("p (h k) -> p h k", h=2)[:, :, 0:KW]
                                        ins = V.tensor_tensor(sub[b_][:, 2 * q:2 * q + 2, :], src,
                                                              mx[b_][:, 2 * q:2 * q + 2].rearrange("p (h o) -> p h o", o=1).broadcast_to([P, 2, KW]), ALU.subtract)
                                    ins.then_inc(m["s_sub"], 1)
                            if 1 <= n <= NU:
                                i, u = unit(n - 1)
                                v.wait_ge(m["pt_ps"], s * NU + n)
                                if n >= 3:
                                    v.wait_ge(m["pv"], s * NU + n - 2)
                                if u < 0:
                                    V.memset(pt2[(n - 1) % 2][0:1, 0:1], 0.0).then_inc(m["pt_d"], 1)
                                else:
                                    V.tensor_copy(pt2[(n - 1) % 2][:], bank[5][0:W, :]).then_inc(m["pt_d"], 1)
                            if n - (UN - 1) - LAG >= 0 and (n - (UN - 1) - LAG) % UN == 0 and (n - (UN - 1) - LAG) // UN < SUP:
                                i = (n - (UN - 1) - LAG) // UN
                                v.wait_ge(m["o_a"], s * SUP + i + 1)
                                o3 = osb[:, 0:272].rearrange("p (h v) -> p h v", v=VW)
                                r3 = osb[:, 272:408].rearrange("p (h v) -> p h v", v=VW)
                                V.tensor_scalar(gsg[:], gsg[:], 1.0, None, ALU.add)
                                V.reciprocal(rcp[:, 0:H], o3[:, :, HD])
                                ch.link(V.reciprocal(rcp[:, H:H + GH], r3[:, :, HD]))
                                V.tensor_tensor(remn[:], r3[:, :, 0:HD], rcp[:, H:H + GH].rearrange("p (h o) -> p h o", o=1).broadcast_to([P, GH, HD]), ALU.mult).then_inc(m["cmb1"], 1)
                                ch.link(V.reciprocal(gsg[:], gsg[:]))
                                ch.link(V.tensor_tensor(rcp[:, 0:H], rcp[:, 0:H], gsg[:, 0, :], ALU.mult))
                                ch.link(V.tensor_tensor(loc[:], o3[:, :, 0:HD], rcp[:, 0:H].rearrange("p (h o) -> p h o", o=1).broadcast_to([P, H, HD]), ALU.mult))
                            if tail(n):
                                i, stage = tail(n)
                                if stage == 1:
                                    v.wait_ge(m["rem_ps"], s * SUP + i + 1)
                                    ch.link(V.tensor_tensor(mix[:], bank[7][:, 0:D].rearrange("p (h d) -> p h d", d=HD),
                                                            gsg[:, 1, :].rearrange("p (h o) -> p h o", o=1).broadcast_to([P, H, HD]), ALU.mult))
                                    V.tensor_tensor(mix[:], mix[:], loc[:], ALU.add).then_inc(m["cmb2"], 1)
                                elif stage == 3:
                                    v.wait_ge(m["o_ps"], s * SUP + i + 1)
                                    at_ = acc[:, bass.ds(s * SUP + i, 1), :].rearrange("p o d -> p (o d)")
                                    V.tensor_tensor(at_, bank[7][:, 0:D], at_, ALU.add).then_inc(m["o_d"], 1)
                        ch.done(NS)

                @block.scalar
                def _(a):
                    A = nc.scalar
                    a.wait_ge(m["consts"], 1)
                    with a.Fori(0, NS // 2) as i:
                        for j in range(2):
                            a.wait_ge(m["rstd_d"], i * 2 + (j + 1))
                            A.activation(rstd[:], mv[:, :, 1], ACT.Sqrt, bias=eps_t[:]).then_inc(m["rstd_a"], 1)
                            a.wait_ge(m["xt_ps"], i * 2 + (j + 1))
                            A.copy(xts[j][:, 0, :], bank[0][:])
                            A.copy(xts[j][:, 1, :], bank[1][:]).then_inc(m["xt_act"], 1)
                    a.wait_ge(m["rt_exp"], 1)
                    A.activation(le[:], le[:], ACT.Exp).then_inc(m["rt_exp"], 1)
                    with a.Fori(0, NS) as s:
                        for p_ in (0, 2, 4, 6, 8, 10, 12):
                            a.wait_ge(m["proj_ps"], s * 13 + p_ + 1)
                            if p_ < 4:
                                ins = A.copy(qt[:, p_ // 2, p_ % 2, :], bank[p_][:])
                            elif p_ == 4:
                                ins = A.copy(kt[:, 0, W:], bank[4][:])
                            elif p_ == 6:
                                ins = A.copy(kt[:, :, 0:W], bank[6][:, 0:2 * W].rearrange("p (g k) -> p g k", g=2))
                            else:
                                ins = A.copy(v2[:, p_ - 8, :, 0:HD], bank[p_ - 8][:, 0:D].rearrange("p (h d) -> p h d", d=HD))
                            ins.then_inc(m["proj_a"], 1)
                        for n in range(STEPS):
                            if 1 <= n <= NU:
                                a.wait_ge(m["pt_ps"], s * NU + n)
                                if n >= 3:
                                    a.wait_ge(m["pv"], s * NU + n - 2)
                                A.copy(pt1[(n - 1) % 2][:], bank[4][:]).then_inc(m["pt_a"], 1)
                            if n < NU:
                                i, u = unit(n)
                                b_ = n % 2
                                a.wait_ge(m["s_sub"], s * NU + n + 1)
                                if n >= 2:
                                    a.wait_ge(m["pt_ps"], s * NU + n - 1)
                                w_ = 512 if u < 0 else 4 * KW
                                A.activation(prob[b_][:].rearrange("p a b -> p (a b)")[:, 0:w_], sub[b_][:].rearrange("p a b -> p (a b)")[:, 0:w_],
                                             ACT.Exp, scale=HD ** -0.5).then_inc(m["p_exp"], 1)
                            q = n - (UN - 1) - LAG
                            if q >= 0 and q % UN == 0 and q // UN < SUP:
                                i = q // UN
                                a.wait_ge(m["pv"], s * NU + n - LAG + 1)
                                if i:
                                    a.wait_ge(m["cmb2"], s * SUP + i)
                                A.copy(osb[:, 0:408], bank[6][:, 0:408])
                                A.activation(gsg[:].rearrange("p a b -> p (a b)"), bank[6][:, 408:440], ACT.Exp, scale=-1.0).then_inc(m["o_a"], 1)
                            if tail(n):
                                i, stage = tail(n)
                                if stage == 0:
                                    a.wait_ge(m["xr_ps"], s * SUP + i + 1)
                                    A.copy(remt[:], bank[7][:, 0:P]).then_inc(m["xr_a"], 1)
                                elif stage == 2:
                                    a.wait_ge(m["yt_ps"], s * SUP + i + 1)
                                    A.copy(mixt[:].rearrange("p k t -> p (k t)"), bank[7][:, 0:D]).then_inc(m["yt_a"], 1)
                        a.wait_ge(m["cmb2"], s * SUP + SUP)

        ffn = ExitStack()
        with ffn:
            def sf(name, shape, dt=F32):
                return sb(name, shape, dt, ffn)

            st13 = sf("st13", [P, KD, 2, FF])
            st2 = sf("st2", [P, FT, D])
            w13h = sf("w13h", [P, 2, KD, 2, FF], F32R)
            w13l = sf("w13l", [P, 2, KD, 2, FF], F32R)
            w2h = sf("w2h", [P, 2, FT, D], F32R)
            w2l = sf("w2l", [P, 2, FT, D], F32R)
            xin = [sf(f"xin{j}", [P, D]) for j in range(2)]
            fxh = sf("fxh", [P, KD, P], F32R)
            fxl = sf("fxl", [P, KD, P], F32R)
            sl = sf("sl", [P, 2, 512])
            gtick = sf("gtick", [1, 1])
            gtick0 = sf("gtick0", [1, 1])
            hs = sf("hs", [P, FF])
            hth = sf("hth", [P, FF], F32R)
            htl = sf("htl", [P, FF], F32R)
            ysb = [sf(f"ysb{j}", [P, D]) for j in range(2)]
            gat = [sf(f"gat{j}", [P, D]) for j in range(4)]

            blk2 = nc.Block()
            with blk2 as block:
                @block.sync
                def _(sp):
                    def load(g, j, rows):
                        sp.dma_start(xin[j][:], rows).then_inc(xin_in[j], 16)

                    load(0, 0, xg_rows[0:P, :])
                    load(1, 1, xg_rows[P:2 * P, :])
                    with sp.Fori(0, NG // 2 - 1) as i:
                        for j in range(2):
                            sp.wait_ge(m["xt2_ps"], i * 2 + (j + 1))
                            load(None, j, xg_rows[bass.ds(i * (2 * P) + (2 + j) * P, P), :])
                            sp.wait_ge(m["y_sb"], i * 2 + (j + 1))
                            sp.dma_start(yg_rows[bass.ds(i * (2 * P) + j * P, P), :], ysb[j][:]).then_inc(y_out[j], 16)
                    for j in range(2):
                        sp.wait_ge(m["xt2_ps"], NG - 1 + j)
                        load(None, j, xn_rows[j * P:j * P + P, :])
                        sp.wait_ge(m["y_sb"], NG - 1 + j)
                        sp.dma_start(yg_rows[(NG - 2 + j) * P:(NG - 1 + j) * P, :], ysb[j][:]).then_inc(y_out[j], 16)
                    with sp.Fori(0, NT // 2 - 1) as i:
                        for j in range(2):
                            sp.wait_ge(m["xt2_ps"], i * 2 + (NG + j + 1))
                            load(None, j, xn_rows[bass.ds(i * (2 * P) + (2 + j) * P, P), :])
                            sp.wait_ge(m["y_sb"], i * 2 + (NG + j + 1))
                            sp.dma_start(out[bass.ds(i * (2 * P) + j * P, P), :], ysb[j][:]).then_inc(y_out[j], 16)
                    for j in range(2):
                        sp.wait_ge(m["y_sb"], NF - 1 + j)
                        sp.dma_start(out[(NT - 2 + j) * P:(NT - 1 + j) * P, :], ysb[j][:]).then_inc(y_out[j], 16)
                    for j in range(2):
                        sp.wait_ge(y_out[j], 16 * (NF // 2))

                @block.scalar
                def _(a):
                    A = nc.scalar
                    w1v = w1_t.rearrange("e (k p) f -> e p k f", p=P)
                    w3v = w3_t.rearrange("e (k p) f -> e p k f", p=P)
                    w2v = w2_t.rearrange("e (k p) n -> e p k n", p=P)

                    def x_hi(g):
                        a.wait_ge(m["xt2_ps"], g + 1)
                        A.copy(fxh[:].rearrange("p k t -> p (k t)"), bank[7][:, 0:D]).then_inc(m["xh2"], 1)

                    def body(g, nxt):
                        for q in range(2):
                            a.wait_ge(m["u_ps"], g * 2 + (q + 1))
                            A.activation(sl[:, q, :], bank[2 * q][:], ACT.Silu).then_inc(m["silu"], 1)
                        if nxt:
                            x_hi(g + 1)
                        a.wait_ge(m["ht_ps"], g + 1)
                        for q in range(2):
                            A.copy(hth[:, 512 * q:512 * q + 512], bank[4 + q][:]).then_inc(m["hh"], 1)

                    x_hi(0)
                    body(0, True)
                    with a.Fori(0, NF // 2 - 1) as i:
                        for j in range(2):
                            body(i * 2 + (1 + j), True)
                    body(NF - 1, False)

                @block.gpsimd
                def _(g):
                    G = nc.gpsimd
                    w1v = w1_t.rearrange("e (k p) f -> e p k f", p=P)
                    w3v = w3_t.rearrange("e (k p) f -> e p k f", p=P)
                    w2v = w2_t.rearrange("e (k p) n -> e p k n", p=P)
                    stores = [0]

                    def stage(e):
                        G.dma_start(st13[:, :, 0, :], w1v[e]).then_inc(m["stage"], 16)
                        G.dma_start(st13[:, :, 1, :], w3v[e]).then_inc(m["stage"], 16)
                        G.dma_start(st2[:], w2v[e]).then_inc(m["stage"], 16)

                    G.memset(gtick0[:], 0.0).then_inc(m["gt"], 1)
                    g.wait_ge(m["gt"], 1)
                    stage(0)
                    for e in range(E):
                        b = e % 2
                        if e >= 2:
                            g.wait_ge(m["y_ps"], g.value_load(end_tab[0:1, e - 2:e - 1], min_val=0, max_val=NG) + 1)
                            G.tensor_tensor(gtick[:], gtick0[:], gtick0[:], ALU.add)
                        g.wait_ge(m["stage"], 48 * (e + 1))
                        G.tensor_copy(w13h[:, b], st13[:]).then_inc(m["st_done"], 1)
                        G.tensor_copy(w2h[:, b], st2[:]).then_inc(m["st_done"], 1)
                        g.wait_ge(m["st_done"], 4 * e + 2)
                        G.tensor_tensor(w13l[:, b], st13[:], w13h[:, b].bitcast(F32), ALU.subtract).then_inc(m["st_done"], 1)
                        G.tensor_tensor(w2l[:, b], st2[:], w2h[:, b].bitcast(F32), ALU.subtract).then_inc(m["st_done"], 1)
                        g.wait_ge(m["st_done"], 4 * e + 4)
                        if e + 1 < E:
                            stage(e + 1)
                        G.memset(gat[0][0:1, 0:1], 0.0).then_inc(m["w_split"], 1)
                    for j in range(2):
                        g.wait_ge(y_out[j], 16 * (NG // 2))
                    g.wait_ge(m["w_split"], E)
                    for t in range(NT):
                        if t >= 4:
                            g.wait_ge(m["fin"], t - 3)
                        G.indirect_dma_start(gat[t % 4][:], None, yg_rows, bass.IndirectOffsetOnAxis(slot[:, t:t + 1], 0)).then_inc(gath[t % 4], 16)

                @block.tensor
                def _(pe):
                    T = nc.tensor

                    def x_turn(pair, j):
                        pe.wait_ge(xin_in[j], pair * 16 + 16)
                        for k in range(KD):
                            last_ = T.transpose(bank[7][:, P * k:P * k + P], xin[j][:, P * k:P * k + P], ident[:])
                        last_.then_inc(m["xt2_ps"], 1)

                    def up(g, first):
                        rank = pe.value_load(rank_tab[0:1, bass.ds(g, 1)], min_val=0, max_val=E - 1)
                        par = pe.value_load(par_tab[0:1, bass.ds(g, 1)], min_val=0, max_val=1)
                        pe.wait_ge(m["w_split"], rank + 1)
                        pe.wait_ge(m["xh2"], g + 1)
                        pe.wait_ge(m["xl2"], g + 1)
                        for q in range(2):
                            if not first:
                                pe.wait_ge(m["h_sb"], g * 2 + (q - 1))
                            cnt_ = [0, 0]
                            for k in range(KD):
                                for st_, wt in ((fxh, w13h), (fxh, w13l), (fxl, w13h)):
                                    for ab in range(2):
                                        cnt_[ab] += 1
                                        last_ = T.matmul(bank[2 * q + ab][:], st_[:, k, :],
                                                         wt[:, bass.ds(par, 1), k, ab, 512 * q:512 * q + 512].rearrange("p o f -> p (o f)"),
                                                         start=(cnt_[ab] == 1), stop=(cnt_[ab] == 3 * KD))
                            last_.then_inc(m["u_ps"], 1)

                    def h_turn(g):
                        pe.wait_ge(m["h_sb"], g * 2 + 2)
                        for c in range(FT):
                            last_ = T.transpose(bank[4 + c // 4][:, P * (c % 4):P * (c % 4) + P], hs[:, P * c:P * c + P], ident[:])
                        last_.then_inc(m["ht_ps"], 1)

                    def down(g, first):
                        par = pe.value_load(par_tab[0:1, bass.ds(g, 1)], min_val=0, max_val=1)
                        pe.wait_ge(m["hl"], g * 2 + 2)
                        if not first:
                            pe.wait_ge(m["y_sb"], g)
                        n = 0
                        for c in range(FT):
                            for st_, wt in ((hth, w2h), (hth, w2l), (htl, w2h)):
                                last_ = T.matmul(bank[6][:, 0:D], st_[:, P * c:P * c + P], wt[:, bass.ds(par, 1), c, :].rearrange("p o n -> p (o n)"),
                                                 start=(n == 0), stop=(n == 3 * FT - 1))
                                n += 1
                        last_.then_inc(m["y_ps"], 1)

                    pe.sem_inc(m["y_ps"], 1)
                    x_turn(0, 0)
                    up(0, True)
                    x_turn(0, 1)
                    h_turn(0)
                    up(1, False)
                    x_turn(1, 0)
                    down(0, True)
                    h_turn(1)
                    with pe.Fori(0, (NF - 4) // 2) as i:
                        for j in range(2):
                            g = i * 2 + (2 + j)
                            up(g, False)
                            x_turn(i + 1 + j, (j + 1) % 2)
                            down(g - 1, False)
                            h_turn(g)
                    up(NF - 2, False)
                    x_turn(NF // 2 - 1, 1)
                    down(NF - 3, False)
                    h_turn(NF - 2)
                    up(NF - 1, False)
                    down(NF - 2, False)
                    h_turn(NF - 1)
                    down(NF - 1, False)

                @block.vector
                def _(v):
                    V = nc.vector

                    def x_lo(g):
                        v.wait_ge(m["xh2"], g + 1)
                        V.tensor_tensor(fxl[:].rearrange("p k t -> p (k t)"), bank[7][:, 0:D], fxh[:].rearrange("p k t -> p (k t)").bitcast(F32), ALU.subtract).then_inc(m["xl2"], 1)

                    def front(g, nxt):
                        for q in range(2):
                            v.wait_ge(m["silu"], g * 2 + (q + 1))
                            V.tensor_tensor(hs[:, 512 * q:512 * q + 512], sl[:, q, :], bank[2 * q + 1][:], ALU.mult).then_inc(m["h_sb"], 1)
                        if nxt:
                            x_lo(g + 1)

                    def back(g):
                        for q in range(2):
                            v.wait_ge(m["hh"], g * 2 + (q + 1))
                            V.tensor_tensor(htl[:, 512 * q:512 * q + 512], bank[4 + q][:], hth[:, 512 * q:512 * q + 512].bitcast(F32), ALU.subtract).then_inc(m["hl"], 1)

                    def routed_out(g, j, pair, ring):
                        v.wait_ge(m["y_ps"], g + 2)
                        if ring:
                            v.wait_ge(y_out[j], pair * 16)
                        V.tensor_copy(ysb[j][:], bank[6][:, 0:D]).then_inc(m["y_sb"], 1)

                    def final_out(t, j, q, quad, half):
                        at_ = acc[:, bass.ds(t, 1), :].rearrange("p o d -> p (o d)")
                        v.wait_ge(gath[q], quad * 16 + 16)
                        V.scalar_tensor_tensor(out=at_, in0=gat[q][:], scalar=gate1[:, bass.ds(t, 1)], in1=at_, op0=ALU.mult, op1=ALU.add).then_inc(m["fin"], 1)
                        v.wait_ge(m["fin"], t + 1)
                        v.wait_ge(m["y_ps"], t + (NG + 2))
                        v.wait_ge(y_out[j], half * 16 + (NG // 2) * 16)
                        V.scalar_tensor_tensor(out=ysb[j][:], in0=bank[6][:, 0:D], scalar=gate0[:, bass.ds(t, 1)], in1=at_, op0=ALU.mult, op1=ALU.add).then_inc(m["y_sb"], 1)

                    x_lo(0)
                    front(0, True)
                    back(0)
                    for g in (1, 2):
                        front(g, True)
                        routed_out(g - 1, (g - 1) % 2, 0, False)
                        back(g)
                    with v.Fori(0, (NG - 2) // 2) as i:
                        for j in range(2):
                            g = i * 2 + (3 + j)
                            front(g, True)
                            routed_out(g - 1, j % 2, i + 1, True)
                            back(g)
                    with v.Fori(0, (NT - 4) // 4) as i:
                        for j in range(4):
                            t = i * 4 + j
                            front(t + (NG + 1), True)
                            final_out(t, j % 2, j, i, i * 2 + j // 2)
                            back(t + (NG + 1))
                    for t in range(NT - 4, NT - 1):
                        front(t + NG + 1, t + NG + 1 < NF - 1)
                        final_out(t, t % 2, t % 4, t // 4, t // 2)
                        back(t + NG + 1)
                    final_out(NT - 1, 1, 3, NT // 4 - 1, NT // 2 - 1)


def kernel(**inputs):
    import numpy as _np
    import concourse.bacc as _bacc
    from concourse import mybir as _mybir
    from concourse.bass_utils import run_bass_kernel_spmd as _run

    a = {k: _np.asarray(v) for k, v in inputs.items()}
    order = list(range(1, E)) + [0]
    feed = {
        "x": a["L0_attn_x"].reshape(S, D),
        "wq": a["L0_attn_wq"], "wk": a["L0_attn_wk"], "wv": a["L0_attn_wv"],
        "wgq": a["L0_attn_wgq"], "wgk": a["L0_attn_wgk"], "wgv": a["L0_attn_wgv"],
        "r_out": a["L0_attn_r_out_w"], "gate_l": a["L0_attn_gate_local_w"], "gate_r": a["L0_attn_gate_remote_w"],
        "w_out": a["L0_attn_w_out"], "wr_t": a["L0_ffn_Wr"].T,
        "w1_t": a["L0_ffn_W1"][order].transpose(0, 2, 1), "w3_t": a["L0_ffn_W3"][order].transpose(0, 2, 1),
        "w2_t": a["L0_ffn_W2"][order].transpose(0, 2, 1),
    }
    nc = _bacc.Bacc("TRN2", target_bir_lowering=False, num_devices=1)
    arrays, args = {}, []
    for name, v in feed.items():
        v = _np.ascontiguousarray(v)
        arrays[f"in_{name}"] = v
        args.append(nc.dram_tensor(f"in_{name}", v.shape, _mybir.dt.from_np(v.dtype), kind="ExternalInput").ap())
    args.append(nc.dram_tensor("out_y", (S, D), _mybir.dt.float32, kind="ExternalOutput").ap())
    moe_block(nc, *args)
    r = _run(nc, [arrays], core_ids=[0])
    return r.results[0]["out_y"].reshape(1, S, D)
```

```python
from contextlib import ExitStack

import concourse.bass as bass
from concourse import mybir

ALU = mybir.AluOpType
ACT = mybir.ActivationFunctionType
AX = mybir.AxisListType
F32 = mybir.dt.float32
F32R = mybir.dt.float32r
BF16 = mybir.dt.bfloat16
I32 = mybir.dt.int32

P = 128
D = 256
KD = D // P
S = 4096
NT = S // P
SUP = 4
NS = NT // SUP
SW = SUP * P
H, HD = 16, 16
VW = HD + 1
GH = 8
NL = 64
W = 64
KW = W + P
E = 8
R = E - 1
FF = 1024
FT = FF // P
NG = (S + R * (P - 1)) // P
NF = NG + NT
NEG = -1.0e30
EPS = 1e-5


def moe_block(nc, x, wq, wk, wv, wgq, wgk, wgv, r_out, gate_l, gate_r, w_out, wr_t, w1_t, w3_t, w2_t, out):
    xn_rows = nc.dram_tensor("xn_rows", (S, D), F32, kind="Internal").ap()
    xg_rows = nc.dram_tensor("xg_rows", (NG * P, D), F32, kind="Internal").ap()
    yg_rows = nc.dram_tensor("yg_rows", (NG * P, D), F32, kind="Internal").ap()

    with ExitStack() as ctx:
        def sb(name, shape, dt=F32, c=ctx):
            return c.enter_context(nc.sbuf_tensor(name, shape, dt))

        def sem(name):
            return ctx.enter_context(nc.semaphore(name))

        bank = [ctx.enter_context(nc.psum_tensor(f"bank{i}", [P, 512], F32)) for i in range(8)]

        acc = sb("acc", [P, NT, D])
        ident = sb("ident", [P, P])
        ident_b = sb("ident_b", [P, P], BF16)
        slot = sb("slot", [P, NT], I32)
        gate0 = sb("gate0", [P, NT])
        gate1 = sb("gate1", [P, NT])
        rank_tab = sb("rank_tab", [1, NF + 2], I32)
        par_tab = sb("par_tab", [1, NF + 2], I32)
        end_tab = sb("end_tab", [1, 8], I32)

        names = """consts x_in w_in x_norm_t xn_out xt_ps xt_dve xt_act lg_ps lg_sb rstd_a rstd_d
            wprep pool_zero pooled zero_out rt_exp rt_oh rt_pre rt_done gk_ps gk_done gmats wqt_ps wqt_sb wg_ps wg_sb
            x_split proj_ps proj_a proj_d prev_k win_k win_v prev_v gate_e s_ps s_rd p_exp pt_ps pt_a pt_d pv o_a cmb cmb1 xr_ps xr_a rem_ps
            cmb2 yt_ps yt_a o_ps o_d mx_done
            stage st_done w_split xt2_ps xh2 xl2 u_ps silu h_sb ht_ps hh hl y_ps y_sb fin gt""".split()
        m = {n: sem("q_" + n) for n in names}
        x_in = [sem(f"q_x_in{j}") for j in range(2)]
        xn_out = [sem(f"q_xn_out{j}") for j in range(2)]
        tl_in = [sem(f"q_tl_in{j}") for j in range(4)]
        sc_out = [sem(f"q_sc_out{j}") for j in range(4)]
        xin_in = [sem(f"q_xin_in{j}") for j in range(2)]
        y_out = [sem(f"q_y_out{j}") for j in range(2)]
        gath = [sem(f"q_gath{j}") for j in range(4)]
        dch, ach, pch = sem("dve_chain"), sem("act_chain"), sem("pool_chain")

        class Chain:
            def __init__(self, eng, s):
                self.eng, self.s, self.n, self.base, self.per, self.it = eng, s, 0, 0, 0, None

            def link(self, ins):
                self.n += 1
                ins.then_inc(self.s, 1)
                v = self.base + self.n
                self.eng.wait_ge(self.s, v if self.it is None else self.it * self.per + v)

            def loop(self, it, per):
                self.it, self.per, self.base, self.n = it, per, self.base + self.n, 0

            def done(self, times):
                assert self.n == self.per, self.n
                self.base, self.n, self.it = self.base + times * self.per, 0, None

        att = ExitStack()
        with att:
            def sa(name, shape, dt=F32):
                return sb(name, shape, dt, att)

            xnt = sa("xnt", [P, KD, W + S + W])
            xn_t = [sa(f"xn_t{j}", [P, SUP, D]) for j in range(2)]
            xts = sa("xts", [P, KD, SW])
            stat = sa("stat", [P, SUP, 6])
            mv = sa("mv", [P, SUP, 2])
            rstd = sa("rstd", [P, SUP])
            tick_v = sa("tick_v", [1, 31])
            tick_g = sa("tick_g", [1, 31])
            eps_t = sa("eps_t", [P, 1])
            wrt = sa("wrt", [P, KD, E])
            logit = sa("logit", [P, NT, E])
            NW = 2 * D + D + P + D + 2 * H
            QC, KC, GC, VC = 0, 2 * D, 3 * D, 3 * D + P
            wraw = sa("wraw", [P, KD, 3 * D + 3 * P])
            wh = sa("wh", [P, KD, NW], F32R)
            wl = sa("wl", [P, KD, NW], F32R)
            rw = sa("rw", [P, D])
            ow = sa("ow", [P, KD, D])
            gw_raw = sa("gw_raw", [P, 2, 2])
            gw = sa("gw", [P, 2, 2 * H])
            hmask = sa("hmask", [P, GH])
            pmask = sa("pmask", [P, 2])
            mask = sa("mask", [P, 2, 2, KW])
            lmask = sa("lmask", [P, 2 * NL], BF16)
            pool_t = sa("pool_t", [P, KD, 2, NL])
            gkbd = sa("gkbd", [P, GH, NL])
            gvbd = sa("gvbd", [P, GH, VW])
            xh = sa("xh", [P, KD, SW], F32R)
            xl = sa("xl", [P, KD, SW], F32R)
            qt = sa("qt", [P, 2, 2, 2, SW])
            kt = sa("kt", [P, 2, 2, W + SW])
            ka = sa("ka", [P, 2, 2, SUP, KW])
            gqt = sa("gqt", [P, 2, SW])
            v2 = sa("v2", [P, 2 * SUP, H, VW])
            vp = sa("vp", [P, 2 * SUP, H, VW])
            wqt = xts[:, 0, :].rearrange("p (g d) -> p g d", g=2)
            mx = [sa(f"mx{j}", [P, 4]) for j in range(2)]
            lmx8 = sa("lmx8", [P, GH])
            units = wraw[:].rearrange("p k n -> p (k n)").rearrange("p (j c k) -> p j c k", j=3, c=4)
            sub = [units[:, j] for j in range(2)]
            prob = [units[:, 2], sa("prob1", [P, 4, KW])[:]]
            pt1 = [xts[:, j, :] for j in range(2)]
            pt2 = [sa(f"pt2_{j}", [P, 256]) for j in range(2)]
            osb = sa("osb", [P, 408])
            rcp = sa("rcp", [P, 24])
            gsg = sa("gsg", [P, 2 * SUP, 2, H])
            loc = sa("loc", [P, H, HD])
            remn = sa("remn", [P, GH, HD])
            remt = sa("remt", [P, P])
            mix = sa("mix", [P, H, HD])
            mixt = sa("mixt", [P, KD, P])
            zrow = sa("zrow", [P, D])
            u_tri = sa("u_tri", [P, P])
            ones = sa("ones", [P, P])
            it128 = sa("it128", [P, NT])
            wgt = sa("wgt", [P, R])
            gidx = sa("gidx", [1, NF + 2])
            last = sa("last", [1, NF + 2])
            lmx = sa("lmx", [P, NT])
            le = sa("le", [P, NT, E])
            lsum = sa("lsum", [P, NT])
            p1 = sa("p1", [P, NT])
            eq = sa("eq", [P, NT, R])
            oh = sa("oh", [P, R, NT])
            cum0, cum1, pre, cnt = [xn_t[1][:].rearrange("p t d -> p (t d)")[:, R * NT * j:R * NT * j + R * NT].rearrange("p (e t) -> p e t", e=R)
                                    for j in range(4)]
            cum = [cum0, cum1]
            ntl = sa("ntl", [P, R])
            st_e = sa("st_e", [P, R + 1])
            ge = sa("ge", [1, R - 1, NF + 2])
            rtf = sa("rtf", [1, 2, NF + 2])
            slotf = sa("slotf", [P, NT])
            tl = [xn_t[0][:, j, :] for j in range(4)]

            UN = 5
            HV = 9
            NU = SUP * UN
            LT, LP = 2, 3
            LAST = (NT - 1) * UN + 12

            def unit(k):
                return k // UN, (0, -1, 1, 2, 3)[k % UN]

            def halves(k):
                return k // UN * HV + (0, 2, 3, 5, 7)[k % UN], (1 if k % UN == 1 else 2)

            def plain(k):
                return k - (k + UN - 2) // UN

            def tail(k, r):
                t = (k - r) // UN
                return t if k >= r and (k - r) % UN == 0 and t < NT else None

            PIECE = {1: 0, 2: 1, 4: 2, 6: 3, 7: 4, 9: 5, 11: 6, 12: 7, 14: 8, 16: 9, 17: 10}
            NPC = 11
            PA = (2, 4, 6, 7, 8, 9, 10)
            pa_before = lambda p: sum(1 for q in PA if q < p)
            pd_before = lambda p: p - pa_before(p)

            def at(it, per, v):
                return v if it is None else it * per + v

            def await_(eng, s_, it, per, v):
                if it is not None or v > 0:
                    eng.wait_ge(s_, at(it, per, v))

            def steps(eng, step):
                for k in range(NU):
                    step(None, k)
                with eng.Fori(0, (NS - 2) // 2) as it:
                    for k in range(NU, 3 * NU):
                        step(it, k)
                for k in range((NS - 1) * NU, LAST + 1):
                    step(None, k)

            carried = [0, 0]

            def carry_v():
                carried[0] += 1
                c = carried[0] % 31
                nc.vector.memset(tick_v[:, c:c + 1], 0.0)

            def carry_g():
                carried[1] += 1
                c = carried[1] % 31
                nc.gpsimd.tensor_tensor(tick_g[:, c:c + 1], zrow[0:1, 0:1], zrow[0:1, 0:1], ALU.add)

            xr = x.rearrange("(t p) d -> p t d", p=P)

            blk = nc.Block()
            with blk as block:
                @block.sync
                def _(sp):
                    for s in range(NS):
                        if s >= 2:
                            sp.wait_ge(x_in[s % 2], 16 * (s // 2))
                        sp.dma_start(acc[:, SUP * s:SUP * s + SUP, :], xr[:, SUP * s:SUP * s + SUP, :]).then_inc(x_in[s % 2], 16)
                        if s == 0:
                            sp.dma_start(wrt[:], wr_t.rearrange("(k p) e -> p k e", p=P)).then_inc(m["w_in"], 16)
                            for w_, c in ((wq, 0), (wk, D), (wv, 2 * D), (wgq, 3 * D), (wgk, 3 * D + P), (wgv, 3 * D + 2 * P)):
                                sp.dma_start(wraw[:, :, c:c + w_.shape[1]], w_.rearrange("(k p) n -> p k n", p=P)).then_inc(m["w_in"], 16)
                            sp.dma_start(rw[:], r_out).then_inc(m["w_in"], 16)
                            sp.dma_start(ow[:], w_out.rearrange("(k p) n -> p k n", p=P)).then_inc(m["w_in"], 16)
                            for j, g in enumerate((gate_l, gate_r)):
                                sp.dma_start(gw_raw[:, :, j:j + 1], g.rearrange("(g h) (d o) -> (h d) g o", g=2, o=1),
                                             allow_slow_non_contiguous=True).then_inc(m["w_in"], 16)
                    sp.wait_ge(m["pool_zero"], 1)
                    sp.dma_start(xg_rows.rearrange("(g p) d -> p g d", p=P),
                                 zrow[:].rearrange("p (o d) -> p o d", o=1).broadcast_to([P, NG, D])).then_inc(m["zero_out"], 16)
                    with sp.Fori(0, NS // 2) as i:
                        for j in range(2):
                            sp.wait_ge(m["x_norm_t"], i * 2 + (j + 1))
                            sp.dma_start(xn_rows[bass.ds(i * (2 * SW) + j * SW, SW), :].rearrange("(t p) d -> p t d", p=P),
                                         xn_t[j][:]).then_inc(xn_out[j], 16)
                    for j in range(2):
                        sp.wait_ge(xn_out[j], 16 * (NS // 2))
                    for t in range(NT):
                        if t >= 4:
                            sp.wait_ge(sc_out[t % 4], 16 * (t // 4))
                        sp.dma_start(tl[t % 4], xn_rows[t * P:t * P + P, :]).then_inc(tl_in[t % 4], 16)

                @block.gpsimd
                def _(g):
                    ch = Chain(g, pch)
                    G = nc.gpsimd
                    G.memset(zrow[:], 0.0).then_inc(m["pool_zero"], 1)
                    G.memset(eps_t[:], EPS)
                    G.memset(ones[:], 1.0)
                    G.memset(v2[:].rearrange("p a h v -> p (a h v)"), 1.0)
                    G.memset(vp[:].rearrange("p a h v -> p (a h v)"), 0.0)
                    G.memset(kt[:, 0, :, 0:W], 0.0)
                    G.memset(xnt[:, :, 0:W], 0.0)
                    G.memset(xnt[:, :, W + S:], 0.0)
                    G.memset(hmask[:], 1.0)
                    G.memset(pmask[:], 1.0)
                    G.memset(ident[:], 0.0)
                    G.memset(u_tri[:], 1.0)
                    G.memset(mask[:], 0.0)
                    ch.link(G.memset(lmask[:], 0.0))
                    G.affine_select(out=ident[:], in_=ident[:], compare_op=ALU.not_equal, fill=1.0, base=0,
                                    pattern=[[-1, P]], channel_multiplier=1)
                    G.affine_select(out=u_tri[:], in_=u_tri[:], compare_op=ALU.is_gt, fill=0.0, base=0,
                                    pattern=[[1, P]], channel_multiplier=-1)
                    ch.link(G.affine_select(out=hmask[:], in_=hmask[:], compare_op=ALU.is_ge, fill=0.0, base=0,
                                            pattern=[[-HD, GH]], channel_multiplier=1))
                    ch.link(G.affine_select(out=hmask[:], in_=hmask[:], compare_op=ALU.is_ge, fill=0.0, base=HD - 1,
                                            pattern=[[HD, GH]], channel_multiplier=-1))
                    ch.link(G.affine_select(out=pmask[:], in_=pmask[:], compare_op=ALU.is_ge, fill=0.0, base=0,
                                            pattern=[[-NL, 2]], channel_multiplier=1))
                    ch.link(G.affine_select(out=pmask[:], in_=pmask[:], compare_op=ALU.is_ge, fill=0.0, base=NL - 1,
                                            pattern=[[NL, 2]], channel_multiplier=-1))
                    late = mask[:, :, 1, :]
                    ch.link(G.affine_select(out=late, in_=late, compare_op=ALU.is_gt, fill=NEG, base=0,
                                            pattern=[[0, 2], [1, KW]], channel_multiplier=-1))
                    ch.link(G.affine_select(out=late, in_=late, compare_op=ALU.is_ge, fill=NEG, base=W,
                                            pattern=[[0, 2], [-1, KW]], channel_multiplier=1))
                    ch.link(G.affine_select(out=mask[:, 0, 1, :], in_=mask[:, 0, 1, :], compare_op=ALU.is_ge, fill=NEG, base=-W,
                                            pattern=[[1, KW]], channel_multiplier=0))
                    G.tensor_copy(mask[:, :, 0, 0:P], mask[:, :, 1, W:])
                    G.tensor_copy(mask[:, :, 0, P:], mask[:, :, 1, 0:W])
                    ch.link(G.affine_select(out=lmask[:], in_=lmask[:], compare_op=ALU.is_ge, fill=NEG, base=NL * (NL - 2),
                                            pattern=[[-NL, 2 * NL]], channel_multiplier=1))
                    G.tensor_copy(ident_b[:], ident[:])
                    G.tensor_copy(vp[:].rearrange("p a (g b) v -> p (a g) b v", b=2)[:, :, :, HD:VW],
                                  pmask[:].rearrange("p (a b o) -> p a b o", a=1, o=1).broadcast_to([P, SUP * H, 2, 1]))
                    G.iota(it128[:], pattern=[[P, NT]], base=0, channel_multiplier=0, allow_small_or_imprecise_dtypes=True)
                    G.iota(wgt[:], pattern=[[-1, R]], base=R, channel_multiplier=0, allow_small_or_imprecise_dtypes=True)
                    ch.link(G.iota(gidx[:], pattern=[[1, NF + 2]], base=0, channel_multiplier=0, allow_small_or_imprecise_dtypes=True))
                    ch.link(G.tensor_scalar(last[:], gidx[:], float(NG), None, ALU.is_ge))
                    G.memset(wh[:, :, 0:2 * D].bitcast(F32), 0.0)
                    G.memset(wl[:, :, 0:2 * D].bitcast(F32), 0.0).then_inc(m["consts"], 1)
                    g.wait_ge(m["w_in"], 16 * 11)
                    g.wait_ge(m["consts"], 1)
                    q_raw = wraw[:, :, 0:D].rearrange("p k (a b d) -> p k a b d", b=2, d=HD)
                    for k in range(KD):
                        for b in range(2):
                            hv = wh[:, k, D * b:D * b + D].rearrange("p (a b d) -> p a b d", b=2, d=HD)[:, :, b, :]
                            lv = wl[:, k, D * b:D * b + D].rearrange("p (a b d) -> p a b d", b=2, d=HD)[:, :, b, :]
                            ch.link(G.tensor_copy(hv, q_raw[:, k, :, b, :]))
                            G.tensor_tensor(lv, q_raw[:, k, :, b, :], hv.bitcast(F32), ALU.subtract)
                        for c0, r0, n in ((KC, D, D), (VC, 2 * D, D), (GC, 3 * D, P)):
                            ch.link(G.tensor_copy(wh[:, k, c0:c0 + n], wraw[:, k, r0:r0 + n]))
                            G.tensor_tensor(wl[:, k, c0:c0 + n], wraw[:, k, r0:r0 + n], wh[:, k, c0:c0 + n].bitcast(F32), ALU.subtract)
                    G.memset(gw[:], 0.0).then_inc(m["wprep"], 1)
                    def split(s_, it=None):
                        cols = xnt[:, :, bass.ds(at(it, 2 * SW, W + s_ * SW), SW)]
                        if it is not None or s_:
                            g.wait_ge(m["proj_ps"], at(it, 2 * NPC, NPC * s_))
                        carry_g()
                        G.tensor_copy(xh[:], cols).then_inc(m["x_split"], 1)
                        g.wait_ge(m["x_split"], at(it, 4, 2 * s_ + 1))
                        carry_g()
                        G.tensor_tensor(xl[:], cols, xh[:].bitcast(F32), ALU.subtract).then_inc(m["x_split"], 1)

                    def windows(s_, it=None):
                        b, nd = s_ % 2, NPC - len(PA)
                        g.wait_ge(m["proj_d"], at(it, 2 * nd, nd * s_ + 2))
                        carry_g()
                        G.tensor_copy(ka[:, b, :, :, 0:P], kt[:, b, :, W:].rearrange("p g (i k) -> p g i k", i=SUP))
                        if it is not None or s_:
                            ch_k = m["win_k"]
                            G.tensor_copy(kt[:, b, :, 0:W], kt[:, 1 - b, :, SW:]).then_inc(ch_k, 1)
                            g.wait_ge(ch_k, at(it, 2, s_))
                            carry_g()
                        G.tensor_copy(ka[:, b, :, :, P:], kt[:, b, :, 0:SW].rearrange("p g (i k) -> p g i k", i=SUP)[:, :, :, 0:W]).then_inc(m["prev_k"], 1)
                        g.wait_ge(m["prev_k"], at(it, 2, s_ + 1))
                        for i in range(SUP):
                            g.wait_ge(m["proj_a"], at(it, 2 * len(PA), len(PA) * s_ + pa_before(7 + i) + 1))
                            carry_g()
                            n_ = (SUP * s_ + i) % (2 * SUP)
                            src = v2[W:P, n_].rearrange("p (g b) v -> p g b v", b=2)
                            to = vp[:, (n_ + 1) % (2 * SUP)].rearrange("p (g b) v -> p g b v", b=2)
                            G.tensor_copy(to[0:W, :, 0, 0:HD], src[:, :, 0, 0:HD]).then_inc(m["win_v"], 1)
                            g.wait_ge(m["win_v"], at(it, 2 * SUP, SUP * s_ + i + 1))
                            carry_g()
                            G.tensor_copy(to[W:P, :, 1, 0:HD], src[:, :, 1, 0:HD]).then_inc(m["prev_v"], 1)
                            g.wait_ge(m["prev_v"], at(it, 2 * SUP, SUP * s_ + i + 1))
                            carry_g()

                    g.wait_ge(m["xt_dve"], NS)
                    split(0)
                    windows(0)
                    split(1)
                    g.wait_ge(m["rt_done"], 1)
                    g.wait_ge(m["zero_out"], 16)
                    for t in range(NT):
                        g.wait_ge(tl_in[t % 4], 16 * (t // 4 + 1))
                        G.indirect_dma_start(xg_rows, bass.IndirectOffsetOnAxis(slot[:, t:t + 1], 0), tl[t % 4], None).then_inc(sc_out[t % 4], 16)
                    for j in range(4):
                        g.wait_ge(sc_out[j], 16 * (NT // 4))
                    with g.Fori(0, (NS - 2) // 2) as it:
                        for s_ in (1, 2):
                            windows(s_, it)
                            split(s_ + 1, it)
                    windows(NS - 1)

                @block.tensor
                def _(pe):
                    T = nc.tensor
                    pe.wait_ge(m["consts"], 1)
                    with pe.Fori(0, NS // 2) as i:
                        for j in range(2):
                            pe.wait_ge(m["x_norm_t"], i * 2 + (j + 1))
                            if j:
                                pe.wait_ge(m["xt_dve"], i * 2 + 1)
                            for k in range(KD):
                                for t in range(SUP):
                                    last_ = T.transpose(bank[k][:, P * t:P * t + P], xn_t[j][:, t, P * k:P * k + P], ident[:])
                            last_.then_inc(m["xt_ps"], 1)
                            pe.wait_ge(m["xt_act"], i * 2 + (j + 1))
                            pe.wait_ge(m["w_in"], 16 * 11)
                            if j:
                                pe.wait_ge(m["lg_sb"], i * 2 + 1)
                            for t in range(SUP):
                                for k in range(KD):
                                    last_ = T.matmul(bank[2][:, E * t:E * t + E], xts[:, k, P * t:P * t + P], wrt[:, k, :],
                                                     start=(k == 0), stop=(k == KD - 1))
                            last_.then_inc(m["lg_ps"], 1)
                        pe.wait_ge(m["xt_dve"], i * 2 + 2)
                        pe.wait_ge(m["lg_sb"], i * 2 + 2)
                    pe.wait_ge(m["rt_oh"], 1)
                    T.matmul(bank[3][:, 0:R * NT], u_tri[:], oh[:].rearrange("p e t -> p (e t)"), start=True, stop=True)
                    T.matmul(bank[3][:, 256:256 + R * NT], ones[:], oh[:].rearrange("p e t -> p (e t)"), start=True, stop=True).then_inc(m["rt_pre"], 1)
                    pe.wait_ge(m["pooled"], 1)
                    for k in range(KD):
                        T.matmul(bank[4][:, 0:NL], wraw[:, k, 3 * D + P:3 * D + 2 * P], pool_t[:, k, 0, :], start=(k == 0), stop=(k == KD - 1))
                    for k in range(KD):
                        last_ = T.matmul(bank[4][:, 256:256 + P], pool_t[:, k, :, :].rearrange("p a n -> p (a n)"),
                                         wraw[:, k, 3 * D + 2 * P:3 * D + 3 * P], start=(k == 0), stop=(k == KD - 1))
                    last_.then_inc(m["gk_ps"], 1)
                    pe.wait_ge(m["gk_done"], 1)
                    for g2 in range(2):
                        for k in range(KD):
                            last_ = T.transpose(bank[5][:, D * g2 + P * k:D * g2 + P * k + P], wraw[:, k, P * g2:P * g2 + P], ident[:])
                    last_.then_inc(m["wqt_ps"], 1)
                    pe.wait_ge(m["wqt_sb"], 1)
                    for k in range(KD):
                        for g2 in range(2):
                            last_ = T.matmul(bank[6][:, 2 * H * k:2 * H * k + 2 * H], wqt[:, g2, P * k:P * k + P], gw[:, g2, :], start=(g2 == 0), stop=(g2 == 1))
                    last_.then_inc(m["wg_ps"], 1)
                    pe.wait_ge(m["wprep"], 1)
                    pe.wait_ge(m["wg_sb"], 1)

                    def three(dst, stat_h, stat_l, mov_h, mov_l, ks):
                        n = 0
                        for k in ks:
                            for a, b in ((stat_h, mov_h), (stat_h, mov_l), (stat_l, mov_h)):
                                last_ = T.matmul(dst, a(k), b(k), start=(n == 0), stop=(n == 3 * len(ks) - 1))
                                n += 1
                        return last_

                    def project(p, dst):
                        if p < 7:
                            c = KC + P * p if p < 2 else QC + P * (p - 2) if p < 6 else GC
                            return three(dst[:], lambda k: wh[:, k, c:c + P], lambda k: wl[:, k, c:c + P],
                                         lambda k: xh[:, k, :], lambda k: xl[:, k, :], range(KD))
                        c = P * (p - 7)
                        return three(dst[:, 0:D + 2 * H], lambda k: xh[:, k, c:c + P], lambda k: xl[:, k, c:c + P],
                                     lambda k: wh[:, k, VC:VC + D + 2 * H], lambda k: wl[:, k, VC:VC + D + 2 * H], range(KD))

                    pe.wait_ge(m["x_split"], 2)
                    for p in range(NPC):
                        if p in (8, 9):
                            pe.wait_ge(m["proj_d"], p - 7)
                        elif p == 10:
                            pe.wait_ge(m["proj_a"], 1)
                        project(p, bank[p % 8]).then_inc(m["proj_ps"], 1)

                    def step(it, k):
                        s_ = k // NU
                        if k < NT * UN:
                            t, u = unit(k)
                            i, b = t % SUP, s_ % 2
                            if k % NU == 0:
                                pe.wait_ge(m["proj_a"], at(it, 2 * len(PA), len(PA) * (s_ + 1)))
                                pe.wait_ge(m["proj_d"], at(it, 2 * (NPC - len(PA)), (NPC - len(PA)) * (s_ + 1)))
                                pe.wait_ge(m["prev_k"], at(it, 2, s_ + 1))
                            h, nh = halves(k)
                            for q in range(nh):
                                await_(pe, m["s_rd"], it, 8 * HV, h + q - 2)
                                dst = bank[(h + q) % 3]
                                if u < 0:
                                    lat = lmask[:, at(it, -2 * 2 * SUP, NL - 2 - 2 * t):][:, 0:NL] if it is None else \
                                        lmask[:, bass.ds(it * (-2 * 2 * SUP) + (NL - 2 - 2 * t), NL)]
                                    T.matmul(dst[:].rearrange("p (h n) -> p h n", h=GH), ident_b[:],
                                             lat.rearrange("p (o n) -> p o n", o=1).broadcast_to([P, GH, NL]), start=True, stop=False)
                                    T.matmul(dst[:], gqt[:, b, P * i:P * i + P], gkbd[:].rearrange("p h n -> p (h n)"),
                                             start=False, stop=True).then_inc(m["s_ps"], 1)
                                else:
                                    g2, j = u // 2, 2 * (u % 2) + q
                                    for o in range(2):
                                        keys = ka[32 * j:32 * j + 32, b, g2, i, :] if o == 0 else kt[32 * j:32 * j + 32, b, g2, P * i:P * i + KW]
                                        last_ = T.matmul(dst[:, KW * o:KW * o + KW], qt[32 * j:32 * j + 32, b, o, g2, P * i:P * i + P],
                                                         keys, start=True, stop=True)
                                    last_.then_inc(m["s_ps"], 1)
                        n = k - LT
                        if 0 <= n < NT * UN:
                            u = unit(n)[1]
                            pe.wait_ge(m["p_exp"], at(it, 2 * NU, n + 1))
                            await_(pe, m["pt_a"], it, 2 * NU, n)
                            if u < 0:
                                pl = prob[n % 2].rearrange("p a b -> p (a b)")
                                for c in range(4):
                                    last_ = T.transpose(bank[4][:, P * c:P * c + P], pl[:, P * c:P * c + P], ident[:])
                            else:
                                await_(pe, m["pt_d"], it, 8 * (UN - 1), plain(n))
                                pr = prob[n % 2].rearrange("p a b -> p (a b)")
                                for q in range(2):
                                    c0 = 2 * KW * q
                                    T.transpose(bank[4][:, 2 * P * q:2 * P * q + P], pr[:, c0:c0 + P], ident[:])
                                    T.transpose(bank[4][:, 2 * P * q + P:2 * P * q + 2 * P], pr[:, c0 + 2 * P:c0 + 3 * P], ident[:])
                                    last_ = T.transpose(bank[5][:, P * q:P * q + P], pr[:, c0 + P:c0 + 2 * P], ident[:])
                            last_.then_inc(m["pt_ps"], 1)
                        if s_ < NS - 1 and k % NU in PIECE:
                            p = PIECE[k % NU]
                            if p == 0:
                                pe.wait_ge(m["x_split"], at(it, 4, 2 * s_ + 4))
                            g_ = NPC * (s_ + 1) + p - 1
                            if (p - 1) % NPC in PA:
                                pe.wait_ge(m["proj_a"], at(it, 2 * len(PA), len(PA) * (g_ // NPC) + pa_before(g_ % NPC) + 1))
                            else:
                                pe.wait_ge(m["proj_d"], at(it, 2 * (NPC - len(PA)), (NPC - len(PA)) * (g_ // NPC) + pd_before(g_ % NPC) + 1))
                            project(p, bank[3]).then_inc(m["proj_ps"], 1)
                        t = tail(k, 9)
                        if t is not None:
                            pe.wait_ge(m["cmb1"], at(it, 8, t + 1))
                            await_(pe, m["o_d"], it, 8, t)
                            T.transpose(bank[7][:, 0:P], remn[:].rearrange("p h d -> p (h d)"), ident[:]).then_inc(m["xr_ps"], 1)
                        t = tail(k, 10)
                        if t is not None:
                            pe.wait_ge(m["xr_a"], at(it, 8, t + 1))
                            T.matmul(bank[7][:, 0:D], remt[:], rw[:], start=True, stop=True).then_inc(m["rem_ps"], 1)
                        t = tail(k, 11)
                        if t is not None:
                            pe.wait_ge(m["cmb2"], at(it, 8, t + 1))
                            for kk in range(KD):
                                last_ = T.transpose(bank[7][:, P * kk:P * kk + P], mix[:].rearrange("p h d -> p (h d)")[:, P * kk:P * kk + P], ident[:])
                            last_.then_inc(m["yt_ps"], 1)
                        t = tail(k, 12)
                        if t is not None:
                            pe.wait_ge(m["yt_a"], at(it, 8, t + 1))
                            for kk in range(KD):
                                last_ = T.matmul(bank[7][:, 0:D], mixt[:, kk, :], ow[:, kk, :], start=(kk == 0), stop=(kk == KD - 1))
                            last_.then_inc(m["o_ps"], 1)
                        n = k - LP
                        if 0 <= n < NT * UN:
                            t, u = unit(n)
                            i = t % (2 * SUP)
                            pe.wait_ge(m["pt_a"], at(it, 2 * NU, n + 1))
                            if u < 0:
                                for c in range(4):
                                    last_ = T.matmul(bank[6][:, 272 + 34 * c:306 + 34 * c], pt1[n % 2][:, P * c:P * c + P],
                                                     gvbd[:, 2 * c:2 * c + 2, :].rearrange("p h v -> p (h v)"), start=True, stop=True)
                            else:
                                pe.wait_ge(m["pt_d"], at(it, 8 * (UN - 1), plain(n) + 1))
                                if u == 0:
                                    await_(pe, m["o_a"], it, 8, t)
                                    await_(pe, m["prev_v"], it, 8, t)
                                for q in range(2):
                                    h = 8 * (u // 2) + 2 * (2 * (u % 2) + q)
                                    T.matmul(bank[6][:, VW * h:VW * h + 2 * VW], pt2[n % 2][:, P * q:P * q + P],
                                             vp[:, i, h:h + 2, :].rearrange("p h v -> p (h v)"), start=True, stop=False)
                                    for o in range(2):
                                        last_ = T.matmul(bank[6][:, VW * (h + o):VW * (h + o) + VW], pt1[n % 2][:, P * (2 * q + o):P * (2 * q + o) + P],
                                                         v2[:, i, h + o, :], start=False, stop=(o == 1))
                            last_.then_inc(m["pv"], 1)

                    steps(pe, step)
                    pe.wait_ge(m["o_d"], NT)

                @block.vector
                def _(v):
                    V = nc.vector
                    ch = Chain(v, dch)
                    v.wait_ge(m["consts"], 1)
                    with v.Fori(0, NS // 2) as i:
                        ch.loop(i, 2 * 2)
                        for j in range(2):
                            v.wait_ge(x_in[j], i * 16 + 16)
                            for t in range(SUP):
                                ins = V.bn_stats(stat[:, t, :], acc[:, bass.ds(i * (2 * SUP) + (SUP * j + t), 1), :].rearrange("p o d -> p (o d)"))
                            ch.link(ins)
                            carry_v()
                            for t in range(SUP):
                                ins = V.bn_aggr(mv[:, t, :], stat[:, t, :])
                            ins.then_inc(m["rstd_d"], 1)
                            v.wait_ge(m["rstd_a"], i * 2 + (j + 1))
                            ch.link(V.reciprocal(rstd[:], rstd[:]))
                            for t in range(SUP):
                                ins = V.tensor_scalar(xn_t[j][:, t, :], acc[:, bass.ds(i * (2 * SUP) + (SUP * j + t), 1), :].rearrange("p o d -> p (o d)"),
                                                      mv[:, t, 0:1], rstd[:, t:t + 1], ALU.subtract, ALU.mult)
                            ins.then_inc(m["x_norm_t"], 1)
                            v.wait_ge(m["xt_act"], i * 2 + (j + 1))
                            for k in range(KD):
                                ins = V.tensor_copy(xnt[:, k, bass.ds(i * (2 * SW) + (W + SW * j), SW)], bank[k][:])
                            ins.then_inc(m["xt_dve"], 1)
                            v.wait_ge(m["lg_ps"], i * 2 + (j + 1))
                            V.tensor_copy(logit[:, bass.ds(i * (2 * SUP) + SUP * j, SUP), :],
                                          bank[2][:, 0:SUP * E].rearrange("p (t e) -> p t e", e=E)).then_inc(m["lg_sb"], 1)
                        for j in range(2):
                            v.wait_ge(xn_out[j], i * 16 + 16)
                        ch.done(NS // 2)

                    v.wait_ge(m["lg_sb"], NS)
                    bc = lambda a, n: a.rearrange("p (t o) -> p t o", o=1).broadcast_to([P, NT, n])
                    be = lambda a: a.rearrange("p (e o) -> p e o", o=1).broadcast_to([P, R, NT])
                    ch.link(V.tensor_reduce(lmx[:], logit[:], AX.X, ALU.max))
                    V.tensor_tensor(le[:], logit[:], bc(lmx[:], E), ALU.subtract).then_inc(m["rt_exp"], 1)
                    v.wait_ge(m["rt_exp"], 2)
                    ch.link(V.tensor_reduce(lsum[:], le[:], AX.X, ALU.add))
                    ch.link(V.reciprocal(lsum[:], lsum[:]))
                    ch.link(V.tensor_tensor(le[:], le[:], bc(lsum[:], E), ALU.mult))
                    ch.link(V.tensor_reduce(p1[:], le[:, :, 1:E], AX.X, ALU.max))
                    ch.link(V.tensor_tensor(eq[:], le[:, :, 1:E], bc(p1[:], R), ALU.is_equal))
                    ch.link(V.tensor_tensor(eq[:], eq[:], wgt[:].rearrange("p (o e) -> p o e", o=1).broadcast_to([P, NT, R]), ALU.mult))
                    ch.link(V.tensor_reduce(lmx[:], eq[:], AX.X, ALU.max))
                    V.tensor_tensor(oh[:].rearrange("p e t -> p t e"), eq[:], bc(lmx[:], R), ALU.is_equal).then_inc(m["rt_oh"], 1)
                    ch.link(V.tensor_tensor(lsum[:], le[:, :, 0], p1[:], ALU.add))
                    ch.link(V.tensor_scalar(lsum[:], lsum[:], 1e-9, None, ALU.max))
                    ch.link(V.reciprocal(lsum[:], lsum[:]))
                    V.tensor_tensor(gate0[:], le[:, :, 0], lsum[:], ALU.mult)
                    V.tensor_tensor(gate1[:], p1[:], lsum[:], ALU.mult)
                    v.wait_ge(m["rt_pre"], 1)
                    V.tensor_copy(pre, bank[3][:, 0:R * NT].rearrange("p (e t) -> p e t", e=R))
                    tot = bank[3][:, 256:256 + R * NT].rearrange("p (e t) -> p e t", e=R)
                    ch.link(V.tensor_copy(cum[0], tot))
                    a = 0
                    for sh in (1, 2, 4, 8, 16):
                        V.tensor_copy(cum[1 - a][:, :, 0:sh], cum[a][:, :, 0:sh])
                        ch.link(V.tensor_tensor(cum[1 - a][:, :, sh:], cum[a][:, :, sh:], cum[a][:, :, 0:NT - sh], ALU.add))
                        a = 1 - a
                    ch.link(V.tensor_tensor(cnt, cum[a][:, :, NT - 1:NT].broadcast_to([P, R, NT]),
                                            it128[:].rearrange("p (o t) -> p o t", o=1).broadcast_to([P, R, NT]), ALU.is_gt))
                    V.memset(st_e[:], 0.0)
                    ch.link(V.tensor_reduce(ntl[:], cnt, AX.X, ALU.add))
                    for e in range(R):
                        ch.link(V.tensor_tensor(st_e[:, e + 1:e + 2], st_e[:, e:e + 1], ntl[:, e:e + 1], ALU.add))
                    ch.link(V.tensor_tensor(cum[a], cum[a], tot, ALU.subtract))
                    ch.link(V.tensor_tensor(pre, pre, cum[a], ALU.add))
                    ch.link(V.scalar_tensor_tensor(out=pre, in0=be(st_e[:, 0:R]), scalar=float(P), in1=pre, op0=ALU.mult, op1=ALU.add))
                    ch.link(V.tensor_tensor(pre, pre, oh[:], ALU.mult))
                    ch.link(V.tensor_reduce(slotf[:], pre.rearrange("p e t -> p t e"), AX.X, ALU.add))
                    V.tensor_copy(slot[:], slotf[:])
                    ch.link(V.tensor_tensor(ge[:], gidx[:].rearrange("p (o g) -> p o g", o=1).broadcast_to([1, R - 1, NF + 2]),
                                            st_e[0:1, 1:R].rearrange("p (e o) -> p e o", o=1).broadcast_to([1, R - 1, NF + 2]), ALU.is_ge))
                    ch.link(V.tensor_reduce(rtf[:, 0, :], ge[:].rearrange("p e g -> p g e"), AX.X, ALU.add))
                    V.tensor_tensor(rtf[:, 0, :], rtf[:, 0, :], last[:], ALU.add)
                    ch.link(V.tensor_tensor(ge[:, 0:3, :], ge[:, 0:6:2, :], ge[:, 1:6:2, :], ALU.subtract))
                    ch.link(V.tensor_reduce(rtf[:, 1, :], ge[:, 0:3, :].rearrange("p e g -> p g e"), AX.X, ALU.add))
                    ch.link(V.tensor_tensor(rtf[:, 1, :], rtf[:, 1, :], last[:], ALU.add))
                    V.tensor_copy(end_tab[0:1, 0:R], st_e[0:1, 1:R + 1])
                    V.tensor_copy(rank_tab[:], rtf[:, 0, :])
                    V.tensor_copy(par_tab[:], rtf[:, 1, :]).then_inc(m["rt_done"], 1)

                    v.wait_ge(m["xt_dve"], NS)
                    for k in range(KD):
                        ins = V.tensor_reduce(pool_t[:, k, 0, :], xnt[:, k, W:W + S].rearrange("p (n c) -> p n c", n=NL), AX.X, ALU.add)
                    ch.link(ins)
                    ch.link(V.tensor_scalar(pool_t[:, :, 0, :], pool_t[:, :, 0, :], 1.0 / (S // NL), None, ALU.mult))
                    V.tensor_copy(pool_t[:, :, 1, :], pool_t[:, :, 0, :]).then_inc(m["pooled"], 1)
                    v.wait_ge(m["gk_ps"], 1)
                    V.tensor_tensor(gkbd[:], bank[4][:, 0:NL].rearrange("p (o n) -> p o n", o=1).broadcast_to([P, GH, NL]),
                                    hmask[:].rearrange("p (h o) -> p h o", o=1).broadcast_to([P, GH, NL]), ALU.mult)
                    pm = pmask[:].rearrange("p (a b o) -> p a b o", a=1, o=1)
                    gv4 = gvbd[:].rearrange("p (a b) v -> p a b v", b=2)
                    for b in range(2):
                        V.tensor_scalar(gv4[:, :, b, 0:HD], bank[4][:, 256:256 + P].rearrange("p (a b d) -> p a b d", b=2, d=HD)[:, :, b, :],
                                        pmask[:, b:b + 1], None, ALU.mult)
                    V.tensor_copy(gv4[:, :, :, HD:VW], pm.broadcast_to([P, 4, 2, 1])).then_inc(m["gk_done"], 1)
                    v.wait_ge(m["wprep"], 1)
                    v.wait_ge(m["w_in"], 16 * 11)
                    for g2 in range(2):
                        for j in range(2):
                            ins = V.tensor_scalar(gw[:, g2, H * j + GH * g2:H * j + GH * g2 + GH], hmask[:], gw_raw[:, g2, j:j + 1], None, ALU.mult)
                    ins.then_inc(m["gmats"], 1)
                    v.wait_ge(m["wqt_ps"], 1)
                    V.tensor_copy(xts[:, 0, :], bank[5][:]).then_inc(m["wqt_sb"], 1)
                    v.wait_ge(m["wg_ps"], 1)
                    gcols = lambda w_: w_[:, :, VC + D:VC + D + 2 * H]
                    wg_ps = bank[6][:, 0:KD * 2 * H].rearrange("p (k n) -> p k n", k=KD)
                    ch.link(V.tensor_copy(gcols(wh), wg_ps))
                    V.tensor_tensor(gcols(wl), wg_ps, gcols(wh).bitcast(F32), ALU.subtract).then_inc(m["wg_sb"], 1)

                    def take_piece(it, s_, p, src):
                        b = s_ % 2
                        v.wait_ge(m["proj_ps"], at(it, 2 * NPC, NPC * s_ + p + 1))
                        dst = kt[:, b, p, W:] if p < 2 else qt[:, b, (p - 2) // 2, (p - 2) % 2, :]
                        V.tensor_copy(dst, src[:]).then_inc(m["proj_d"], 1)

                    def gates(it, s_):
                        g_ = gsg[:, SUP * (s_ % 2):SUP * (s_ % 2) + SUP].rearrange("p t a h -> p (t a h)")
                        v.wait_ge(m["proj_a"], at(it, 2 * len(PA), len(PA) * (s_ + 1)))
                        V.tensor_scalar(g_, g_, 1.0, None, ALU.add).then_inc(m["gate_e"], 1)
                        v.wait_ge(m["gate_e"], at(it, 4, 2 * s_ + 1))
                        carry_v()
                        V.reciprocal(g_, g_).then_inc(m["gate_e"], 1)

                    for p in range(NPC):
                        if p not in PA:
                            take_piece(None, 0, p, bank[p])
                    gates(None, 0)

                    def step(it, k):
                        s_ = k // NU
                        if k < NT * UN:
                            t, u = unit(k)
                            h, nh = halves(k)
                            await_(v, m["p_exp"], it, 2 * NU, k - 1)
                            if it is not None:
                                carry_v()
                            for q in range(nh):
                                v.wait_ge(m["s_ps"], at(it, 8 * HV, h + q + 1))
                                if it is not None:
                                    carry_v()
                                if u < 0:
                                    src = bank[h % 3][:].rearrange("p (h n) -> p h n", h=GH)
                                    V.tensor_reduce(lmx8[:], src, AX.X, ALU.max).then_inc(m["mx_done"], 1)
                                    v.wait_ge(m["mx_done"], at(it, 8, t + 1))
                                    V.tensor_tensor(sub[k % 2].rearrange("p a b -> p (a b)")[:, 0:512].rearrange("p (h n) -> p h n", h=GH), src,
                                                    lmx8[:].rearrange("p (h o) -> p h o", o=1).broadcast_to([P, GH, NL]), ALU.subtract).then_inc(m["s_rd"], 1)
                                else:
                                    for o in range(2):
                                        c = 2 * q + o
                                        ins = V.tensor_tensor_reduce(sub[k % 2][:, c, :], bank[(h + q) % 3][:, KW * o:KW * o + KW],
                                                                     mask[:, 0 if (it is None and t == 0) else 1, o, :], -HD ** -0.5, 3.0e38,
                                                                     ALU.add, ALU.min, mx[k % 2][:, c:c + 1])
                                    ins.then_inc(m["s_rd"], 1)
                        n = k - LT
                        if 0 <= n < NT * UN and unit(n)[1] >= 0:
                            await_(v, m["pv"], it, 2 * NU, n - 1)
                            v.wait_ge(m["pt_ps"], at(it, 2 * NU, n + 1))
                            V.tensor_copy(pt2[n % 2][:], bank[5][:, 0:256]).then_inc(m["pt_d"], 1)
                        t = tail(k, 8)
                        if t is not None:
                            o3 = osb[:, 0:272].rearrange("p (h v) -> p h v", v=VW)
                            r3 = osb[:, 272:408].rearrange("p (h v) -> p h v", v=VW)
                            gl = gsg[:, t % (2 * SUP), 0, :]
                            v.wait_ge(m["o_a"], at(it, 8, t + 1))
                            V.reciprocal(rcp[:, 0:H], o3[:, :, HD])
                            V.reciprocal(rcp[:, H:H + GH], r3[:, :, HD]).then_inc(m["cmb"], 1)
                            v.wait_ge(m["cmb"], at(it, 8 * 3, 3 * t + 1))
                            V.tensor_tensor(remn[:], r3[:, :, 0:HD], rcp[:, H:H + GH].rearrange("p (h o) -> p h o", o=1).broadcast_to([P, GH, HD]), ALU.mult).then_inc(m["cmb1"], 1)
                            v.wait_ge(m["gate_e"], at(it, 4, 2 * (t // SUP) + 2))
                            V.tensor_tensor(rcp[:, 0:H], rcp[:, 0:H], gl, ALU.mult).then_inc(m["cmb"], 1)
                            v.wait_ge(m["cmb"], at(it, 8 * 3, 3 * t + 2))
                            V.tensor_tensor(loc[:], o3[:, :, 0:HD], rcp[:, 0:H].rearrange("p (h o) -> p h o", o=1).broadcast_to([P, H, HD]), ALU.mult)
                        t = tail(k, 10)
                        if t is not None:
                            v.wait_ge(m["rem_ps"], at(it, 8, t + 1))
                            V.tensor_tensor(mix[:], bank[7][:, 0:D].rearrange("p (h d) -> p h d", d=HD),
                                            gsg[:, t % (2 * SUP), 1, :].rearrange("p (h o) -> p h o", o=1).broadcast_to([P, H, HD]), ALU.mult).then_inc(m["cmb"], 1)
                            v.wait_ge(m["cmb"], at(it, 8 * 3, 3 * t + 3))
                            V.tensor_tensor(mix[:], mix[:], loc[:], ALU.add).then_inc(m["cmb2"], 1)
                        t = tail(k, 12)
                        if t is not None:
                            v.wait_ge(m["o_ps"], at(it, 8, t + 1))
                            at_ = acc[:, t, :] if it is None else acc[:, bass.ds(it * 8 + t, 1), :].rearrange("p o d -> p (o d)")
                            V.tensor_tensor(at_, bank[7][:, 0:D], at_, ALU.add).then_inc(m["o_d"], 1)
                        if s_ < NS - 1:
                            p = PIECE.get(k % NU)
                            if p is not None and p not in PA:
                                take_piece(it, s_ + 1, p, bank[3])
                            if k % NU == NU - 1:
                                gates(it, s_ + 1)

                    steps(v, step)

                @block.scalar
                def _(a):
                    A = nc.scalar
                    a.wait_ge(m["consts"], 1)
                    with a.Fori(0, NS // 2) as i:
                        for j in range(2):
                            a.wait_ge(m["rstd_d"], i * 2 + (j + 1))
                            A.activation(rstd[:], mv[:, :, 1], ACT.Sqrt, bias=eps_t[:]).then_inc(m["rstd_a"], 1)
                            a.wait_ge(m["xt_ps"], i * 2 + (j + 1))
                            if j:
                                a.wait_ge(m["lg_ps"], i * 2 + 1)
                            A.copy(xts[:, 0, :], bank[0][:])
                            A.copy(xts[:, 1, :], bank[1][:]).then_inc(m["xt_act"], 1)
                        a.wait_ge(m["lg_ps"], i * 2 + 2)
                    a.wait_ge(m["rt_exp"], 1)
                    A.activation(le[:], le[:], ACT.Exp).then_inc(m["rt_exp"], 1)
                    def take_piece(it, s_, p, src):
                        b = s_ % 2
                        a.wait_ge(m["proj_ps"], at(it, 2 * NPC, NPC * s_ + p + 1))
                        if p < 6:
                            A.copy(qt[:, b, (p - 2) // 2, (p - 2) % 2, :], src[:]).then_inc(m["proj_a"], 1)
                        elif p == 6:
                            A.copy(gqt[:, b, :], src[:]).then_inc(m["proj_a"], 1)
                        else:
                            n_ = SUP * b + p - 7
                            A.copy(v2[:, n_, :, 0:HD], src[:, 0:D].rearrange("p (h d) -> p h d", d=HD))
                            A.activation(gsg[:, n_].rearrange("p a h -> p (a h)"), src[:, D:D + 2 * H], ACT.Exp, scale=-1.0).then_inc(m["proj_a"], 1)

                    for p in PA:
                        take_piece(None, 0, p, bank[p % 8])

                    def step(it, k):
                        s_ = k // NU
                        n = k - LT
                        if 0 <= n < NT * UN:
                            await_(a, m["pv"], it, 2 * NU, n - 1)
                            a.wait_ge(m["pt_ps"], at(it, 2 * NU, n + 1))
                            A.copy(pt1[n % 2], bank[4][:]).then_inc(m["pt_a"], 1)
                        if k < NT * UN:
                            u = unit(k)[1]
                            h, nh = halves(k)
                            for q in range(nh):
                                a.wait_ge(m["s_rd"], at(it, 8 * HV, h + q + 1))
                                if u < 0:
                                    ins = A.activation(prob[k % 2].rearrange("p a b -> p (a b)")[:, 0:512], sub[k % 2].rearrange("p a b -> p (a b)")[:, 0:512],
                                                       ACT.Exp, scale=HD ** -0.5)
                                else:
                                    for c in (2 * q, 2 * q + 1):
                                        ins = A.activation(prob[k % 2][:, c, :], sub[k % 2][:, c, :], ACT.Exp, scale=-1.0, bias=mx[k % 2][:, c:c + 1])
                            ins.then_inc(m["p_exp"], 1)
                        t = tail(k, 9)
                        if t is not None:
                            a.wait_ge(m["xr_ps"], at(it, 8, t + 1))
                            A.copy(remt[:], bank[7][:, 0:P]).then_inc(m["xr_a"], 1)
                        t = tail(k, 11)
                        if t is not None:
                            a.wait_ge(m["yt_ps"], at(it, 8, t + 1))
                            A.copy(mixt[:].rearrange("p k t -> p (k t)"), bank[7][:, 0:D]).then_inc(m["yt_a"], 1)
                        if s_ < NS - 1 and PIECE.get(k % NU) in PA:
                            take_piece(it, s_ + 1, PIECE[k % NU], bank[3])
                        t = tail(k, 7)
                        if t is not None:
                            await_(a, m["cmb2"], it, 8, t)
                            a.wait_ge(m["pv"], at(it, 2 * NU, UN * t + UN))
                            A.copy(osb[:], bank[6][:, 0:408]).then_inc(m["o_a"], 1)

                    steps(a, step)

        ffn = ExitStack()
        with ffn:
            def sf(name, shape, dt=F32):
                return sb(name, shape, dt, ffn)

            st13 = sf("st13", [P, KD, 2, FF])
            st2 = sf("st2", [P, FT, D])
            w13h = sf("w13h", [P, 2, KD, 2, FF], F32R)
            w13l = sf("w13l", [P, 2, KD, 2, FF], F32R)
            w2h = sf("w2h", [P, 2, FT, D], F32R)
            w2l = sf("w2l", [P, 2, FT, D], F32R)
            xin = [sf(f"xin{j}", [P, D]) for j in range(2)]
            fxh = sf("fxh", [P, KD, P], F32R)
            fxl = sf("fxl", [P, KD, P], F32R)
            sl = sf("sl", [P, 2, 512])
            gtick = sf("gtick", [1, 1])
            gtick0 = sf("gtick0", [1, 1])
            hs = sf("hs", [P, FF])
            hth = sf("hth", [P, FF], F32R)
            htl = sf("htl", [P, FF], F32R)
            ysb = [sf(f"ysb{j}", [P, D]) for j in range(2)]
            gat = [sf(f"gat{j}", [P, D]) for j in range(4)]

            blk2 = nc.Block()
            with blk2 as block:
                @block.sync
                def _(sp):
                    def load(g, j, rows):
                        sp.dma_start(xin[j][:], rows).then_inc(xin_in[j], 16)

                    load(0, 0, xg_rows[0:P, :])
                    load(1, 1, xg_rows[P:2 * P, :])
                    with sp.Fori(0, NG // 2 - 1) as i:
                        for j in range(2):
                            sp.wait_ge(m["xt2_ps"], i * 2 + (j + 1))
                            load(None, j, xg_rows[bass.ds(i * (2 * P) + (2 + j) * P, P), :])
                            sp.wait_ge(m["y_sb"], i * 2 + (j + 1))
                            sp.dma_start(yg_rows[bass.ds(i * (2 * P) + j * P, P), :], ysb[j][:]).then_inc(y_out[j], 16)
                    for j in range(2):
                        sp.wait_ge(m["xt2_ps"], NG - 1 + j)
                        load(None, j, xn_rows[j * P:j * P + P, :])
                        sp.wait_ge(m["y_sb"], NG - 1 + j)
                        sp.dma_start(yg_rows[(NG - 2 + j) * P:(NG - 1 + j) * P, :], ysb[j][:]).then_inc(y_out[j], 16)
                    with sp.Fori(0, NT // 2 - 1) as i:
                        for j in range(2):
                            sp.wait_ge(m["xt2_ps"], i * 2 + (NG + j + 1))
                            load(None, j, xn_rows[bass.ds(i * (2 * P) + (2 + j) * P, P), :])
                            sp.wait_ge(m["y_sb"], i * 2 + (NG + j + 1))
                            sp.dma_start(out[bass.ds(i * (2 * P) + j * P, P), :], ysb[j][:]).then_inc(y_out[j], 16)
                    for j in range(2):
                        sp.wait_ge(m["y_sb"], NF - 1 + j)
                        sp.dma_start(out[(NT - 2 + j) * P:(NT - 1 + j) * P, :], ysb[j][:]).then_inc(y_out[j], 16)
                    for j in range(2):
                        sp.wait_ge(y_out[j], 16 * (NF // 2))

                @block.scalar
                def _(a):
                    A = nc.scalar
                    w1v = w1_t.rearrange("e (k p) f -> e p k f", p=P)
                    w3v = w3_t.rearrange("e (k p) f -> e p k f", p=P)
                    w2v = w2_t.rearrange("e (k p) n -> e p k n", p=P)

                    def x_hi(g):
                        a.wait_ge(m["xt2_ps"], g + 1)
                        A.copy(fxh[:].rearrange("p k t -> p (k t)"), bank[7][:, 0:D]).then_inc(m["xh2"], 1)

                    def body(g, nxt):
                        for q in range(2):
                            a.wait_ge(m["u_ps"], g * 2 + (q + 1))
                            A.activation(sl[:, q, :], bank[2 * q][:], ACT.Silu).then_inc(m["silu"], 1)
                        if nxt:
                            x_hi(g + 1)
                        a.wait_ge(m["ht_ps"], g + 1)
                        for q in range(2):
                            A.copy(hth[:, 512 * q:512 * q + 512], bank[4 + q][:]).then_inc(m["hh"], 1)

                    x_hi(0)
                    body(0, True)
                    with a.Fori(0, NF // 2 - 1) as i:
                        for j in range(2):
                            body(i * 2 + (1 + j), True)
                    body(NF - 1, False)

                @block.gpsimd
                def _(g):
                    G = nc.gpsimd
                    w1v = w1_t.rearrange("e (k p) f -> e p k f", p=P)
                    w3v = w3_t.rearrange("e (k p) f -> e p k f", p=P)
                    w2v = w2_t.rearrange("e (k p) n -> e p k n", p=P)
                    stores = [0]

                    def stage(e):
                        G.dma_start(st13[:, :, 0, :], w1v[e]).then_inc(m["stage"], 16)
                        G.dma_start(st13[:, :, 1, :], w3v[e]).then_inc(m["stage"], 16)
                        G.dma_start(st2[:], w2v[e]).then_inc(m["stage"], 16)

                    G.memset(gtick0[:], 0.0).then_inc(m["gt"], 1)
                    g.wait_ge(m["gt"], 1)
                    stage(0)
                    for e in range(E):
                        b = e % 2
                        if e >= 2:
                            g.wait_ge(m["y_ps"], g.value_load(end_tab[0:1, e - 2:e - 1], min_val=0, max_val=NG) + 1)
                            G.tensor_tensor(gtick[:], gtick0[:], gtick0[:], ALU.add)
                        g.wait_ge(m["stage"], 48 * (e + 1))
                        G.tensor_copy(w13h[:, b], st13[:]).then_inc(m["st_done"], 1)
                        G.tensor_copy(w2h[:, b], st2[:]).then_inc(m["st_done"], 1)
                        g.wait_ge(m["st_done"], 4 * e + 2)
                        G.tensor_tensor(w13l[:, b], st13[:], w13h[:, b].bitcast(F32), ALU.subtract).then_inc(m["st_done"], 1)
                        G.tensor_tensor(w2l[:, b], st2[:], w2h[:, b].bitcast(F32), ALU.subtract).then_inc(m["st_done"], 1)
                        g.wait_ge(m["st_done"], 4 * e + 4)
                        if e + 1 < E:
                            stage(e + 1)
                        G.memset(gat[0][0:1, 0:1], 0.0).then_inc(m["w_split"], 1)
                    for j in range(2):
                        g.wait_ge(y_out[j], 16 * (NG // 2))
                    g.wait_ge(m["w_split"], E)
                    for t in range(NT):
                        if t >= 4:
                            g.wait_ge(m["fin"], t - 3)
                        G.indirect_dma_start(gat[t % 4][:], None, yg_rows, bass.IndirectOffsetOnAxis(slot[:, t:t + 1], 0)).then_inc(gath[t % 4], 16)

                @block.tensor
                def _(pe):
                    T = nc.tensor

                    def x_turn(pair, j):
                        pe.wait_ge(xin_in[j], pair * 16 + 16)
                        for k in range(KD):
                            last_ = T.transpose(bank[7][:, P * k:P * k + P], xin[j][:, P * k:P * k + P], ident[:])
                        last_.then_inc(m["xt2_ps"], 1)

                    def up(g, first):
                        rank = pe.value_load(rank_tab[0:1, bass.ds(g, 1)], min_val=0, max_val=E - 1)
                        par = pe.value_load(par_tab[0:1, bass.ds(g, 1)], min_val=0, max_val=1)
                        pe.wait_ge(m["w_split"], rank + 1)
                        pe.wait_ge(m["xh2"], g + 1)
                        pe.wait_ge(m["xl2"], g + 1)
                        for q in range(2):
                            if not first:
                                pe.wait_ge(m["h_sb"], g * 2 + (q - 1))
                            cnt_ = [0, 0]
                            for k in range(KD):
                                for st_, wt in ((fxh, w13h), (fxh, w13l), (fxl, w13h)):
                                    for ab in range(2):
                                        cnt_[ab] += 1
                                        last_ = T.matmul(bank[2 * q + ab][:], st_[:, k, :],
                                                         wt[:, bass.ds(par, 1), k, ab, 512 * q:512 * q + 512].rearrange("p o f -> p (o f)"),
                                                         start=(cnt_[ab] == 1), stop=(cnt_[ab] == 3 * KD))
                            last_.then_inc(m["u_ps"], 1)

                    def h_turn(g):
                        pe.wait_ge(m["h_sb"], g * 2 + 2)
                        for c in range(FT):
                            last_ = T.transpose(bank[4 + c // 4][:, P * (c % 4):P * (c % 4) + P], hs[:, P * c:P * c + P], ident[:])
                        last_.then_inc(m["ht_ps"], 1)

                    def down(g, first):
                        par = pe.value_load(par_tab[0:1, bass.ds(g, 1)], min_val=0, max_val=1)
                        pe.wait_ge(m["hl"], g * 2 + 2)
                        if not first:
                            pe.wait_ge(m["y_sb"], g)
                        n = 0
                        for c in range(FT):
                            for st_, wt in ((hth, w2h), (hth, w2l), (htl, w2h)):
                                last_ = T.matmul(bank[6][:, 0:D], st_[:, P * c:P * c + P], wt[:, bass.ds(par, 1), c, :].rearrange("p o n -> p (o n)"),
                                                 start=(n == 0), stop=(n == 3 * FT - 1))
                                n += 1
                        last_.then_inc(m["y_ps"], 1)

                    pe.sem_inc(m["y_ps"], 1)
                    x_turn(0, 0)
                    up(0, True)
                    x_turn(0, 1)
                    h_turn(0)
                    up(1, False)
                    x_turn(1, 0)
                    down(0, True)
                    h_turn(1)
                    with pe.Fori(0, (NF - 4) // 2) as i:
                        for j in range(2):
                            g = i * 2 + (2 + j)
                            up(g, False)
                            x_turn(i + 1 + j, (j + 1) % 2)
                            down(g - 1, False)
                            h_turn(g)
                    up(NF - 2, False)
                    x_turn(NF // 2 - 1, 1)
                    down(NF - 3, False)
                    h_turn(NF - 2)
                    up(NF - 1, False)
                    down(NF - 2, False)
                    h_turn(NF - 1)
                    down(NF - 1, False)

                @block.vector
                def _(v):
                    V = nc.vector

                    def x_lo(g):
                        v.wait_ge(m["xh2"], g + 1)
                        V.tensor_tensor(fxl[:].rearrange("p k t -> p (k t)"), bank[7][:, 0:D], fxh[:].rearrange("p k t -> p (k t)").bitcast(F32), ALU.subtract).then_inc(m["xl2"], 1)

                    def front(g, nxt):
                        for q in range(2):
                            v.wait_ge(m["silu"], g * 2 + (q + 1))
                            V.tensor_tensor(hs[:, 512 * q:512 * q + 512], sl[:, q, :], bank[2 * q + 1][:], ALU.mult).then_inc(m["h_sb"], 1)
                        if nxt:
                            x_lo(g + 1)

                    def back(g):
                        for q in range(2):
                            v.wait_ge(m["hh"], g * 2 + (q + 1))
                            V.tensor_tensor(htl[:, 512 * q:512 * q + 512], bank[4 + q][:], hth[:, 512 * q:512 * q + 512].bitcast(F32), ALU.subtract).then_inc(m["hl"], 1)

                    def routed_out(g, j, pair, ring):
                        v.wait_ge(m["y_ps"], g + 2)
                        if ring:
                            v.wait_ge(y_out[j], pair * 16)
                        V.tensor_copy(ysb[j][:], bank[6][:, 0:D]).then_inc(m["y_sb"], 1)

                    def final_out(t, j, q, quad, half):
                        at_ = acc[:, bass.ds(t, 1), :].rearrange("p o d -> p (o d)")
                        v.wait_ge(gath[q], quad * 16 + 16)
                        V.scalar_tensor_tensor(out=at_, in0=gat[q][:], scalar=gate1[:, bass.ds(t, 1)], in1=at_, op0=ALU.mult, op1=ALU.add).then_inc(m["fin"], 1)
                        v.wait_ge(m["fin"], t + 1)
                        v.wait_ge(m["y_ps"], t + (NG + 2))
                        v.wait_ge(y_out[j], half * 16 + (NG // 2) * 16)
                        V.scalar_tensor_tensor(out=ysb[j][:], in0=bank[6][:, 0:D], scalar=gate0[:, bass.ds(t, 1)], in1=at_, op0=ALU.mult, op1=ALU.add).then_inc(m["y_sb"], 1)

                    x_lo(0)
                    front(0, True)
                    back(0)
                    for g in (1, 2):
                        front(g, True)
                        routed_out(g - 1, (g - 1) % 2, 0, False)
                        back(g)
                    with v.Fori(0, (NG - 2) // 2) as i:
                        for j in range(2):
                            g = i * 2 + (3 + j)
                            front(g, True)
                            routed_out(g - 1, j % 2, i + 1, True)
                            back(g)
                    with v.Fori(0, (NT - 4) // 4) as i:
                        for j in range(4):
                            t = i * 4 + j
                            front(t + (NG + 1), True)
                            final_out(t, j % 2, j, i, i * 2 + j // 2)
                            back(t + (NG + 1))
                    for t in range(NT - 4, NT - 1):
                        front(t + NG + 1, t + NG + 1 < NF - 1)
                        final_out(t, t % 2, t % 4, t // 4, t // 2)
                        back(t + NG + 1)
                    final_out(NT - 1, 1, 3, NT // 4 - 1, NT // 2 - 1)


def kernel(**inputs):
    import numpy as _np
    import concourse.bacc as _bacc
    from concourse import mybir as _mybir
    from concourse.bass_utils import run_bass_kernel_spmd as _run

    a = {k: _np.asarray(v) for k, v in inputs.items()}
    order = list(range(1, E)) + [0]
    feed = {
        "x": a["L0_attn_x"].reshape(S, D),
        "wq": a["L0_attn_wq"], "wk": a["L0_attn_wk"], "wv": a["L0_attn_wv"],
        "wgq": a["L0_attn_wgq"], "wgk": a["L0_attn_wgk"], "wgv": a["L0_attn_wgv"],
        "r_out": a["L0_attn_r_out_w"], "gate_l": a["L0_attn_gate_local_w"], "gate_r": a["L0_attn_gate_remote_w"],
        "w_out": a["L0_attn_w_out"], "wr_t": a["L0_ffn_Wr"].T,
        "w1_t": a["L0_ffn_W1"][order].transpose(0, 2, 1), "w3_t": a["L0_ffn_W3"][order].transpose(0, 2, 1),
        "w2_t": a["L0_ffn_W2"][order].transpose(0, 2, 1),
    }
    nc = _bacc.Bacc("TRN2", target_bir_lowering=False, num_devices=1)
    arrays, args = {}, []
    for name, v in feed.items():
        v = _np.ascontiguousarray(v)
        arrays[f"in_{name}"] = v
        args.append(nc.dram_tensor(f"in_{name}", v.shape, _mybir.dt.from_np(v.dtype), kind="ExternalInput").ap())
    args.append(nc.dram_tensor("out_y", (S, D), _mybir.dt.float32, kind="ExternalOutput").ap())
    moe_block(nc, *args)
    r = _run(nc, [arrays], core_ids=[0])
    return r.results[0]["out_y"].reshape(1, S, D)
```

```python
from contextlib import ExitStack

import concourse.bass as bass
from concourse import mybir

ALU = mybir.AluOpType
ACT = mybir.ActivationFunctionType
AX = mybir.AxisListType
F32 = mybir.dt.float32
F32R = mybir.dt.float32r
BF16 = mybir.dt.bfloat16
I32 = mybir.dt.int32

P = 128
D = 256
KD = D // P
S = 4096
NT = S // P
SUP = 4
NS = NT // SUP
SW = SUP * P
H, HD = 16, 16
VW = HD + 1
GH = 8
NL = 64
W = 64
KW = W + P
E = 8
R = E - 1
FF = 1024
FT = FF // P
NG = (S + R * (P - 1)) // P
NF = NG + NT
NEG = -1.0e30
EPS = 1e-5


def moe_block(nc, x, wq, wk, wv, wgq, wgk, wgv, r_out, gate_l, gate_r, w_out, wr_t, w1_t, w3_t, w2_t, out):
    xn_rows = nc.dram_tensor("xn_rows", (S, D), F32, kind="Internal").ap()
    xg_rows = nc.dram_tensor("xg_rows", (NG * P, D), F32, kind="Internal").ap()
    yg_rows = nc.dram_tensor("yg_rows", (NG * P, D), F32, kind="Internal").ap()

    by_rows = lambda w: w.rearrange("e (k p) f -> e p k f", p=P)

    with ExitStack() as ctx:
        def sb(name, shape, dt=F32, c=ctx):
            return c.enter_context(nc.sbuf_tensor(name, shape, dt))

        def sem(name):
            return ctx.enter_context(nc.semaphore(name))

        bank = [ctx.enter_context(nc.psum_tensor(f"bank{i}", [P, 512], F32)) for i in range(8)]

        acc = sb("acc", [P, NT, D])
        ident = sb("ident", [P, P])
        ident_b = sb("ident_b", [P, P], BF16)
        slot = sb("slot", [P, NT], I32)
        gate0 = sb("gate0", [P, NT])
        gate1 = sb("gate1", [P, NT])
        rank_tab = sb("rank_tab", [1, NF + 2], I32)
        end_tab = sb("end_tab", [1, 8], I32)

        w13n, w2n = KD * 2 * FF, FT * D
        wn = 2 * (w13n + w2n)
        NW = D + D + P + D + 2 * H
        with ExitStack() as over:
            o = lambda name, shape, dt=F32: sb(name, shape, dt, over)
            xnt = o("xnt", [P, KD, W + S + W])
            xn_t = [o(f"xn_t{j}", [P, SUP, D]) for j in range(2)]
            xh = o("xh", [P, KD, SW], F32R)
            xl = o("xl", [P, KD, SW], F32R)
            used = KD * (W + S + W) + 2 * SUP * D + 2 * KD * SW
            wh = o("wh", [P, KD, NW], F32R)
            wl = o("wl", [P, KD, NW], F32R)
            assert wn <= used and w13n <= 2 * KD * NW + 4 * SW
            qt = o("qt", [P, 2, 2, 2, SW])
            kt = o("kt", [P, 2, 2, W + SW])
            prob1 = o("prob1", [P, 4, KW])
            assert used + 2 * KD * NW + 8 * SW + 4 * (W + SW) + 4 * KW <= 2 * wn
        with ExitStack() as over:
            sb("above", [P, used], F32, over)
            first13 = sb("first13", [P, KD, 2, FF], F32, over)
        with ExitStack() as over:
            sb("above2", [P, used], F32, over)
            first2 = sb("first2", [P, FT, D], F32, over)
        weights = sb("weights", [P, 2, wn], F32R)
        part = lambda c, n: weights[:, :, c:c + n]
        w13h = part(0, w13n).rearrange("p b (k a f) -> p b k a f", k=KD, a=2)
        w13l = part(w13n, w13n).rearrange("p b (k a f) -> p b k a f", k=KD, a=2)
        w2h = part(2 * w13n, w2n).rearrange("p b (c n) -> p b c n", c=FT)
        w2l = part(2 * w13n + w2n, w2n).rearrange("p b (c n) -> p b c n", c=FT)
        xin = [sb(f"xin{j}", [P, D]) for j in range(2)]

        names = """consts early x_in w_in bn rcp_d rt_mm rt_link x_norm_t xn_out xt_ps xt_dve xt_act lg_ps lg_sb rstd_a rstd_d
            wprep pool_zero pooled zero_out rt_exp rt_oh rt_pre rt_done gk_ps gk_done gmats wqt_ps wqt_sb wg_ps wg_sb
            x_split proj_ps proj_a proj_d prev_k win_k win_v prev_v gate_e s_ps s_rd p_exp pt_ps pt_a pt_d pv o_a cmb cmb1 xr_ps xr_a rem_ps
            cmb2 yt_ps yt_a o_ps o_d mx_done
            stage0 stage st_done w_split xt2_ps xh2 xl2 u_ps silu h_sb ht_ps hh hl y_ps y_sb fin gt""".split()
        m = {n: sem("q_" + n) for n in names}
        x_in = [sem(f"q_x_in{j}") for j in range(2)]
        xn_out = [sem(f"q_xn_out{j}") for j in range(2)]
        tl_in = [sem(f"q_tl_in{j}") for j in range(4)]
        sc_out = [sem(f"q_sc_out{j}") for j in range(4)]
        xin_in = [sem(f"q_xin_in{j}") for j in range(2)]
        y_out = [sem(f"q_y_out{j}") for j in range(2)]
        gath = [sem(f"q_gath{j}") for j in range(4)]
        dch, ach, pch = sem("dve_chain"), sem("act_chain"), sem("pool_chain")

        class Chain:
            def __init__(self, eng, s):
                self.eng, self.s, self.n, self.base, self.per, self.it = eng, s, 0, 0, 0, None

            def link(self, ins):
                self.n += 1
                ins.then_inc(self.s, 1)
                v = self.base + self.n
                self.eng.wait_ge(self.s, v if self.it is None else self.it * self.per + v)

            def loop(self, it, per):
                self.it, self.per, self.base, self.n = it, per, self.base + self.n, 0

            def done(self, times):
                assert self.n == self.per, self.n
                self.base, self.n, self.it = self.base + times * self.per, 0, None

        att = ExitStack()
        with att:
            def sa(name, shape, dt=F32):
                return sb(name, shape, dt, att)

            xts0 = sa("xts0", [P, KD, SW])
            stat = sa("stat", [P, SUP, 6])
            mv = sa("mv", [P, SUP, 2])
            rstd = sa("rstd", [P, SUP])
            tick_v = sa("tick_v", [1, 29])
            tick_g = sa("tick_g", [1, 29])
            eps_t = sa("eps_t", [P, 1])
            wrt = sa("wrt", [P, KD, E])
            logit = sa("logit", [P, NT, E])
            QC, KC, GC, VC = 0, D, 2 * D, 2 * D + P
            wraw = sa("wraw", [P, KD, 3 * D + 3 * P])
            rw = sa("rw", [P, D])
            ow = sa("ow", [P, KD, D])
            gw_raw = sa("gw_raw", [P, 2, 2])
            gw = sa("gw", [P, 2, 2 * H])
            hmask = sa("hmask", [P, GH])
            qmask = sa("qmask", [P, 2])
            pmask = sa("pmask", [P, 2])
            mask = sa("mask", [P, 2, 2, KW])
            lmask = sa("lmask", [P, 2 * NL], BF16)
            pool_t = sa("pool_t", [P, KD, 2, NL])
            gkbd = sa("gkbd", [P, GH, NL])
            gvbd = sa("gvbd", [P, GH, VW])
            xts = [xts0[:], qt[:, 1, 0]]
            ka = sa("ka", [P, 2, 2, SUP, KW])
            gqt = sa("gqt", [P, 2, SW])
            v2 = sa("v2", [P, 2 * SUP, H, VW])
            vp = sa("vp", [P, 2 * SUP, H, VW])
            wqt = xts0[:, 0, :].rearrange("p (g d) -> p g d", g=2)
            mx = [sa(f"mx{j}", [P, 4]) for j in range(2)]
            lmx8 = sa("lmx8", [P, GH])
            units = wraw[:].rearrange("p k n -> p (k n)").rearrange("p (j c k) -> p j c k", j=3, c=4)
            sub = [units[:, j] for j in range(2)]
            prob = [units[:, 2], prob1[:]]
            pt1 = [xts0[:, j, :] for j in range(2)]
            pt2 = [sa(f"pt2_{j}", [P, 256]) for j in range(2)]
            osb = sa("osb", [P, 408])
            rcp = sa("rcp", [P, 24])
            gsg = sa("gsg", [P, 2 * SUP, 2, H])
            loc = sa("loc", [P, H, HD])
            remn = sa("remn", [P, GH, HD])
            remt = sa("remt", [P, P])
            mix = sa("mix", [P, H, HD])
            mixt = sa("mixt", [P, KD, P])
            zrow = sa("zrow", [P, D])
            u_tri = sa("u_tri", [P, P])
            ones = sa("ones", [P, P])
            it128 = sa("it128", [P, NT])
            wgt = sa("wgt", [P, R])
            gidx = sa("gidx", [1, NF + 2])
            last = sa("last", [1, NF + 2])
            lmx = sa("lmx", [P, NT])
            le = sa("le", [P, NT, E])
            lsum = sa("lsum", [P, NT])
            p1 = sa("p1", [P, NT])
            eq = sa("eq", [P, NT, R])
            oh = sa("oh", [P, R, NT])
            cum0, cum1, pre, cnt = [xn_t[1][:].rearrange("p t d -> p (t d)")[:, R * NT * j:R * NT * j + R * NT].rearrange("p (e t) -> p e t", e=R)
                                    for j in range(4)]
            cum = [cum0, cum1]
            ntl = sa("ntl", [P, R])
            st_e = sa("st_e", [P, R + 1])
            ge = sa("ge", [1, R - 1, NF + 2])
            rtf = sa("rtf", [1, NF + 2])
            slotf = sa("slotf", [P, NT])
            tl = [xn_t[0][:, j, :] for j in range(4)]

            UN = 5
            HV = 9
            NU = SUP * UN
            LT, LP = 2, 3
            LAST = (NT - 1) * UN + 12

            def unit(k):
                return k // UN, (0, -1, 1, 2, 3)[k % UN]

            def halves(k):
                return k // UN * HV + (0, 2, 3, 5, 7)[k % UN], (1 if k % UN == 1 else 2)

            def plain(k):
                return k - (k + UN - 2) // UN

            def tail(k, r):
                t = (k - r) // UN
                return t if k >= r and (k - r) % UN == 0 and t < NT else None

            PIECES = {(2 + 2 * p + k) % NU: (p, k) for p in range(9) for k in range(KD)}

            def piece(k):
                p, part = PIECES.get(k % NU, (None, None))
                s = k // NU + (0 if k % NU == 0 else 1)
                return (s, p, part) if p is not None and 0 < s < NS else (None, None, None)

            NPC, FV = 9, 5
            PA = (2, 4, 5, 6, 7, 8)
            pa_before = lambda p: sum(1 for q in PA if q < p)
            pd_before = lambda p: p - pa_before(p)

            def at(it, per, v):
                return v if it is None else it * per + v

            def await_(eng, s_, it, per, v):
                if it is not None or v > 0:
                    eng.wait_ge(s_, at(it, per, v))

            def supers(eng, part):
                for s in (0, 1):
                    part(None, s)
                with eng.Fori(0, (NS - 4) // 2) as it:
                    for s in (2, 3):
                        part(it, s)
                for s in (NS - 2, NS - 1):
                    part(None, s)

            def steps(eng, step):
                for k in range(NU):
                    step(None, k)
                with eng.Fori(0, (NS - 2) // 2) as it:
                    for k in range(NU, 3 * NU):
                        step(it, k)
                for k in range((NS - 1) * NU, LAST + 1):
                    step(None, k)

            carried = [0, 0]

            def carry_v():
                carried[0] += 1
                c = carried[0] % 29
                nc.vector.memset(tick_v[:, c:c + 1], 0.0)

            def carry_g():
                carried[1] += 1
                c = carried[1] % 29
                nc.gpsimd.tensor_tensor(tick_g[:, c:c + 1], zrow[0:1, 0:1], zrow[0:1, 0:1], ALU.add)

            xr = x.rearrange("(t p) d -> p t d", p=P)

            blk = nc.Block()
            with blk as block:
                @block.sync
                def _(sp):
                    for s in range(NS):
                        if s >= 2:
                            sp.wait_ge(x_in[s % 2], 16 * (s // 2))
                        sp.dma_start(acc[:, SUP * s:SUP * s + SUP, :], xr[:, SUP * s:SUP * s + SUP, :]).then_inc(x_in[s % 2], 16)
                        if s == 0:
                            sp.dma_start(wrt[:], wr_t.rearrange("(k p) e -> p k e", p=P)).then_inc(m["w_in"], 16)
                            for w_, c in ((wq, 0), (wk, D), (wv, 2 * D), (wgq, 3 * D), (wgk, 3 * D + P), (wgv, 3 * D + 2 * P)):
                                sp.dma_start(wraw[:, :, c:c + w_.shape[1]], w_.rearrange("(k p) n -> p k n", p=P)).then_inc(m["w_in"], 16)
                            sp.dma_start(rw[:], r_out).then_inc(m["w_in"], 16)
                            sp.dma_start(ow[:], w_out.rearrange("(k p) n -> p k n", p=P)).then_inc(m["w_in"], 16)
                            for j, g in enumerate((gate_l, gate_r)):
                                sp.dma_start(gw_raw[:, :, j:j + 1], g.rearrange("(g h) (d o) -> (h d) g o", g=2, o=1),
                                             allow_slow_non_contiguous=True).then_inc(m["w_in"], 16)
                    with sp.Fori(0, NS // 2) as i:
                        for j in range(2):
                            sp.wait_ge(m["x_norm_t"], i * 2 + (j + 1))
                            sp.dma_start(xn_rows[bass.ds(i * (2 * SW) + j * SW, SW), :].rearrange("(t p) d -> p t d", p=P),
                                         xn_t[j][:]).then_inc(xn_out[j], 16)
                    sp.wait_ge(m["pool_zero"], 1)
                    sp.dma_start(xg_rows.rearrange("(g p) d -> p g d", p=P),
                                 zrow[:].rearrange("p (o d) -> p o d", o=1).broadcast_to([P, NG, D])).then_inc(m["zero_out"], 16)
                    sp.wait_ge(m["xt_ps"], NS)
                    for j in range(2):
                        sp.wait_ge(xn_out[j], 16 * (NS // 2))
                    for t in range(NT):
                        if t >= 4:
                            sp.wait_ge(sc_out[t % 4], 16 * (t // 4))
                        sp.dma_start(tl[t % 4], xn_rows[t * P:t * P + P, :]).then_inc(tl_in[t % 4], 16)
                    for j in range(4):
                        sp.wait_ge(sc_out[j], 16 * (NT // 4))
                    for j in range(2):
                        sp.dma_start(xin[j][:], xg_rows[j * P:j * P + P, :]).then_inc(xin_in[j], 16)

                @block.gpsimd
                def _(g):
                    ch = Chain(g, pch)
                    G = nc.gpsimd
                    G.memset(eps_t[:], EPS)
                    G.memset(pmask[:], 1.0)
                    ch.link(G.memset(ident[:], 0.0))
                    G.affine_select(out=ident[:], in_=ident[:], compare_op=ALU.not_equal, fill=1.0, base=0,
                                    pattern=[[-1, P]], channel_multiplier=1)
                    ch.link(G.affine_select(out=pmask[:], in_=pmask[:], compare_op=ALU.is_ge, fill=0.0, base=0,
                                            pattern=[[-NL, 2]], channel_multiplier=1))
                    G.affine_select(out=pmask[:], in_=pmask[:], compare_op=ALU.is_ge, fill=0.0, base=NL - 1,
                                    pattern=[[NL, 2]], channel_multiplier=-1).then_inc(m["early"], 1)
                    G.memset(zrow[:], 0.0).then_inc(m["pool_zero"], 1)
                    g.wait_ge(m["early"], 1)
                    G.memset(ones[:], 1.0)
                    G.memset(v2[:].rearrange("p a h v -> p (a h v)"), 1.0)
                    G.memset(vp[:].rearrange("p a h v -> p (a h v)"), 0.0)
                    G.memset(kt[:, 0, :, 0:W], 0.0)
                    G.memset(xnt[:, :, 0:W], 0.0)
                    G.memset(xnt[:, :, W + S:], 0.0)
                    G.memset(hmask[:], 1.0)
                    G.memset(u_tri[:], 1.0)
                    G.memset(mask[:], 0.0)
                    ch.link(G.memset(lmask[:], 0.0))
                    G.affine_select(out=u_tri[:], in_=u_tri[:], compare_op=ALU.is_gt, fill=0.0, base=0,
                                    pattern=[[1, P]], channel_multiplier=-1)
                    ch.link(G.affine_select(out=hmask[:], in_=hmask[:], compare_op=ALU.is_ge, fill=0.0, base=0,
                                            pattern=[[-HD, GH]], channel_multiplier=1))
                    ch.link(G.affine_select(out=hmask[:], in_=hmask[:], compare_op=ALU.is_ge, fill=0.0, base=HD - 1,
                                            pattern=[[HD, GH]], channel_multiplier=-1))
                    late = mask[:, :, 1, :]
                    ch.link(G.affine_select(out=late, in_=late, compare_op=ALU.is_gt, fill=NEG, base=0,
                                            pattern=[[0, 2], [1, KW]], channel_multiplier=-1))
                    ch.link(G.affine_select(out=late, in_=late, compare_op=ALU.is_ge, fill=NEG, base=W,
                                            pattern=[[0, 2], [-1, KW]], channel_multiplier=1))
                    ch.link(G.affine_select(out=mask[:, 0, 1, :], in_=mask[:, 0, 1, :], compare_op=ALU.is_ge, fill=NEG, base=-W,
                                            pattern=[[1, KW]], channel_multiplier=0))
                    G.tensor_copy(mask[:, :, 0, 0:P], mask[:, :, 1, W:])
                    G.tensor_copy(mask[:, :, 0, P:], mask[:, :, 1, 0:W])
                    ch.link(G.affine_select(out=lmask[:], in_=lmask[:], compare_op=ALU.is_ge, fill=NEG, base=NL * (NL - 2),
                                            pattern=[[-NL, 2 * NL]], channel_multiplier=1))
                    G.tensor_copy(ident_b[:], ident[:])
                    G.tensor_copy(vp[:].rearrange("p a (g b) v -> p (a g) b v", b=2)[:, :, :, HD:VW],
                                  pmask[:].rearrange("p (a b o) -> p a b o", a=1, o=1).broadcast_to([P, SUP * H, 2, 1]))
                    G.iota(it128[:], pattern=[[P, NT]], base=0, channel_multiplier=0, allow_small_or_imprecise_dtypes=True)
                    G.iota(wgt[:], pattern=[[-1, R]], base=R, channel_multiplier=0, allow_small_or_imprecise_dtypes=True)
                    ch.link(G.iota(gidx[:], pattern=[[1, NF + 2]], base=0, channel_multiplier=0, allow_small_or_imprecise_dtypes=True))
                    G.tensor_scalar(last[:], gidx[:], float(NG), None, ALU.is_ge).then_inc(m["consts"], 1)
                    g.wait_ge(m["w_in"], 16 * 11)
                    g.wait_ge(m["consts"], 1)
                    for k in range(KD):
                        for c0, r0, n in ((QC, 0, D), (KC, D, D), (VC, 2 * D, D), (GC, 3 * D, P)):
                            ch.link(G.tensor_copy(wh[:, k, c0:c0 + n], wraw[:, k, r0:r0 + n]))
                            G.tensor_tensor(wl[:, k, c0:c0 + n], wraw[:, k, r0:r0 + n], wh[:, k, c0:c0 + n].bitcast(F32), ALU.subtract)
                    G.memset(gw[:], 0.0).then_inc(m["wprep"], 1)
                    def split(s_, it=None):
                        cols = xnt[:, :, bass.ds(at(it, 2 * SW, W + s_ * SW), SW)]
                        if it is not None or s_:
                            g.wait_ge(m["proj_ps"], at(it, 2 * NPC, NPC * s_))
                        carry_g()
                        G.tensor_copy(xh[:], cols).then_inc(m["x_split"], 1)
                        g.wait_ge(m["x_split"], at(it, 4, 2 * s_ + 1))
                        carry_g()
                        G.tensor_tensor(xl[:], cols, xh[:].bitcast(F32), ALU.subtract).then_inc(m["x_split"], 1)

                    def keys(s_, it=None):
                        b, nd = s_ % 2, NPC - len(PA)
                        g.wait_ge(m["proj_d"], at(it, 2 * nd, nd * s_ + 2))
                        carry_g()
                        G.tensor_copy(ka[:, b, :, :, 0:P], kt[:, b, :, W:].rearrange("p g (i k) -> p g i k", i=SUP))
                        if it is not None or s_:
                            ch_k = m["win_k"]
                            G.tensor_copy(kt[:, b, :, 0:W], kt[:, 1 - b, :, SW:]).then_inc(ch_k, 1)
                            g.wait_ge(ch_k, at(it, 2, s_))
                            carry_g()
                        G.tensor_copy(ka[:, b, :, :, P:], kt[:, b, :, 0:SW].rearrange("p g (i k) -> p g i k", i=SUP)[:, :, :, 0:W]).then_inc(m["prev_k"], 1)

                    def values(s_, it=None):
                        if s_ < NS - 1:
                            g.wait_ge(m["x_split"], at(it, 4, 2 * s_ + 4))
                        else:
                            g.wait_ge(m["prev_k"], s_ + 1)
                        for i in range(SUP):
                            g.wait_ge(m["proj_a"], at(it, 2 * len(PA), len(PA) * s_ + pa_before(FV + i) + 1))
                            carry_g()
                            n_ = (SUP * s_ + i) % (2 * SUP)
                            src = v2[W:P, n_].rearrange("p (g b) v -> p g b v", b=2)
                            to = vp[:, (n_ + 1) % (2 * SUP)].rearrange("p (g b) v -> p g b v", b=2)
                            G.tensor_copy(to[0:W, :, 0, 0:HD], src[:, :, 0, 0:HD]).then_inc(m["win_v"], 1)
                            g.wait_ge(m["win_v"], at(it, 2 * SUP, SUP * s_ + i + 1))
                            carry_g()
                            G.tensor_copy(to[W:P, :, 1, 0:HD], src[:, :, 1, 0:HD]).then_inc(m["prev_v"], 1)
                            g.wait_ge(m["prev_v"], at(it, 2 * SUP, SUP * s_ + i + 1))
                            carry_g()

                    g.wait_ge(m["xt_act"], 1)
                    split(0)
                    keys(0)
                    g.wait_ge(m["xt_act"], NS)
                    split(1)
                    values(0)
                    keys(1)
                    g.wait_ge(m["rt_done"], 1)
                    g.wait_ge(m["zero_out"], 16)
                    for t in range(NT):
                        g.wait_ge(tl_in[t % 4], 16 * (t // 4 + 1))
                        G.indirect_dma_start(xg_rows, bass.IndirectOffsetOnAxis(slot[:, t:t + 1], 0), tl[t % 4], None).then_inc(sc_out[t % 4], 16)
                    for j in range(4):
                        g.wait_ge(sc_out[j], 16 * (NT // 4))
                    with g.Fori(0, (NS - 2) // 2) as it:
                        for s_ in (1, 2):
                            split(s_ + 1, it)
                            values(s_, it)
                            keys(s_ + 1, it)
                    values(NS - 1)
                    g.wait_ge(m["proj_ps"], NPC * NS)
                    w1v, w3v, w2v = by_rows(w1_t), by_rows(w3_t), by_rows(w2_t)
                    for a_, w_ in enumerate((w1v, w3v)):
                        G.dma_start(first13[:, :, a_, :], w_[0]).then_inc(m["stage0"], 16)
                    g.wait_ge(m["stage0"], 32)
                    G.tensor_copy(w13h[:, 0], first13[:]).then_inc(m["st_done"], 1)
                    g.wait_ge(m["st_done"], 1)
                    G.tensor_tensor(w13l[:, 0], first13[:], w13h[:, 0].bitcast(F32), ALU.subtract).then_inc(m["st_done"], 1)
                    g.wait_ge(m["st_done"], 2)
                    G.dma_start(first2[:], w2v[0]).then_inc(m["stage0"], 16)
                    g.wait_ge(m["stage0"], 48)
                    G.tensor_copy(w2h[:, 0], first2[:]).then_inc(m["st_done"], 1)
                    g.wait_ge(m["st_done"], 3)
                    G.tensor_tensor(w2l[:, 0], first2[:], w2h[:, 0].bitcast(F32), ALU.subtract).then_inc(m["w_split"], 1)
                    g.wait_ge(m["w_split"], 1)

                @block.tensor
                def _(pe):
                    T = nc.tensor
                    pe.wait_ge(m["early"], 1)

                    def logits(it, s):
                        pe.wait_ge(m["xt_act"], at(it, 2, s + 1))
                        if it is None or s == 2:
                            await_(pe, m["lg_sb"], it, 2, s - 1)
                        for t in range(SUP):
                            for k in range(KD):
                                last_ = T.matmul(bank[2 + s % 2][:, E * t:E * t + E], xts[s % 2][:, k, P * t:P * t + P], wrt[:, k, :],
                                                 start=(k == 0), stop=(k == KD - 1))
                        last_.then_inc(m["lg_ps"], 1)

                    def turned(it, s):
                        pe.wait_ge(m["x_norm_t"], at(it, 2, s + 1))
                        await_(pe, m["xt_act"], it, 2, s - 1)
                        for k in range(KD):
                            for t in range(SUP):
                                last_ = T.transpose(bank[4 * (s % 2) + k][:, P * t:P * t + P], xn_t[s % 2][:, t, P * k:P * k + P], ident[:])
                        last_.then_inc(m["xt_ps"], 1)
                        if s == 0:
                            pe.wait_ge(m["w_in"], 16 * 11)
                        if it is not None or s:
                            logits(it, s - 1)
                        if it is not None and s == 3:
                            pe.wait_ge(m["lg_sb"], at(it, 2, 2))

                    supers(pe, turned)
                    logits(None, NS - 1)

                    def three(dst, stat_h, stat_l, mov_h, mov_l, ks):
                        for k in ks:
                            for n, (a, b) in enumerate(((stat_h, mov_h), (stat_h, mov_l), (stat_l, mov_h))):
                                last_ = T.matmul(dst, a(k), b(k), start=(k == 0 and n == 0), stop=(k == KD - 1 and n == 2))
                        return last_

                    def project(p, dst, ks=(0, 1)):
                        if p < FV:
                            c = KC + P * p if p < 2 else QC + P * (p - 2) if p < 4 else GC
                            return three(dst[:], lambda k: wh[:, k, c:c + P], lambda k: wl[:, k, c:c + P],
                                         lambda k: xh[:, k, :], lambda k: xl[:, k, :], ks)
                        c = P * (p - FV)
                        return three(dst[:, 0:D + 2 * H], lambda k: xh[:, k, c:c + P], lambda k: xl[:, k, c:c + P],
                                     lambda k: wh[:, k, VC:VC + D + 2 * H], lambda k: wl[:, k, VC:VC + D + 2 * H], ks)

                    pe.wait_ge(m["wprep"], 1)
                    pe.wait_ge(m["x_split"], 2)
                    pe.wait_ge(m["xt_act"], NS)
                    pe.wait_ge(m["lg_sb"], NS)
                    for p in range(NPC):
                        if p == 2:
                            pe.wait_ge(m["pooled"], 1)
                            for g2 in range(2):
                                for k in range(KD):
                                    last_ = T.transpose(bank[6][:, D * g2 + P * k:D * g2 + P * k + P], wraw[:, k, P * g2:P * g2 + P], ident[:])
                            last_.then_inc(m["wqt_ps"], 1)
                            for k in range(KD):
                                T.matmul(bank[7][:, 0:NL], wraw[:, k, 3 * D + P:3 * D + 2 * P], pool_t[:, k, 0, :], start=(k == 0), stop=(k == KD - 1))
                            for k in range(KD):
                                last_ = T.matmul(bank[7][:, 256:256 + P], pool_t[:, k, :, :].rearrange("p a n -> p (a n)"),
                                                 wraw[:, k, 3 * D + 2 * P:3 * D + 3 * P], start=(k == 0), stop=(k == KD - 1))
                            last_.then_inc(m["gk_ps"], 1)
                        if p == FV:
                            pe.wait_ge(m["wqt_sb"], 1)
                            pe.wait_ge(m["gmats"], 1)
                            for k in range(KD):
                                for g2 in range(2):
                                    last_ = T.matmul(bank[6][:, 2 * H * k:2 * H * k + 2 * H], wqt[:, g2, P * k:P * k + P], gw[:, g2, :], start=(g2 == 0), stop=(g2 == 1))
                            last_.then_inc(m["wg_ps"], 1)
                            pe.wait_ge(m["wg_sb"], 1)
                        if p >= 6:
                            if p - 6 in PA:
                                pe.wait_ge(m["proj_a"], pa_before(p - 6) + 1)
                            else:
                                pe.wait_ge(m["proj_d"], pd_before(p - 6) + 1)
                        project(p, bank[p % 6]).then_inc(m["proj_ps"], 1)
                    pe.wait_ge(m["gk_done"], 1)

                    def step(it, k):
                        s_ = k // NU
                        if k < NT * UN:
                            t, u = unit(k)
                            i, b = t % SUP, s_ % 2
                            if k % NU == 0:
                                pe.wait_ge(m["proj_a"], at(it, 2 * len(PA), len(PA) * s_ + (pa_before(FV) if k else len(PA))))
                                pe.wait_ge(m["proj_d"], at(it, 2 * (NPC - len(PA)), (NPC - len(PA)) * (s_ + 1)))
                                pe.wait_ge(m["prev_k"], at(it, 2, s_ + 1))
                            h, nh = halves(k)
                            for q in range(nh):
                                await_(pe, m["s_rd"], it, 8 * HV, h + q - 2)
                                dst = bank[(h + q) % 3]
                                if u < 0:
                                    lat = lmask[:, at(it, -2 * 2 * SUP, NL - 2 - 2 * t):][:, 0:NL] if it is None else \
                                        lmask[:, bass.ds(it * (-2 * 2 * SUP) + (NL - 2 - 2 * t), NL)]
                                    T.matmul(dst[:].rearrange("p (h n) -> p h n", h=GH), ident_b[:],
                                             lat.rearrange("p (o n) -> p o n", o=1).broadcast_to([P, GH, NL]), start=True, stop=False)
                                    T.matmul(dst[:], gqt[:, b, P * i:P * i + P], gkbd[:].rearrange("p h n -> p (h n)"),
                                             start=False, stop=True).then_inc(m["s_ps"], 1)
                                else:
                                    g2, j = u // 2, 2 * (u % 2) + q
                                    for o in range(2):
                                        keys = ka[32 * j:32 * j + 32, b, g2, i, :] if o == 0 else kt[32 * j:32 * j + 32, b, g2, P * i:P * i + KW]
                                        last_ = T.matmul(dst[:, KW * o:KW * o + KW], qt[32 * j:32 * j + 32, b, o, g2, P * i:P * i + P],
                                                         keys, start=True, stop=True)
                                    last_.then_inc(m["s_ps"], 1)
                        n = k - LT
                        if 0 <= n < NT * UN:
                            u = unit(n)[1]
                            pe.wait_ge(m["p_exp"], at(it, 2 * NU, n + 1))
                            await_(pe, m["pt_a"], it, 2 * NU, n)
                            if u < 0:
                                pl = prob[n % 2].rearrange("p a b -> p (a b)")
                                for c in range(4):
                                    last_ = T.transpose(bank[4][:, P * c:P * c + P], pl[:, P * c:P * c + P], ident[:])
                            else:
                                await_(pe, m["pt_d"], it, 8 * (UN - 1), plain(n))
                                pr = prob[n % 2].rearrange("p a b -> p (a b)")
                                for q in range(2):
                                    c0 = 2 * KW * q
                                    T.transpose(bank[4][:, 2 * P * q:2 * P * q + P], pr[:, c0:c0 + P], ident[:])
                                    T.transpose(bank[4][:, 2 * P * q + P:2 * P * q + 2 * P], pr[:, c0 + 2 * P:c0 + 3 * P], ident[:])
                                    last_ = T.transpose(bank[5][:, P * q:P * q + P], pr[:, c0 + P:c0 + 2 * P], ident[:])
                            last_.then_inc(m["pt_ps"], 1)
                        ps, p, part = piece(k)
                        if p is not None:
                            if part == 0:
                                if p == 0:
                                    pe.wait_ge(m["x_split"], at(it, 4, 2 * ps + 2))
                                s1, p1_ = (ps, p - 1) if p else (ps - 1, NPC - 1)
                                if p1_ in PA:
                                    pe.wait_ge(m["proj_a"], at(it, 2 * len(PA), len(PA) * s1 + pa_before(p1_) + 1))
                                else:
                                    pe.wait_ge(m["proj_d"], at(it, 2 * (NPC - len(PA)), (NPC - len(PA)) * s1 + pd_before(p1_) + 1))
                            last_ = project(p, bank[3], (part,))
                            if part == KD - 1:
                                last_.then_inc(m["proj_ps"], 1)
                        if k == 4:
                            pe.wait_ge(m["rt_oh"], 1)
                            T.matmul(bank[7][:, 0:R * NT], u_tri[:], oh[:].rearrange("p e t -> p (e t)"), start=True, stop=True)
                            T.matmul(bank[7][:, 256:256 + R * NT], ones[:], oh[:].rearrange("p e t -> p (e t)"), start=True, stop=True).then_inc(m["rt_pre"], 1)
                        t = tail(k, 9)
                        if t == 0 and it is None:
                            pe.wait_ge(m["rt_done"], 1)
                        if t is not None:
                            pe.wait_ge(m["cmb1"], at(it, 8, t + 1))
                            await_(pe, m["o_d"], it, 8, t)
                            T.transpose(bank[7][:, 0:P], remn[:].rearrange("p h d -> p (h d)"), ident[:]).then_inc(m["xr_ps"], 1)
                        t = tail(k, 10)
                        if t is not None:
                            pe.wait_ge(m["xr_a"], at(it, 8, t + 1))
                            T.matmul(bank[7][:, 0:D], remt[:], rw[:], start=True, stop=True).then_inc(m["rem_ps"], 1)
                        t = tail(k, 11)
                        if t is not None:
                            pe.wait_ge(m["cmb2"], at(it, 8, t + 1))
                            for kk in range(KD):
                                last_ = T.transpose(bank[7][:, P * kk:P * kk + P], mix[:].rearrange("p h d -> p (h d)")[:, P * kk:P * kk + P], ident[:])
                            last_.then_inc(m["yt_ps"], 1)
                        t = tail(k, 12)
                        if t is not None:
                            pe.wait_ge(m["yt_a"], at(it, 8, t + 1))
                            for kk in range(KD):
                                last_ = T.matmul(bank[7][:, 0:D], mixt[:, kk, :], ow[:, kk, :], start=(kk == 0), stop=(kk == KD - 1))
                            last_.then_inc(m["o_ps"], 1)
                        n = k - LP
                        if 0 <= n < NT * UN:
                            t, u = unit(n)
                            i = t % (2 * SUP)
                            pe.wait_ge(m["pt_a"], at(it, 2 * NU, n + 1))
                            if u < 0:
                                for c in range(4):
                                    last_ = T.matmul(bank[6][:, 272 + 34 * c:306 + 34 * c], pt1[n % 2][:, P * c:P * c + P],
                                                     gvbd[:, 2 * c:2 * c + 2, :].rearrange("p h v -> p (h v)"), start=True, stop=True)
                            else:
                                pe.wait_ge(m["pt_d"], at(it, 8 * (UN - 1), plain(n) + 1))
                                if u == 0:
                                    await_(pe, m["o_a"], it, 8, t)
                                    if t % SUP == 0:
                                        pe.wait_ge(m["proj_a"], at(it, 2 * len(PA), len(PA) * (s_ + 1)))
                                    await_(pe, m["prev_v"], it, 8, t)
                                for q in range(2):
                                    h = 8 * (u // 2) + 2 * (2 * (u % 2) + q)
                                    T.matmul(bank[6][:, VW * h:VW * h + 2 * VW], pt2[n % 2][:, P * q:P * q + P],
                                             vp[:, i, h:h + 2, :].rearrange("p h v -> p (h v)"), start=True, stop=False)
                                    for o in range(2):
                                        last_ = T.matmul(bank[6][:, VW * (h + o):VW * (h + o) + VW], pt1[n % 2][:, P * (2 * q + o):P * (2 * q + o) + P],
                                                         v2[:, i, h + o, :], start=False, stop=(o == 1))
                            last_.then_inc(m["pv"], 1)

                    steps(pe, step)
                    pe.wait_ge(m["o_d"], NT)

                @block.vector
                def _(v):
                    V = nc.vector
                    ch = Chain(v, dch)
                    row = lambda it, s, t: acc[:, SUP * s + t, :] if it is None else \
                        acc[:, bass.ds(it * (2 * SUP) + (SUP * s + t), 1), :].rearrange("p o d -> p (o d)")

                    def moments(it, s):
                        v.wait_ge(x_in[s % 2], at(it, 16, 16 * (s // 2) + 16))
                        for t in range(SUP):
                            ins = V.bn_stats(stat[:, t, :], row(it, s, t))
                        ins.then_inc(m["bn"], 1)
                        v.wait_ge(m["bn"], at(it, 2, s + 1))
                        carry_v()
                        for t in range(SUP):
                            ins = V.bn_aggr(mv[:, t, :], stat[:, t, :])
                        ins.then_inc(m["rstd_d"], 1)

                    def turned(it, s):
                        v.wait_ge(m["xt_act"], at(it, 2, s + 1))
                        if it is not None:
                            carry_v()
                        c = 2 * SUP * s
                        to = pool_t[:, :, 0, c:c + 2 * SUP] if it is None else pool_t[:, :, 0, bass.ds(it * (4 * SUP) + c, 2 * SUP)]
                        V.tensor_reduce(to, xts[s % 2].rearrange("p k (n c) -> p k n c", n=2 * SUP), AX.X, ALU.add).then_inc(m["xt_dve"], 1)

                    def logits(it, s):
                        v.wait_ge(m["lg_ps"], at(it, 2, s + 1))
                        to = logit[:, SUP * s:SUP * s + SUP, :] if it is None else logit[:, bass.ds(it * (2 * SUP) + SUP * s, SUP), :]
                        V.tensor_copy(to, bank[2 + s % 2][:, 0:SUP * E].rearrange("p (t e) -> p t e", e=E)).then_inc(m["lg_sb"], 1)

                    def normalize(it, s):
                        await_(v, xn_out[s % 2], it, 16, 16 * (s // 2))
                        if it is not None:
                            carry_v()
                        v.wait_ge(m["rstd_a"], at(it, 2, s + 1))
                        V.reciprocal(rstd[:], rstd[:]).then_inc(m["rcp_d"], 1)
                        v.wait_ge(m["rcp_d"], at(it, 2, s + 1))
                        for t in range(SUP):
                            ins = V.tensor_scalar(xn_t[s % 2][:, t, :], row(it, s, t), mv[:, t, 0:1], rstd[:, t:t + 1], ALU.subtract, ALU.mult)
                        ins.then_inc(m["x_norm_t"], 1)
                        if it is not None or s < NS - 1:
                            moments(it, s + 1)
                        if it is not None or s:
                            turned(it, s - 1)
                        if it is not None or s > 1:
                            logits(it, s - 2)

                    moments(None, 0)
                    supers(v, normalize)
                    turned(None, NS - 1)
                    for s in (NS - 2, NS - 1):
                        logits(None, s)

                    v.wait_ge(m["xt_dve"], NS)
                    for a_ in (1, 0):
                        ins = V.tensor_scalar(pool_t[:, :, a_, :], pool_t[:, :, 0, :], NL / S, None, ALU.mult)
                    ins.then_inc(m["pooled"], 1)
                    def take_piece(it, s_, p, src):
                        b = s_ % 2
                        v.wait_ge(m["proj_ps"], at(it, 2 * NPC, NPC * s_ + p + 1))
                        if p < 2:
                            ins = V.tensor_copy(kt[:, b, p, W:], src[:])
                        else:
                            for o in range(2):
                                ins = V.tensor_scalar(qt[:, b, o, p - 2, :], src[:], qmask[:, o:o + 1], None, ALU.mult)
                        ins.then_inc(m["proj_d"], 1)

                    def gates(it, s_):
                        g_ = gsg[:, SUP * (s_ % 2):SUP * (s_ % 2) + SUP].rearrange("p t a h -> p (t a h)")
                        v.wait_ge(m["proj_a"], at(it, 2 * len(PA), len(PA) * (s_ + 1)))
                        V.tensor_scalar(g_, g_, 1.0, None, ALU.add).then_inc(m["gate_e"], 1)
                        v.wait_ge(m["gate_e"], at(it, 4, 2 * s_ + 1))
                        carry_v()
                        V.reciprocal(g_, g_).then_inc(m["gate_e"], 1)

                    for p in (0, 1):
                        take_piece(None, 0, p, bank[p])
                    v.wait_ge(m["consts"], 1)
                    v.wait_ge(m["wprep"], 1)
                    v.wait_ge(m["w_in"], 16 * 11)
                    ch.link(V.tensor_reduce(qmask[:], hmask[:].rearrange("p (a o) -> p o a", o=2), AX.X, ALU.add))
                    for g2 in range(2):
                        for j in range(2):
                            ins = V.tensor_scalar(gw[:, g2, H * j + GH * g2:H * j + GH * g2 + GH], hmask[:], gw_raw[:, g2, j:j + 1], None, ALU.mult)
                    ins.then_inc(m["gmats"], 1)
                    v.wait_ge(m["gk_ps"], 1)
                    V.tensor_tensor(gkbd[:], bank[7][:, 0:NL].rearrange("p (o n) -> p o n", o=1).broadcast_to([P, GH, NL]),
                                    hmask[:].rearrange("p (h o) -> p h o", o=1).broadcast_to([P, GH, NL]), ALU.mult)
                    pm = pmask[:].rearrange("p (a b o) -> p a b o", a=1, o=1)
                    gv4 = gvbd[:].rearrange("p (a b) v -> p a b v", b=2)
                    for b in range(2):
                        V.tensor_scalar(gv4[:, :, b, 0:HD], bank[7][:, 256:256 + P].rearrange("p (a b d) -> p a b d", b=2, d=HD)[:, :, b, :],
                                        pmask[:, b:b + 1], None, ALU.mult)
                    V.tensor_copy(gv4[:, :, :, HD:VW], pm.broadcast_to([P, 4, 2, 1])).then_inc(m["gk_done"], 1)
                    take_piece(None, 0, 3, bank[3])
                    v.wait_ge(m["wg_ps"], 1)
                    gcols = lambda w_: w_[:, :, VC + D:VC + D + 2 * H]
                    wg_ps = bank[6][:, 0:KD * 2 * H].rearrange("p (k n) -> p k n", k=KD)
                    ch.link(V.tensor_copy(gcols(wh), wg_ps))
                    V.tensor_tensor(gcols(wl), wg_ps, gcols(wh).bitcast(F32), ALU.subtract).then_inc(m["wg_sb"], 1)
                    gates(None, 0)

                    bc = lambda a, n: a.rearrange("p (t o) -> p t o", o=1).broadcast_to([P, NT, n])
                    be = lambda a: a.rearrange("p (e o) -> p e o", o=1).broadcast_to([P, R, NT])
                    scan = [cum0, cum1]

                    def routing(k):
                        if k == 0:
                            ch.link(V.tensor_reduce(lmx[:], logit[:], AX.X, ALU.max))
                            V.tensor_tensor(le[:], logit[:], bc(lmx[:], E), ALU.subtract).then_inc(m["rt_exp"], 1)
                        elif k == 2:
                            v.wait_ge(m["rt_exp"], 2)
                            ch.link(V.tensor_reduce(lsum[:], le[:], AX.X, ALU.add))
                            ch.link(V.reciprocal(lsum[:], lsum[:]))
                            ch.link(V.tensor_tensor(le[:], le[:], bc(lsum[:], E), ALU.mult))
                            ch.link(V.tensor_reduce(p1[:], le[:, :, 1:E], AX.X, ALU.max))
                            ch.link(V.tensor_tensor(eq[:], le[:, :, 1:E], bc(p1[:], R), ALU.is_equal))
                            ch.link(V.tensor_tensor(eq[:], eq[:], wgt[:].rearrange("p (o e) -> p o e", o=1).broadcast_to([P, NT, R]), ALU.mult))
                        elif k == 3:
                            ch.link(V.tensor_reduce(lmx[:], eq[:], AX.X, ALU.max))
                            V.tensor_tensor(oh[:].rearrange("p e t -> p t e"), eq[:], bc(lmx[:], R), ALU.is_equal).then_inc(m["rt_oh"], 1)
                            ch.link(V.tensor_tensor(lsum[:], le[:, :, 0], p1[:], ALU.add))
                            ch.link(V.tensor_scalar(lsum[:], lsum[:], 1e-9, None, ALU.max))
                            ch.link(V.reciprocal(lsum[:], lsum[:]))
                            V.tensor_tensor(gate0[:], le[:, :, 0], lsum[:], ALU.mult)
                            V.tensor_tensor(gate1[:], p1[:], lsum[:], ALU.mult)
                        elif k == 5:
                            v.wait_ge(m["rt_pre"], 1)
                            v.wait_ge(xn_out[1], 16 * (NS // 2))
                            V.tensor_copy(pre, bank[7][:, 0:R * NT].rearrange("p (e t) -> p e t", e=R))
                            ch.link(V.tensor_copy(scan[0], bank[7][:, 256:256 + R * NT].rearrange("p (e t) -> p e t", e=R)))
                            for sh in (1, 2, 4):
                                V.tensor_copy(scan[1][:, :, 0:sh], scan[0][:, :, 0:sh])
                                ch.link(V.tensor_tensor(scan[1][:, :, sh:], scan[0][:, :, sh:], scan[0][:, :, 0:NT - sh], ALU.add))
                                scan.reverse()
                        elif k == 6:
                            for sh in (8, 16):
                                V.tensor_copy(scan[1][:, :, 0:sh], scan[0][:, :, 0:sh])
                                ch.link(V.tensor_tensor(scan[1][:, :, sh:], scan[0][:, :, sh:], scan[0][:, :, 0:NT - sh], ALU.add))
                                scan.reverse()
                            ch.link(V.tensor_tensor(cnt, scan[0][:, :, NT - 1:NT].broadcast_to([P, R, NT]),
                                                    it128[:].rearrange("p (o t) -> p o t", o=1).broadcast_to([P, R, NT]), ALU.is_gt))
                            V.memset(st_e[:], 0.0)
                            ch.link(V.tensor_reduce(ntl[:], cnt, AX.X, ALU.add))
                            ch.link(V.tensor_tensor(pre[:, :, 1:], pre[:, :, 1:], scan[0][:, :, 0:NT - 1], ALU.add))
                        elif k == 7:
                            for e in range(R):
                                ch.link(V.tensor_tensor(st_e[:, e + 1:e + 2], st_e[:, e:e + 1], ntl[:, e:e + 1], ALU.add))
                            ch.link(V.scalar_tensor_tensor(out=pre, in0=be(st_e[:, 0:R]), scalar=float(P), in1=pre, op0=ALU.mult, op1=ALU.add))
                            ch.link(V.tensor_tensor(pre, pre, oh[:], ALU.mult))
                            ch.link(V.tensor_reduce(slotf[:], pre.rearrange("p e t -> p t e"), AX.X, ALU.add))
                            V.tensor_copy(slot[:], slotf[:])
                        elif k == 8:
                            ch.link(V.tensor_tensor(ge[:], gidx[:].rearrange("p (o g) -> p o g", o=1).broadcast_to([1, R - 1, NF + 2]),
                                                    st_e[0:1, 1:R].rearrange("p (e o) -> p e o", o=1).broadcast_to([1, R - 1, NF + 2]), ALU.is_ge))
                            ch.link(V.tensor_reduce(rtf[:], ge[:].rearrange("p e g -> p g e"), AX.X, ALU.add))
                            ch.link(V.tensor_tensor(rtf[:], rtf[:], last[:], ALU.add))
                            V.tensor_copy(end_tab[0:1, 0:R], st_e[0:1, 1:R + 1])
                            V.tensor_copy(rank_tab[:], rtf[:]).then_inc(m["rt_done"], 1)

                    def step(it, k):
                        s_ = k // NU
                        if k < NT * UN:
                            t, u = unit(k)
                            h, nh = halves(k)
                            await_(v, m["p_exp"], it, 2 * NU, k - 1)
                            if it is not None:
                                carry_v()
                            for q in range(nh):
                                v.wait_ge(m["s_ps"], at(it, 8 * HV, h + q + 1))
                                if it is not None:
                                    carry_v()
                                if u < 0:
                                    src = bank[h % 3][:].rearrange("p (h n) -> p h n", h=GH)
                                    V.tensor_reduce(lmx8[:], src, AX.X, ALU.max).then_inc(m["mx_done"], 1)
                                    v.wait_ge(m["mx_done"], at(it, 8, t + 1))
                                    V.tensor_tensor(sub[k % 2].rearrange("p a b -> p (a b)")[:, 0:512].rearrange("p (h n) -> p h n", h=GH), src,
                                                    lmx8[:].rearrange("p (h o) -> p h o", o=1).broadcast_to([P, GH, NL]), ALU.subtract).then_inc(m["s_rd"], 1)
                                else:
                                    for o in range(2):
                                        c = 2 * q + o
                                        ins = V.tensor_tensor_reduce(sub[k % 2][:, c, :], bank[(h + q) % 3][:, KW * o:KW * o + KW],
                                                                     mask[:, 0 if (it is None and t == 0) else 1, o, :], -HD ** -0.5, 3.0e38,
                                                                     ALU.add, ALU.min, mx[k % 2][:, c:c + 1])
                                    ins.then_inc(m["s_rd"], 1)
                        n = k - LT
                        if 0 <= n < NT * UN and unit(n)[1] >= 0:
                            await_(v, m["pv"], it, 2 * NU, n - 1)
                            v.wait_ge(m["pt_ps"], at(it, 2 * NU, n + 1))
                            V.tensor_copy(pt2[n % 2][:], bank[5][:, 0:256]).then_inc(m["pt_d"], 1)
                        if it is None:
                            routing(k)
                        t = tail(k, 8)
                        if t is not None:
                            o3 = osb[:, 0:272].rearrange("p (h v) -> p h v", v=VW)
                            r3 = osb[:, 272:408].rearrange("p (h v) -> p h v", v=VW)
                            gl = gsg[:, t % (2 * SUP), 0, :]
                            v.wait_ge(m["o_a"], at(it, 8, t + 1))
                            V.reciprocal(rcp[:, 0:H], o3[:, :, HD])
                            V.reciprocal(rcp[:, H:H + GH], r3[:, :, HD]).then_inc(m["cmb"], 1)
                            v.wait_ge(m["cmb"], at(it, 8 * 3, 3 * t + 1))
                            V.tensor_tensor(remn[:], r3[:, :, 0:HD], rcp[:, H:H + GH].rearrange("p (h o) -> p h o", o=1).broadcast_to([P, GH, HD]), ALU.mult).then_inc(m["cmb1"], 1)
                            v.wait_ge(m["gate_e"], at(it, 4, 2 * (t // SUP) + 2))
                            V.tensor_tensor(rcp[:, 0:H], rcp[:, 0:H], gl, ALU.mult).then_inc(m["cmb"], 1)
                            v.wait_ge(m["cmb"], at(it, 8 * 3, 3 * t + 2))
                            V.tensor_tensor(loc[:], o3[:, :, 0:HD], rcp[:, 0:H].rearrange("p (h o) -> p h o", o=1).broadcast_to([P, H, HD]), ALU.mult)
                        t = tail(k, 10)
                        if t is not None:
                            v.wait_ge(m["rem_ps"], at(it, 8, t + 1))
                            V.tensor_tensor(mix[:], bank[7][:, 0:D].rearrange("p (h d) -> p h d", d=HD),
                                            gsg[:, t % (2 * SUP), 1, :].rearrange("p (h o) -> p h o", o=1).broadcast_to([P, H, HD]), ALU.mult).then_inc(m["cmb"], 1)
                            v.wait_ge(m["cmb"], at(it, 8 * 3, 3 * t + 3))
                            V.tensor_tensor(mix[:], mix[:], loc[:], ALU.add).then_inc(m["cmb2"], 1)
                        t = tail(k, 12)
                        if t is not None:
                            v.wait_ge(m["o_ps"], at(it, 8, t + 1))
                            at_ = acc[:, t, :] if it is None else acc[:, bass.ds(it * 8 + t, 1), :].rearrange("p o d -> p (o d)")
                            V.tensor_tensor(at_, bank[7][:, 0:D], at_, ALU.add).then_inc(m["o_d"], 1)
                        ps, p, part = piece(k)
                        if p is not None and p not in PA and part == KD - 1:
                            take_piece(it, ps, p, bank[3])
                        if k % NU == 1 and 0 < s_ < NS:
                            gates(it, s_)

                    steps(v, step)

                @block.scalar
                def _(a):
                    A = nc.scalar
                    a.wait_ge(m["early"], 1)

                    def root(it, s):
                        a.wait_ge(m["rstd_d"], at(it, 2, s + 1))
                        A.activation(rstd[:], mv[:, :, 1], ACT.Sqrt, bias=eps_t[:]).then_inc(m["rstd_a"], 1)

                    def turned(it, s):
                        if it is not None or s < NS - 1:
                            root(it, s + 1)
                        await_(a, m["lg_ps"], it, 2, s - 1)
                        await_(a, m["xt_dve"], it, 2, s - 1)
                        a.wait_ge(m["xt_ps"], at(it, 2, s + 1))
                        A.copy(xts[s % 2][:, 0, :], bank[4 * (s % 2)][:])
                        A.copy(xts[s % 2][:, 1, :], bank[4 * (s % 2) + 1][:])
                        for k in range(KD):
                            to = xnt[:, k, W + SW * s:W + SW * s + SW] if it is None else xnt[:, k, bass.ds(it * (2 * SW) + (W + SW * s), SW)]
                            ins = A.copy(to, bank[4 * (s % 2) + k][:])
                        ins.then_inc(m["xt_act"], 1)

                    root(None, 0)
                    supers(a, turned)
                    a.wait_ge(m["wqt_ps"], 1)
                    a.wait_ge(m["lg_ps"], NS)
                    A.copy(xts0[:, 0, :], bank[6][:]).then_inc(m["wqt_sb"], 1)

                    def take_piece(it, s_, p, src):
                        b = s_ % 2
                        a.wait_ge(m["proj_ps"], at(it, 2 * NPC, NPC * s_ + p + 1))
                        if p < 4:
                            for o in range(2):
                                ins = A.activation(qt[:, b, o, p - 2, :], src[:], ACT.Copy, scale=qmask[:, o:o + 1])
                            ins.then_inc(m["proj_a"], 1)
                        elif p < FV:
                            A.copy(gqt[:, b, :], src[:]).then_inc(m["proj_a"], 1)
                        else:
                            n_ = SUP * b + p - FV
                            A.copy(v2[:, n_, :, 0:HD], src[:, 0:D].rearrange("p (h d) -> p h d", d=HD))
                            A.activation(gsg[:, n_].rearrange("p a h -> p (a h)"), src[:, D:D + 2 * H], ACT.Exp, scale=-1.0).then_inc(m["proj_a"], 1)

                    a.wait_ge(m["gmats"], 1)
                    for p in PA:
                        take_piece(None, 0, p, bank[p % 6])

                    def step(it, k):
                        s_ = k // NU
                        n = k - LT
                        if 0 <= n < NT * UN:
                            await_(a, m["pv"], it, 2 * NU, n - 1)
                            a.wait_ge(m["pt_ps"], at(it, 2 * NU, n + 1))
                            A.copy(pt1[n % 2], bank[4][:]).then_inc(m["pt_a"], 1)
                        if k < NT * UN:
                            u = unit(k)[1]
                            h, nh = halves(k)
                            for q in range(nh):
                                a.wait_ge(m["s_rd"], at(it, 8 * HV, h + q + 1))
                                if u < 0:
                                    ins = A.activation(prob[k % 2].rearrange("p a b -> p (a b)")[:, 0:512], sub[k % 2].rearrange("p a b -> p (a b)")[:, 0:512],
                                                       ACT.Exp, scale=HD ** -0.5)
                                else:
                                    for c in (2 * q, 2 * q + 1):
                                        ins = A.activation(prob[k % 2][:, c, :], sub[k % 2][:, c, :], ACT.Exp, scale=-1.0, bias=mx[k % 2][:, c:c + 1])
                            ins.then_inc(m["p_exp"], 1)
                        if it is None and k == 1:
                            a.wait_ge(m["rt_exp"], 1)
                            A.activation(le[:], le[:], ACT.Exp).then_inc(m["rt_exp"], 1)
                        t = tail(k, 9)
                        if t is not None:
                            a.wait_ge(m["xr_ps"], at(it, 8, t + 1))
                            A.copy(remt[:], bank[7][:, 0:P]).then_inc(m["xr_a"], 1)
                        t = tail(k, 11)
                        if t is not None:
                            a.wait_ge(m["yt_ps"], at(it, 8, t + 1))
                            A.copy(mixt[:].rearrange("p k t -> p (k t)"), bank[7][:, 0:D]).then_inc(m["yt_a"], 1)
                        ps, p, part = piece(k)
                        if p in PA and part == KD - 1:
                            take_piece(it, ps, p, bank[3])
                        t = tail(k, 7)
                        if t is not None:
                            await_(a, m["cmb2"], it, 8, t)
                            a.wait_ge(m["pv"], at(it, 2 * NU, UN * t + UN))
                            A.copy(osb[:], bank[6][:, 0:408]).then_inc(m["o_a"], 1)

                    steps(a, step)

        ffn = ExitStack()
        with ffn:
            def sf(name, shape, dt=F32):
                return sb(name, shape, dt, ffn)

            st13 = sf("st13", [P, KD, 2, FF])
            st2 = sf("st2", [P, FT, D])
            fxh = sf("fxh", [P, KD, P], F32R)
            fxl = sf("fxl", [P, KD, P], F32R)
            sl = sf("sl", [P, 2, 512])
            gtick = sf("gtick", [1, 1])
            gtick0 = sf("gtick0", [1, 1])
            hs = sf("hs", [P, FF])
            hth = sf("hth", [P, FF], F32R)
            htl = sf("htl", [P, FF], F32R)
            ysb = [sf(f"ysb{j}", [P, D]) for j in range(2)]
            gat = [sf(f"gat{j}", [P, D]) for j in range(4)]

            blk2 = nc.Block()
            with blk2 as block:
                @block.sync
                def _(sp):
                    def load(g, j, rows):
                        sp.dma_start(xin[j][:], rows).then_inc(xin_in[j], 16)

                    with sp.Fori(0, NG // 2 - 1) as i:
                        for j in range(2):
                            sp.wait_ge(m["xt2_ps"], i * 2 + (j + 1))
                            load(None, j, xg_rows[bass.ds(i * (2 * P) + (2 + j) * P, P), :])
                            sp.wait_ge(m["y_sb"], i * 2 + (j + 1))
                            sp.dma_start(yg_rows[bass.ds(i * (2 * P) + j * P, P), :], ysb[j][:]).then_inc(y_out[j], 16)
                    for j in range(2):
                        sp.wait_ge(m["xt2_ps"], NG - 1 + j)
                        load(None, j, xn_rows[j * P:j * P + P, :])
                        sp.wait_ge(m["y_sb"], NG - 1 + j)
                        sp.dma_start(yg_rows[(NG - 2 + j) * P:(NG - 1 + j) * P, :], ysb[j][:]).then_inc(y_out[j], 16)
                    with sp.Fori(0, NT // 2 - 1) as i:
                        for j in range(2):
                            sp.wait_ge(m["xt2_ps"], i * 2 + (NG + j + 1))
                            load(None, j, xn_rows[bass.ds(i * (2 * P) + (2 + j) * P, P), :])
                            sp.wait_ge(m["y_sb"], i * 2 + (NG + j + 1))
                            sp.dma_start(out[bass.ds(i * (2 * P) + j * P, P), :], ysb[j][:]).then_inc(y_out[j], 16)
                    for j in range(2):
                        sp.wait_ge(m["y_sb"], NF - 1 + j)
                        sp.dma_start(out[(NT - 2 + j) * P:(NT - 1 + j) * P, :], ysb[j][:]).then_inc(y_out[j], 16)
                    for j in range(2):
                        sp.wait_ge(y_out[j], 16 * (NF // 2))

                @block.scalar
                def _(a):
                    A = nc.scalar

                    def x_hi(g):
                        a.wait_ge(m["xt2_ps"], g + 1)
                        A.copy(fxh[:].rearrange("p k t -> p (k t)"), bank[7][:, 0:D]).then_inc(m["xh2"], 1)

                    def body(g, nxt):
                        for q in range(2):
                            a.wait_ge(m["u_ps"], g * 2 + (q + 1))
                            A.activation(sl[:, q, :], bank[2 * q][:], ACT.Silu).then_inc(m["silu"], 1)
                        if nxt:
                            x_hi(g + 1)
                        a.wait_ge(m["ht_ps"], g + 1)
                        for q in range(2):
                            A.copy(hth[:, 512 * q:512 * q + 512], bank[4 + q][:]).then_inc(m["hh"], 1)

                    x_hi(0)
                    body(0, True)
                    with a.Fori(0, NF // 2 - 1) as i:
                        for j in range(2):
                            body(i * 2 + (1 + j), True)
                    body(NF - 1, False)

                @block.gpsimd
                def _(g):
                    G = nc.gpsimd
                    w1v, w3v, w2v = by_rows(w1_t), by_rows(w3_t), by_rows(w2_t)

                    def stage(e):
                        G.dma_start(st13[:, :, 0, :], w1v[e]).then_inc(m["stage"], 16)
                        G.dma_start(st13[:, :, 1, :], w3v[e]).then_inc(m["stage"], 16)
                        G.dma_start(st2[:], w2v[e]).then_inc(m["stage"], 16)

                    G.memset(gtick0[:], 0.0).then_inc(m["gt"], 1)
                    g.wait_ge(m["gt"], 1)
                    stage(1)
                    for e in range(1, E):
                        b = e % 2
                        if e >= 2:
                            g.wait_ge(m["y_ps"], g.value_load(end_tab[0:1, e - 2:e - 1], min_val=0, max_val=NG) + 1)
                            G.tensor_tensor(gtick[:], gtick0[:], gtick0[:], ALU.add)
                        g.wait_ge(m["stage"], 48 * e)
                        G.tensor_copy(w13h[:, b], st13[:]).then_inc(m["st_done"], 1)
                        G.tensor_copy(w2h[:, b], st2[:]).then_inc(m["st_done"], 1)
                        g.wait_ge(m["st_done"], 4 * e + 1)
                        G.tensor_tensor(w13l[:, b], st13[:], w13h[:, b].bitcast(F32), ALU.subtract).then_inc(m["st_done"], 1)
                        G.tensor_tensor(w2l[:, b], st2[:], w2h[:, b].bitcast(F32), ALU.subtract).then_inc(m["st_done"], 1)
                        g.wait_ge(m["st_done"], 4 * e + 3)
                        if e + 1 < E:
                            stage(e + 1)
                        G.memset(gat[0][0:1, 0:1], 0.0).then_inc(m["w_split"], 1)
                    for j in range(2):
                        g.wait_ge(y_out[j], 16 * (NG // 2))
                    g.wait_ge(m["w_split"], E)
                    for t in range(NT):
                        if t >= 4:
                            g.wait_ge(m["fin"], t - 3)
                        G.indirect_dma_start(gat[t % 4][:], None, yg_rows, bass.IndirectOffsetOnAxis(slot[:, t:t + 1], 0)).then_inc(gath[t % 4], 16)

                @block.tensor
                def _(pe):
                    T = nc.tensor

                    def x_turn(pair, j):
                        pe.wait_ge(xin_in[j], pair * 16 + 16)
                        for k in range(KD):
                            last_ = T.transpose(bank[7][:, P * k:P * k + P], xin[j][:, P * k:P * k + P], ident[:])
                        last_.then_inc(m["xt2_ps"], 1)

                    def expert(g):
                        return pe.value_load(rank_tab[0:1, bass.ds(g, 1)], min_val=0, max_val=E - 1)

                    def up(g, first):
                        rank = expert(g)
                        par = rank % 2
                        pe.wait_ge(m["w_split"], rank + 1)
                        pe.wait_ge(m["xh2"], g + 1)
                        pe.wait_ge(m["xl2"], g + 1)
                        for q in range(2):
                            if not first:
                                pe.wait_ge(m["h_sb"], g * 2 + (q - 1))
                            cnt_ = [0, 0]
                            for k in range(KD):
                                for st_, wt in ((fxh, w13h), (fxh, w13l), (fxl, w13h)):
                                    for ab in range(2):
                                        cnt_[ab] += 1
                                        last_ = T.matmul(bank[2 * q + ab][:], st_[:, k, :],
                                                         wt[:, bass.ds(par, 1), k, ab, 512 * q:512 * q + 512].rearrange("p o f -> p (o f)"),
                                                         start=(cnt_[ab] == 1), stop=(cnt_[ab] == 3 * KD))
                            last_.then_inc(m["u_ps"], 1)

                    def h_turn(g):
                        pe.wait_ge(m["h_sb"], g * 2 + 2)
                        for c in range(FT):
                            last_ = T.transpose(bank[4 + c // 4][:, P * (c % 4):P * (c % 4) + P], hs[:, P * c:P * c + P], ident[:])
                        last_.then_inc(m["ht_ps"], 1)

                    def down(g, first):
                        par = expert(g) % 2
                        pe.wait_ge(m["hl"], g * 2 + 2)
                        if not first:
                            pe.wait_ge(m["y_sb"], g)
                        n = 0
                        for c in range(FT):
                            for st_, wt in ((hth, w2h), (hth, w2l), (htl, w2h)):
                                last_ = T.matmul(bank[6][:, 0:D], st_[:, P * c:P * c + P], wt[:, bass.ds(par, 1), c, :].rearrange("p o n -> p (o n)"),
                                                 start=(n == 0), stop=(n == 3 * FT - 1))
                                n += 1
                        last_.then_inc(m["y_ps"], 1)

                    pe.sem_inc(m["y_ps"], 1)
                    x_turn(0, 0)
                    up(0, True)
                    x_turn(0, 1)
                    h_turn(0)

                    def tile(g, nxt, first=False):
                        up(g, False)
                        if nxt:
                            x_turn(*nxt)
                        down(g - 1, first)
                        h_turn(g)

                    tile(1, (1, 0), True)
                    with pe.Fori(0, (NF - 4) // 2) as i:
                        for j in range(2):
                            tile(i * 2 + (2 + j), (i + 1 + j, (j + 1) % 2))
                    tile(NF - 2, (NF // 2 - 1, 1))
                    tile(NF - 1, None)
                    down(NF - 1, False)

                @block.vector
                def _(v):
                    V = nc.vector

                    def x_lo(g):
                        v.wait_ge(m["xh2"], g + 1)
                        V.tensor_tensor(fxl[:].rearrange("p k t -> p (k t)"), bank[7][:, 0:D], fxh[:].rearrange("p k t -> p (k t)").bitcast(F32), ALU.subtract).then_inc(m["xl2"], 1)

                    def front(g, nxt):
                        for q in range(2):
                            v.wait_ge(m["silu"], g * 2 + (q + 1))
                            V.tensor_tensor(hs[:, 512 * q:512 * q + 512], sl[:, q, :], bank[2 * q + 1][:], ALU.mult).then_inc(m["h_sb"], 1)
                        if nxt:
                            x_lo(g + 1)

                    def back(g):
                        for q in range(2):
                            v.wait_ge(m["hh"], g * 2 + (q + 1))
                            V.tensor_tensor(htl[:, 512 * q:512 * q + 512], bank[4 + q][:], hth[:, 512 * q:512 * q + 512].bitcast(F32), ALU.subtract).then_inc(m["hl"], 1)

                    def routed_out(g, j, pair, ring):
                        v.wait_ge(m["y_ps"], g + 2)
                        if ring:
                            v.wait_ge(y_out[j], pair * 16)
                        V.tensor_copy(ysb[j][:], bank[6][:, 0:D]).then_inc(m["y_sb"], 1)

                    def final_out(t, j, q, quad, half):
                        at_ = acc[:, bass.ds(t, 1), :].rearrange("p o d -> p (o d)")
                        v.wait_ge(gath[q], quad * 16 + 16)
                        V.scalar_tensor_tensor(out=at_, in0=gat[q][:], scalar=gate1[:, bass.ds(t, 1)], in1=at_, op0=ALU.mult, op1=ALU.add).then_inc(m["fin"], 1)
                        v.wait_ge(m["fin"], t + 1)
                        v.wait_ge(m["y_ps"], t + (NG + 2))
                        v.wait_ge(y_out[j], half * 16 + (NG // 2) * 16)
                        V.scalar_tensor_tensor(out=ysb[j][:], in0=bank[6][:, 0:D], scalar=gate0[:, bass.ds(t, 1)], in1=at_, op0=ALU.mult, op1=ALU.add).then_inc(m["y_sb"], 1)

                    x_lo(0)
                    front(0, True)
                    back(0)
                    for g in (1, 2):
                        front(g, True)
                        routed_out(g - 1, (g - 1) % 2, 0, False)
                        back(g)
                    with v.Fori(0, (NG - 2) // 2) as i:
                        for j in range(2):
                            g = i * 2 + (3 + j)
                            front(g, True)
                            routed_out(g - 1, j % 2, i + 1, True)
                            back(g)
                    with v.Fori(0, (NT - 4) // 4) as i:
                        for j in range(4):
                            t = i * 4 + j
                            front(t + (NG + 1), True)
                            final_out(t, j % 2, j, i, i * 2 + j // 2)
                            back(t + (NG + 1))
                    for t in range(NT - 4, NT - 1):
                        front(t + NG + 1, t + NG + 1 < NF - 1)
                        final_out(t, t % 2, t % 4, t // 4, t // 2)
                        back(t + NG + 1)
                    final_out(NT - 1, 1, 3, NT // 4 - 1, NT // 2 - 1)


def kernel(**inputs):
    import numpy as _np
    import concourse.bacc as _bacc
    from concourse import mybir as _mybir
    from concourse.bass_utils import run_bass_kernel_spmd as _run

    a = {k: _np.asarray(v) for k, v in inputs.items()}
    order = list(range(1, E)) + [0]
    feed = {
        "x": a["L0_attn_x"].reshape(S, D),
        "wq": a["L0_attn_wq"], "wk": a["L0_attn_wk"], "wv": a["L0_attn_wv"],
        "wgq": a["L0_attn_wgq"], "wgk": a["L0_attn_wgk"], "wgv": a["L0_attn_wgv"],
        "r_out": a["L0_attn_r_out_w"], "gate_l": a["L0_attn_gate_local_w"], "gate_r": a["L0_attn_gate_remote_w"],
        "w_out": a["L0_attn_w_out"], "wr_t": a["L0_ffn_Wr"].T,
        "w1_t": a["L0_ffn_W1"][order].transpose(0, 2, 1), "w3_t": a["L0_ffn_W3"][order].transpose(0, 2, 1),
        "w2_t": a["L0_ffn_W2"][order].transpose(0, 2, 1),
    }
    nc = _bacc.Bacc("TRN2", target_bir_lowering=False, num_devices=1)
    arrays, args = {}, []
    for name, v in feed.items():
        v = _np.ascontiguousarray(v)
        arrays[f"in_{name}"] = v
        args.append(nc.dram_tensor(f"in_{name}", v.shape, _mybir.dt.from_np(v.dtype), kind="ExternalInput").ap())
    args.append(nc.dram_tensor("out_y", (S, D), _mybir.dt.float32, kind="ExternalOutput").ap())
    moe_block(nc, *args)
    r = _run(nc, [arrays], core_ids=[0])
    return r.results[0]["out_y"].reshape(1, S, D)
```
